# Optimizing a Trainium2 kernel written in Bass

```python
import numpy as np
import jax
import jax.numpy as jnp

def _softmax(x, axis=-1):
    return jax.nn.softmax(x, axis=axis)

def _gelu(x):
    return jax.nn.gelu(x, approximate=True)

def _silu(x):
    return jax.nn.silu(x)

def _sigmoid(x):
    return jax.nn.sigmoid(x)

def _layernorm(x, axis=-1, eps=1e-05):
    m = jnp.mean(x, axis=axis, keepdims=True)
    v = jnp.var(x, axis=axis, keepdims=True)
    return (x - m) / jnp.sqrt(v + eps)

def _scatter_add(tgt, idx, src, axis=0):
    return tgt.at[idx].add(src)

def _segment_sum(src, seg, n):
    return jax.ops.segment_sum(src, seg, n)
kernel_name = 'mk_lm_tower_d2_tok_ids512_r4_52a926'

def setup_inputs(seed: int=0):
    np.random.seed(seed)
    _w = jnp.asarray

    def _rec_inputs():
        import jax
        import jax.numpy as jnp
        _rk = jax.random.key(seed)
        x = jax.random.randint(jax.random.fold_in(_rk, 1), (16, 512), 0, 12564, jnp.int32)
        return x
    x = _rec_inputs()

    def _L0_tok_setup():
        import jax, jax.numpy as jnp
        import numpy as np
        VOCAB = 50257
        PROJ_DIM = 128
        B, S = (8, 1024)
        key = jax.random.key(seed)
        kx, kw = jax.random.split(key)
        x = jax.random.randint(kx, (B, S), 0, VOCAB)
        W = jax.random.normal(kw, (PROJ_DIM, VOCAB), dtype=jnp.float32) * 0.02
        return {'x': x, 'W': W}
    _L0_tok_all = _L0_tok_setup()
    _L0_tok_in = {k: v for k, v in _L0_tok_all.items() if k in ('W',)}
    del _L0_tok_all

    def _L0_attn_setup():
        import jax, jax.numpy as jnp
        import numpy as np
        import math
        CYCLES = [5, 6, 7, 8]

        def gamaka_pe(T, D):
            pos = np.arange(T, dtype=np.float32)[:, None]
            div = np.exp(np.arange(0, D, 2, dtype=np.float32) * (-math.log(10000.0) / D))
            pe = np.zeros((T, D), np.float32)
            pe[:, 0::2] = np.sin(pos * div)
            pe[:, 1::2] = np.cos(pos * div[:D // 2])
            tala = np.zeros((T, D), np.float32)
            slots = D // 4
            half = slots // 2
            harm = np.arange(1, half + 1, dtype=np.float32)
            for t_idx, c in enumerate(CYCLES):
                phase = pos % c / c * 2.0 * math.pi
                s = t_idx * slots
                tala[:, s:s + half] = np.sin(phase * harm)
                tala[:, s + half:s + slots] = np.cos(phase * harm)
            return jnp.asarray(0.5 * pe + 0.5 * tala)

        def layer_norm(x, g, b, eps=1e-05):
            m = x.mean(-1, keepdims=True)
            v = ((x - m) ** 2).mean(-1, keepdims=True)
            return (x - m) / jnp.sqrt(v + eps) * g + b

        def gru_all_threads(x, wih, whh, bih, bhh):
            xp = jnp.einsum('kij,btj->kbti', wih, x) + bih[:, None, None, :]
            K, B, T, _ = xp.shape
            D = x.shape[-1]

            def step(h, xt):
                gh = jnp.einsum('kij,kbj->kbi', whh, h) + bhh[:, None, :]
                xr, xz, xn = jnp.split(xt, 3, axis=-1)
                hr, hz, hn = jnp.split(gh, 3, axis=-1)
                r = jax.nn.sigmoid(xr + hr)
                z = jax.nn.sigmoid(xz + hz)
                n = jnp.tanh(xn + r * hn)
                h = (1.0 - z) * n + z * h
                return (h, h)
            h0 = jnp.zeros((K, B, D), x.dtype)
            _, hs = jax.lax.scan(step, h0, jnp.moveaxis(xp, 2, 0))
            return jnp.moveaxis(hs, 0, 2)
        key = jax.random.key(seed)
        ks = jax.random.split(key, 16)
        B, T, D = (4, 512, 128)
        s = 0.02
        return {'x': jax.random.normal(ks[0], (B, T, D), jnp.float32), 'gru_wih': s * jax.random.normal(ks[1], (4, 3 * D, D), jnp.float32), 'gru_whh': s * jax.random.normal(ks[2], (4, 3 * D, D), jnp.float32), 'gru_bih': s * jax.random.normal(ks[3], (4, 3 * D), jnp.float32), 'gru_bhh': s * jax.random.normal(ks[4], (4, 3 * D), jnp.float32), 'wq': s * jax.random.normal(ks[5], (4, D, D), jnp.float32), 'wk': s * jax.random.normal(ks[6], (4, D, D), jnp.float32), 'wv': s * jax.random.normal(ks[7], (4, D, D), jnp.float32), 'w_beat': s * jax.random.normal(ks[8], (4, D, 2 * D), jnp.float32), 'norm_g': jnp.ones((4, D), jnp.float32), 'norm_b': jnp.zeros((4, D), jnp.float32), 'w_mix': s * jax.random.normal(ks[9], (D, 4 * D), jnp.float32), 'bn_g': jnp.ones((D,), jnp.float32), 'bn_b': jnp.zeros((D,), jnp.float32)}
    _L0_attn_all = _L0_attn_setup()
    _L0_attn_in = {k: v for k, v in _L0_attn_all.items() if k in ('gru_wih', 'gru_whh', 'gru_bih', 'gru_bhh', 'wq', 'wk', 'wv', 'w_beat', 'norm_g', 'norm_b', 'w_mix', 'bn_g', 'bn_b')}
    del _L0_attn_all

    def _L0_ffn_setup():
        import jax, jax.numpy as jnp
        import numpy as np
        import math
        D_MODEL = 128
        N_EXPERTS = 128
        TOP_K = 8
        N_HEADS = 8
        D_KEYS = 128
        HALF = D_KEYS // 2
        N_BATCH, T_SEQ = (2, 512)
        key = jax.random.key(seed)
        k1, k2, k3, k4, k5, k6 = jax.random.split(key, 6)
        queries = jax.random.normal(k1, (N_BATCH, T_SEQ, D_MODEL), dtype=jnp.float32)
        bound_q = 1.0 / math.sqrt(D_MODEL)
        Wq = jax.random.uniform(k2, (N_HEADS * D_KEYS, D_MODEL), minval=-bound_q, maxval=bound_q, dtype=jnp.float32)
        bq = jax.random.uniform(k3, (N_HEADS * D_KEYS,), minval=-bound_q, maxval=bound_q, dtype=jnp.float32)
        bound_k = 1.0 / math.sqrt(HALF)
        keys = jax.random.uniform(k4, (N_HEADS, 2, N_EXPERTS, HALF), minval=-bound_k, maxval=bound_k, dtype=jnp.float32)
        std = D_MODEL ** (-0.5)
        w_down_embed = std * jax.random.normal(k5, (N_EXPERTS * N_EXPERTS, D_MODEL), dtype=jnp.float32)
        w_up_embed = std * jax.random.normal(k6, (N_EXPERTS * N_EXPERTS, D_MODEL), dtype=jnp.float32)
        return {'queries': queries, 'Wq': Wq, 'bq': bq, 'keys': keys, 'w_down_embed': w_down_embed, 'w_up_embed': w_up_embed}
    _L0_ffn_all = _L0_ffn_setup()
    _L0_ffn_in = {k: v for k, v in _L0_ffn_all.items() if k in ('Wq', 'bq', 'keys', 'w_down_embed', 'w_up_embed')}
    del _L0_ffn_all

    def _L1_attn_setup():
        import jax, jax.numpy as jnp
        import numpy as np
        DIM = 128
        NUM_HEADS = 8
        DIM_HEAD = 64
        EPS = 1e-08
        ROPE_THETA = 10000.0

        def rms_norm(x, gamma):
            norm = jnp.sqrt(jnp.sum(x * x, axis=-1, keepdims=True))
            x = x / jnp.maximum(norm, EPS)
            return x * DIM ** 0.5 * gamma

        def apply_rope(x):
            n, d = (x.shape[-2], x.shape[-1])
            inv_freq = 1.0 / ROPE_THETA ** (jnp.arange(0, d, 2, dtype=jnp.float32) / d)
            freqs = jnp.arange(n, dtype=jnp.float32)[:, None] * inv_freq[None, :]
            freqs = jnp.repeat(freqs, 2, axis=-1)
            cos, sin = (jnp.cos(freqs), jnp.sin(freqs))
            x1 = x[..., ::2]
            x2 = x[..., 1::2]
            rot = jnp.stack((-x2, x1), axis=-1).reshape(x.shape)
            return x * cos + rot * sin
        key = jax.random.key(seed)
        k1, k2, k3, k4 = jax.random.split(key, 4)
        b, n = (4, 512)
        dim_inner = NUM_HEADS * DIM_HEAD
        x = jax.random.normal(k1, (b, n, DIM), dtype=jnp.float32)
        gamma = jnp.ones((DIM,), dtype=jnp.float32)
        w_qkv = jax.random.normal(k2, (DIM, 3 * dim_inner), dtype=jnp.float32) * DIM ** (-0.5)
        w_out = jax.random.normal(k3, (dim_inner, DIM), dtype=jnp.float32) * dim_inner ** (-0.5)
        return {'x': x, 'gamma': gamma, 'w_qkv': w_qkv, 'w_out': w_out}
    _L1_attn_all = _L1_attn_setup()
    _L1_attn_in = {k: v for k, v in _L1_attn_all.items() if k in ('gamma', 'w_qkv', 'w_out')}
    del _L1_attn_all

    def _L1_ffn_setup():
        import jax, jax.numpy as jnp
        import numpy as np
        from jax import lax
        N, M, DIM, HEADS, TOPK = (4, 512, 128, 8, 16)

        def _split_heads(t, h):
            n, m, c = t.shape
            return t.reshape(n, m, h, c // h).transpose(0, 2, 1, 3).reshape(n * h, m, c // h)
        key = jax.random.key(seed)
        ks = jax.random.split(key, 7)
        f = lambda k, s, sc=1.0: jax.random.normal(k, s, dtype=jnp.float32) * sc
        return {'x': f(ks[0], (N, M, DIM)), 'pos_w': f(ks[1], (DIM, 1, 3), 0.1), 'pos_b': f(ks[2], (DIM,), 0.02), 'qkv_w': f(ks[3], (3 * DIM, DIM), 0.02), 'qkv_b': f(ks[4], (3 * DIM,), 0.02), 'wo_w': f(ks[5], (DIM, DIM), 0.02), 'wo_b': f(ks[6], (DIM,), 0.02)}
    _L1_ffn_all = _L1_ffn_setup()
    _L1_ffn_in = {k: v for k, v in _L1_ffn_all.items() if k in ('pos_w', 'pos_b', 'qkv_w', 'qkv_b', 'wo_w', 'wo_b')}
    del _L1_ffn_all
    return {'x': x, 'L0_tok_W': _L0_tok_in['W'], 'L0_attn_gru_wih': _L0_attn_in['gru_wih'], 'L0_attn_gru_whh': _L0_attn_in['gru_whh'], 'L0_attn_gru_bih': _L0_attn_in['gru_bih'], 'L0_attn_gru_bhh': _L0_attn_in['gru_bhh'], 'L0_attn_wq': _L0_attn_in['wq'], 'L0_attn_wk': _L0_attn_in['wk'], 'L0_attn_wv': _L0_attn_in['wv'], 'L0_attn_w_beat': _L0_attn_in['w_beat'], 'L0_attn_norm_g': _L0_attn_in['norm_g'], 'L0_attn_norm_b': _L0_attn_in['norm_b'], 'L0_attn_w_mix': _L0_attn_in['w_mix'], 'L0_attn_bn_g': _L0_attn_in['bn_g'], 'L0_attn_bn_b': _L0_attn_in['bn_b'], 'L0_ffn_Wq': _L0_ffn_in['Wq'], 'L0_ffn_bq': _L0_ffn_in['bq'], 'L0_ffn_keys': _L0_ffn_in['keys'], 'L0_ffn_w_down_embed': _L0_ffn_in['w_down_embed'], 'L0_ffn_w_up_embed': _L0_ffn_in['w_up_embed'], 'L1_attn_gamma': _L1_attn_in['gamma'], 'L1_attn_w_qkv': _L1_attn_in['w_qkv'], 'L1_attn_w_out': _L1_attn_in['w_out'], 'L1_ffn_pos_w': _L1_ffn_in['pos_w'], 'L1_ffn_pos_b': _L1_ffn_in['pos_b'], 'L1_ffn_qkv_w': _L1_ffn_in['qkv_w'], 'L1_ffn_qkv_b': _L1_ffn_in['qkv_b'], 'L1_ffn_wo_w': _L1_ffn_in['wo_w'], 'L1_ffn_wo_b': _L1_ffn_in['wo_b']}

def reference(x, L0_tok_W, L0_attn_gru_wih, L0_attn_gru_whh, L0_attn_gru_bih, L0_attn_gru_bhh, L0_attn_wq, L0_attn_wk, L0_attn_wv, L0_attn_w_beat, L0_attn_norm_g, L0_attn_norm_b, L0_attn_w_mix, L0_attn_bn_g, L0_attn_bn_b, L0_ffn_Wq, L0_ffn_bq, L0_ffn_keys, L0_ffn_w_down_embed, L0_ffn_w_up_embed, L1_attn_gamma, L1_attn_w_qkv, L1_attn_w_out, L1_ffn_pos_w, L1_ffn_pos_b, L1_ffn_qkv_w, L1_ffn_qkv_b, L1_ffn_wo_w, L1_ffn_wo_b):
    import jax
    import jax.numpy as jnp

    def _L0_tok_ref(x, W):
        import jax, jax.numpy as jnp
        import numpy as np
        VOCAB = 50257
        PROJ_DIM = 128
        B, S = (8, 1024)
        return jnp.take(W.T, x, axis=0)

    def _L0_attn_ref(x, gru_wih, gru_whh, gru_bih, gru_bhh, wq, wk, wv, w_beat, norm_g, norm_b, w_mix, bn_g, bn_b):
        import jax, jax.numpy as jnp
        import numpy as np
        import math
        CYCLES = [5, 6, 7, 8]

        def gamaka_pe(T, D):
            pos = np.arange(T, dtype=np.float32)[:, None]
            div = np.exp(np.arange(0, D, 2, dtype=np.float32) * (-math.log(10000.0) / D))
            pe = np.zeros((T, D), np.float32)
            pe[:, 0::2] = np.sin(pos * div)
            pe[:, 1::2] = np.cos(pos * div[:D // 2])
            tala = np.zeros((T, D), np.float32)
            slots = D // 4
            half = slots // 2
            harm = np.arange(1, half + 1, dtype=np.float32)
            for t_idx, c in enumerate(CYCLES):
                phase = pos % c / c * 2.0 * math.pi
                s = t_idx * slots
                tala[:, s:s + half] = np.sin(phase * harm)
                tala[:, s + half:s + slots] = np.cos(phase * harm)
            return jnp.asarray(0.5 * pe + 0.5 * tala)

        def layer_norm(x, g, b, eps=1e-05):
            m = x.mean(-1, keepdims=True)
            v = ((x - m) ** 2).mean(-1, keepdims=True)
            return (x - m) / jnp.sqrt(v + eps) * g + b

        def gru_all_threads(x, wih, whh, bih, bhh):
            xp = jnp.einsum('kij,btj->kbti', wih, x) + bih[:, None, None, :]
            K, B, T, _ = xp.shape
            D = x.shape[-1]

            def step(h, xt):
                gh = jnp.einsum('kij,kbj->kbi', whh, h) + bhh[:, None, :]
                xr, xz, xn = jnp.split(xt, 3, axis=-1)
                hr, hz, hn = jnp.split(gh, 3, axis=-1)
                r = jax.nn.sigmoid(xr + hr)
                z = jax.nn.sigmoid(xz + hz)
                n = jnp.tanh(xn + r * hn)
                h = (1.0 - z) * n + z * h
                return (h, h)
            h0 = jnp.zeros((K, B, D), x.dtype)
            _, hs = jax.lax.scan(step, h0, jnp.moveaxis(xp, 2, 0))
            return jnp.moveaxis(hs, 0, 2)
        B, T, D = x.shape
        x = x + gamaka_pe(T, D)[None]
        gru_out = gru_all_threads(x, gru_wih, gru_whh, gru_bih, gru_bhh)
        q = jnp.einsum('kij,btj->kbti', wq, x)
        k = jnp.einsum('kij,btj->kbti', wk, x)
        v = jnp.einsum('kij,btj->kbti', wv, x)
        idx = jnp.arange(T)
        diff = idx[:, None] - idx[None, :]
        cyc = jnp.asarray(CYCLES)[:, None, None]
        valid = (diff[None] >= 0) & (diff[None] < cyc)
        mask = jnp.where(valid, 0.0, -jnp.inf).astype(x.dtype)
        scores = jnp.einsum('kbtd,kbsd->kbts', q, k) / jnp.sqrt(jnp.asarray(D, x.dtype))
        attn = jax.nn.softmax(scores + mask[:, None], axis=-1)
        attn_out = jnp.einsum('kbts,kbsd->kbtd', attn, v)
        comb = jnp.concatenate([gru_out, attn_out], axis=-1)
        beat = jnp.einsum('kij,kbtj->kbti', w_beat, comb)
        thr = layer_norm(beat + x[None], norm_g[:, None, None, :], norm_b[:, None, None, :])
        merged = jnp.moveaxis(thr, 0, 2).reshape(B, T, 4 * D)
        out = jnp.einsum('ij,btj->bti', w_mix, merged)
        return layer_norm(out + x, bn_g, bn_b)

    def _L0_ffn_ref(queries, Wq, bq, keys, w_down_embed, w_up_embed):
        import jax, jax.numpy as jnp
        import numpy as np
        import math
        D_MODEL = 128
        N_EXPERTS = 128
        TOP_K = 8
        N_HEADS = 8
        D_KEYS = 128
        HALF = D_KEYS // 2
        N_BATCH, T_SEQ = (2, 512)
        N, T, D = queries.shape
        H, E, K = (N_HEADS, N_EXPERTS, TOP_K)
        q_tok = queries.reshape(-1, D)
        qh = q_tok @ Wq.T + bq
        qh = qh.reshape(-1, H, 2, HALF)
        sub_scores = jnp.einsum('nhcf,hcef->nhce', qh, keys)
        s, idx = jax.lax.top_k(sub_scores, K)
        all_scores = (s[:, :, 0, :, None] + s[:, :, 1, None, :]).reshape(-1, H, K * K)
        all_idx = (idx[:, :, 0, :, None] * E + idx[:, :, 1, None, :]).reshape(-1, H, K * K)
        best_s, best_pos = jax.lax.top_k(all_scores, K)
        indices = jnp.take_along_axis(all_idx, best_pos, axis=-1)
        w_down = w_down_embed[indices]
        w_up = w_up_embed[indices]
        x = jnp.einsum('nd,nhkd->nhk', q_tok, w_down)
        x = jax.nn.gelu(x)
        vals = x * jax.nn.softmax(best_s, axis=-1)
        out = jnp.einsum('nhk,nhkd->nd', vals, w_up)
        return out.reshape(N, T, D)

    def _L1_attn_ref(x, gamma, w_qkv, w_out):
        import jax, jax.numpy as jnp
        import numpy as np
        DIM = 128
        NUM_HEADS = 8
        DIM_HEAD = 64
        EPS = 1e-08
        ROPE_THETA = 10000.0

        def rms_norm(x, gamma):
            norm = jnp.sqrt(jnp.sum(x * x, axis=-1, keepdims=True))
            x = x / jnp.maximum(norm, EPS)
            return x * DIM ** 0.5 * gamma

        def apply_rope(x):
            n, d = (x.shape[-2], x.shape[-1])
            inv_freq = 1.0 / ROPE_THETA ** (jnp.arange(0, d, 2, dtype=jnp.float32) / d)
            freqs = jnp.arange(n, dtype=jnp.float32)[:, None] * inv_freq[None, :]
            freqs = jnp.repeat(freqs, 2, axis=-1)
            cos, sin = (jnp.cos(freqs), jnp.sin(freqs))
            x1 = x[..., ::2]
            x2 = x[..., 1::2]
            rot = jnp.stack((-x2, x1), axis=-1).reshape(x.shape)
            return x * cos + rot * sin
        b, n, _ = x.shape
        h, d = (NUM_HEADS, DIM_HEAD)
        xn = rms_norm(x, gamma)
        qkv = xn @ w_qkv
        qkv = qkv.reshape(b, n, 3, h, d)
        q = jnp.transpose(qkv[:, :, 0], (0, 2, 1, 3))
        k = jnp.transpose(qkv[:, :, 1], (0, 2, 1, 3))
        v = jnp.transpose(qkv[:, :, 2], (0, 2, 1, 3))
        q = apply_rope(q)
        k = apply_rope(k)
        scale = d ** (-0.5)
        attn = jnp.einsum('bhnd,bhmd->bhnm', q, k) * scale
        attn = jax.nn.softmax(attn, axis=-1)
        out = jnp.einsum('bhnm,bhmd->bhnd', attn, v)
        out = jnp.transpose(out, (0, 2, 1, 3)).reshape(b, n, h * d)
        return out @ w_out

    def _L1_ffn_ref(x, pos_w, pos_b, qkv_w, qkv_b, wo_w, wo_b):
        import jax, jax.numpy as jnp
        import numpy as np
        from jax import lax
        N, M, DIM, HEADS, TOPK = (4, 512, 128, 8, 16)

        def _split_heads(t, h):
            n, m, c = t.shape
            return t.reshape(n, m, h, c // h).transpose(0, 2, 1, 3).reshape(n * h, m, c // h)
        n, m, c = x.shape
        h = HEADS
        scale = c ** (-0.5)
        pos = lax.conv_general_dilated(x.transpose(0, 2, 1), pos_w, window_strides=(1,), padding=[(1, 1)], feature_group_count=c, dimension_numbers=('NCH', 'OIH', 'NCH'))
        x = x + (pos + pos_b[None, :, None]).transpose(0, 2, 1)
        qkv = x @ qkv_w.T + qkv_b
        q, k, v = jnp.split(qkv, [c, 2 * c], axis=-1)
        q = _split_heads(q, h)
        k = _split_heads(k, h)
        v = _split_heads(v, h)
        qd = lax.stop_gradient(q)
        kd = lax.stop_gradient(k)
        logits = jnp.einsum('bmd,bpd->bmp', qd * scale, kd)
        _, idx = lax.top_k(logits, TOPK)
        gather = jax.vmap(lambda t, i: t[i])
        k_sel = gather(k, idx)
        v_sel = gather(v, idx)
        attn = jax.nn.softmax(jnp.einsum('bmd,bmkd->bmk', q * scale, k_sel), axis=-1)
        out = jnp.einsum('bmk,bmkd->bmd', attn, v_sel)
        d = c // h
        out = out.reshape(n, h, m, d).transpose(0, 2, 1, 3).reshape(n, m, c)
        return out @ wo_w.T + wo_b
    h = _L0_tok_ref(x, L0_tok_W)
    h = h + _L0_attn_ref(_layernorm(h, axis=-1), L0_attn_gru_wih, L0_attn_gru_whh, L0_attn_gru_bih, L0_attn_gru_bhh, L0_attn_wq, L0_attn_wk, L0_attn_wv, L0_attn_w_beat, L0_attn_norm_g, L0_attn_norm_b, L0_attn_w_mix, L0_attn_bn_g, L0_attn_bn_b)
    h = h + _L0_ffn_ref(_layernorm(h, axis=-1), L0_ffn_Wq, L0_ffn_bq, L0_ffn_keys, L0_ffn_w_down_embed, L0_ffn_w_up_embed)
    h = h + _L1_attn_ref(_layernorm(h, axis=-1), L1_attn_gamma, L1_attn_w_qkv, L1_attn_w_out)
    h = h + _L1_ffn_ref(_layernorm(h, axis=-1), L1_ffn_pos_w, L1_ffn_pos_b, L1_ffn_qkv_w, L1_ffn_qkv_b, L1_ffn_wo_w, L1_ffn_wo_b)
    return h

_drawn_inputs = setup_inputs


def setup_inputs(seed=0):
    import zlib

    import numpy as np

    out = dict(_drawn_inputs(seed))
    spreads = {'L0_attn_norm_g': (1.0, 0.2),
     'L0_attn_norm_b': (0.0, 0.1),
     'L0_attn_bn_g': (1.0, 0.2),
     'L0_attn_bn_b': (0.0, 0.1),
     'L1_attn_gamma': (1.0, 0.2)}
    factors = {'L0_attn_gru_wih': 3.703,
     'L0_attn_gru_whh': 8.0,
     'L0_attn_gru_bih': 8.0,
     'L0_attn_gru_bhh': 8.0,
     'L0_attn_wq': 8.0,
     'L0_attn_wk': 8.0,
     'L0_attn_wv': 4.134,
     'L0_attn_w_beat': 2.949,
     'L1_ffn_pos_w': 7.107,
     'L1_ffn_pos_b': 8.0,
     'L1_ffn_qkv_w': 2.732,
     'L1_ffn_qkv_b': 8.0,
     'L1_ffn_wo_w': 2.738,
     'L1_ffn_wo_b': 2.89}
    for name, (base, spread) in spreads.items():
        noise = np.random.default_rng([zlib.crc32(name.encode()), seed]).standard_normal(out[name].shape)
        drawn = base * np.exp(spread * noise) if base else spread * noise
        out[name] = jnp.asarray(drawn.astype(out[name].dtype))
    for name, factor in factors.items():
        out[name] = (out[name] * factor).astype(out[name].dtype)
    return out
```

```python
from contextlib import ExitStack

import numpy as np
import concourse.bass as bass
from concourse import mybir

ALU = mybir.AluOpType
ACT = mybir.ActivationFunctionType
AX = mybir.AxisListType.X
F32 = mybir.dt.float32
I32 = mybir.dt.int32
U32 = mybir.dt.uint32

P = 128
B, T, D = 16, 512, 128
VOCAB = 50257
STEPS = P // B
TILES = T // STEPS
K = 4
CYCLES = (5, 6, 7, 8)
GATES = 3
KB = K * B
NEG = -1e30
LN_EPS = 1e-5
H = 8
TOP = 8
EXPERTS = 128
HALF = 64
SLOTS = H * TOP
GROUPS = 4
GS = SLOTS // GROUPS
GELU_A = 0.7978845608028654
GELU_B = GELU_A * 0.044715
CH = T // P
UNITS = CH * H
DH, HD = 64, 16
ROPE_THETA = 10000.0
RSQRT_SEED = float(0x5F3759DF)


def wait_apart(eng, met, *waits):
    values = [v if isinstance(v, int) else eng.to_reg(v) for _, v in waits]
    eng.wait_ge(*met)
    for (sem, _), value in zip(waits, values):
        eng.wait_ge(sem, value)


class Steps:

    def __init__(self, eng, sem):
        self.eng, self.sem, self.n = eng, sem, 0

    def restart(self):
        self.eng.sem_clear(self.sem)
        self.n = 0

    def then(self, ins):
        ins.then_inc(self.sem, 1)
        self.n += 1
        self.eng.wait_ge(self.sem, self.n)

    def mark(self, ins):
        ins.then_inc(self.sem, 1)
        self.n += 1

    def wait(self):
        self.eng.wait_ge(self.sem, self.n)


def rsqrt(nc, own, out, var, tmp, width, eps):
    v, a, b = (tmp[:, j, 0:width] for j in range(3))
    own.then(nc.vector.tensor_scalar(v, var, eps, None, ALU.add))
    own.then(nc.vector.tensor_scalar(a.bitcast(I32), v.bitcast(I32), 1, None, ALU.logical_shift_right))
    own.then(nc.vector.tensor_scalar(out.bitcast(I32), a.bitcast(I32), -1.0, RSQRT_SEED, ALU.mult, ALU.add))
    for _ in range(3):
        own.then(nc.vector.tensor_tensor(a, out, out, ALU.mult))
        own.then(nc.vector.scalar_tensor_tensor(b, a, -0.5, v, ALU.mult, ALU.mult))
        own.then(nc.vector.scalar_tensor_tensor(out, b, 1.5, out, ALU.add, ALU.mult))


def layer0(nc, d, hidden):
    with ExitStack() as ctx:
        def sb(name, shape, dt=F32):
            return ctx.enter_context(nc.sbuf_tensor(name, shape, dt))

        def sem(name):
            return ctx.enter_context(nc.semaphore(name))

        w_ih = sb("w_ih", [P, K * GATES * P])
        w_hh = sb("w_hh", [P, K * GATES * P])
        gru_bias = sb("gru_bias", [2, K * GATES * P])
        bias_rows = sb("bias_rows", [2, 3, 64])
        w_q = sb("w_q", [P, K * P])
        w_k = sb("w_k", [P, K * P])
        w_v = sb("w_v", [P, K * P])
        w_beat = sb("w_beat", [P, K, 2, P])
        w_mix = sb("w_mix", [P, K, P])
        norm_g = sb("norm_g", [P, K * P])
        norm_b = sb("norm_b", [P, K * P])
        bn_g = sb("bn_g", [P, P])
        bn_b = sb("bn_b", [P, P])
        key_wq = sb("key_wq", [P, H * P])
        key_bq = sb("key_bq", [P, H])
        keys = sb("keys", [P, H, EXPERTS])
        ident = sb("ident", [P, P])
        iota8 = sb("iota8", [P, TOP])
        mask = sb("mask", [P, K, 2 * P])
        token_ids = sb("token_ids", [P, TILES], I32)
        tile_ids = sb("tile_ids", [P, 1], I32)
        emb = sb("emb", [P, P])
        res = sb("res", [P, P])
        pe_rows = sb("pe_rows", [P, P])
        x_tok = sb("x_tok", [P, P])
        x_t = sb("x_t", [P, P])
        q_t = sb("q_t", [P, K, P])
        k_t = sb("k_t", [P, K, 2, P])
        v_prev = sb("v_prev", [P, K, P])
        v_cur = sb("v_cur", [P, K, P])
        sm = sb("sm", [P, K, 2 * P])
        neg_max = sb("neg_max", [P, K])
        p_sum = sb("p_sum", [P, K])
        p_inv = sb("p_inv", [P, K])
        p_t = sb("p_t", [P, 2, K, P])
        ao_t = sb("ao_t", [P, K, P])
        h_t = sb("h_t", [P, K, STEPS, B])
        th_rz = sb("th_rz", [P, 2, KB])
        zp = sb("zp", [P, KB])
        zm = sb("zm", [P, KB])
        zh = sb("zh", [P, KB])
        np1 = sb("np1", [P, KB])
        np2 = sb("np2", [P, KB])
        nn = sb("nn", [P, KB])
        nz = sb("nz", [P, KB])
        thr = sb("thr", [P, K * P])
        thr_t = sb("thr_t", [P, K, P])
        mixed = sb("mixed", [P, P])
        h1 = sb("h1", [P, P])
        stats = sb("stats", [P, K, 6])
        mv = sb("mv", [P, K, 2])
        rstd = sb("rstd", [P, K])
        nt = sb("nt", [P, 3, K])
        q_tok = sb("q_tok", [P, P])
        qk_t = sb("qk_t", [P, P])
        qh_t = sb("qh_t", [P, H, P])
        top_s = sb("top_s", [P, H, 2, TOP])
        top_i = sb("top_i", [P, H, 2, TOP], U32)
        pairs = sb("pairs", [P, H, TOP * TOP])
        best = sb("best", [P, H, TOP])
        pos = sb("pos", [P, SLOTS], U32)
        pos_hi = sb("pos_hi", [P, SLOTS], U32)
        pos_lo = sb("pos_lo", [P, SLOTS], U32)
        onehot = sb("onehot", [P, SLOTS, TOP])
        onehot2 = sb("onehot2", [P, SLOTS, TOP])
        row_i = sb("row_i", [P, SLOTS])
        row_j = sb("row_j", [P, SLOTS])
        idx_next = sb("idx_next", [P, SLOTS], I32)
        best_e = sb("best_e", [P, H, TOP])
        e_sum = sb("e_sum", [P, H])
        e_inv = sb("e_inv", [P, H])
        prob = sb("prob", [P, SLOTS])
        idx = sb("idx", [P, SLOTS], I32)
        rows = sb("rows", [P, SLOTS, 2 * P])
        q_exp = sb("q_exp", [P, P])
        prob_exp = sb("prob_exp", [P, SLOTS])
        h_acc = sb("h_acc", [P, P])
        h_out = sb("h_out", [P, P])
        xd = sb("xd", [P, GS])
        g1 = sb("g1", [P, GS])
        g2 = sb("g2", [P, GS])
        g3 = sb("g3", [P, GS])
        g4 = sb("g4", [P, GS])
        val = sb("val", [P, GS])

        def bank(name):
            return ctx.enter_context(nc.psum_tensor(name, [P, 512], F32))

        rz_bank = [bank(f"rz{i}") for i in range(2)]
        n_bank = [bank(f"n{i}") for i in range(2)]
        G = [bank(f"G{i}") for i in range(4)]

        def rz(s):
            return rz_bank[s // 4][:, (s % 4) * 128:(s % 4 + 1) * 128]

        def n_in(s):
            return n_bank[s // 4][:, (s % 4) * 128:(s % 4) * 128 + 64]

        def n_hid(s):
            return n_bank[s // 4][:, (s % 4) * 128 + 64:(s % 4) * 128 + 128]

        weights_in = sem("weights_in")
        mask_in = sem("mask_in")
        zeroed = sem("zeroed")
        id_copied = sem("id_copied")
        emb_in = sem("emb_in")
        pe_in = sem("pe_in")
        emb_used = sem("emb_used")
        x_ready = sem("x_ready")
        x_turned = sem("x_turned")
        x_t_ready = sem("x_t_ready")
        qkv_done = sem("qkv_done")
        qkv_ready = sem("qkv_ready")
        win_scores = sem("win_scores")
        win_max = sem("win_max")
        win_exp = sem("win_exp")
        win_inv = sem("win_inv")
        win_probs = sem("win_probs")
        win_turned = sem("win_turned")
        win_t_ready = sem("win_t_ready")
        ao_done = sem("ao_done")
        ao_ready = sem("ao_ready")
        rz_ready = sem("rz_ready")
        hn_ready = sem("hn_ready")
        rz_tanh = sem("rz_tanh")
        n_pre = sem("n_pre")
        n_tanh = sem("n_tanh")
        h_ready = sem("h_ready")
        beat_done = sem("beat_done")
        thr_ready = sem("thr_ready")
        thr_turned = sem("thr_turned")
        thr_t_ready = sem("thr_t_ready")
        mix_done = sem("mix_done")
        q_ready = sem("q_ready")
        q_turned = sem("q_turned")
        qk_ready = sem("qk_ready")
        qh_done = sem("qh_done")
        qh_ready = sem("qh_ready")
        key_scores = sem("key_scores")
        key_top = sem("key_top")
        best_ready = sem("best_ready")
        best_exp = sem("best_exp")
        idx_ready = sem("idx_ready")
        idx_copied = sem("idx_copied")
        rows_in = [sem(f"rows_in{g}") for g in range(GROUPS)]
        gelu_in = sem("gelu_in")
        gelu_tanh = sem("gelu_tanh")
        group_used = sem("group_used")
        h_out_ready = sem("h_out_ready")
        stored = sem("stored")
        dve_step = sem("dve_step")
        act_step = sem("act_step")
        LOADS = 0

        consts = [(w_ih, "w_ih"), (w_hh, "w_hh"), (gru_bias, "gru_bias"), (bias_rows, "bias_rows"),
                  (w_q, "w_q"), (w_k, "w_k"), (w_v, "w_v"), (w_beat, "w_beat"), (w_mix, "w_mix"),
                  (key_wq, "key_wq"), (key_bq, "key_bq"), (keys, "keys"), (ident, "ident"),
                  (iota8, "iota8"), (token_ids, "token_ids")]
        spread = [(norm_g, "norm_g"), (norm_b, "norm_b"), (bn_g, "bn_g"), (bn_b, "bn_b")]
        LOADS = 16 * (len(consts) + len(spread))

        block = ctx.enter_context(nc.Block())

        @block.sync
        def _(sync):
            sync.dma_start(mask[:, :, :], d["mask_first"]).then_inc(mask_in, 16)
            for t, name in consts:
                sync.dma_start(t[tuple(slice(None) for _ in t.shape)], d[name]).then_inc(weights_in, 16)
            for t, name in spread:
                sync.dma_start(t[:, :], d[name].partition_broadcast(P)).then_inc(weights_in, 16)

            def load_pe(n):
                sync.dma_start(pe_rows[:, :], d["pe"][n]).then_inc(pe_in, 16)

            def store(n):
                sync.wait_ge(h_out_ready, n + 1)
                sync.dma_start(hidden[n], h_out[:, :]).then_inc(stored, 16)

            load_pe(0)
            sync.wait_ge(win_max, 1)
            sync.dma_start(mask[:, :, :], d["mask"]).then_inc(mask_in, 16)
            sync.wait_ge(x_ready, 1)
            load_pe(1)
            with sync.Fori(1, TILES - 1) as i:
                sync.wait_ge(x_ready, i + 1)
                load_pe(i + 1)
                store(i - 1)
            store(TILES - 2)
            store(TILES - 1)
            sync.wait_ge(stored, 16 * TILES)

        @block.gpsimd
        def _(pool):
            pool.memset(h_t[:, :, :, :], 0.0).then_inc(zeroed, 1)
            pool.memset(k_t[:, :, :, :], 0.0).then_inc(zeroed, 1)
            pool.memset(v_cur[:, :, :], 0.0).then_inc(zeroed, 1)
            pool.wait_ge(weights_in, LOADS)

            def embed(n, first=False):
                if not first:
                    pool.wait_ge(emb_used, 2 * n)
                    pool.wait_ge(emb_in, 16 * n)
                pool.tensor_copy(tile_ids[:, :], token_ids[:, bass.ds(n, 1)]).then_inc(id_copied, 1)
                wait_apart(pool, (weights_in, LOADS), (id_copied, n + 1))
                pool.indirect_dma_start(out=emb[:, :], out_offset=None, in_=d["tok_w"],
                                        in_offset=bass.IndirectOffsetOnAxis(ap=tile_ids[:, :].bitcast(U32), axis=0)
                                        ).then_inc(emb_in, 16)

            def gather(n, first=False):
                wait_apart(pool, (weights_in, LOADS), (idx_ready, n + 1),
                           *(() if first else ((r, 16 * GS * n) for r in rows_in)))
                pool.tensor_copy(idx[:, :], idx_next[:, :]).then_inc(idx_copied, 1)
                wait_apart(pool, (weights_in, LOADS), (idx_copied, n + 1))
                for g in range(GROUPS):
                    if not first:
                        wait_apart(pool, (weights_in, LOADS), (group_used, GROUPS * (n - 1) + g + 1))
                    for j in range(g * GS, (g + 1) * GS):
                        pool.indirect_dma_start(out=rows[:, j, :], out_offset=None, in_=d["experts"],
                                                in_offset=bass.IndirectOffsetOnAxis(ap=idx[:, j:j + 1].bitcast(U32), axis=0)
                                                ).then_inc(rows_in[g], 16)

            embed(0, first=True)
            embed(1)
            embed(2)
            gather(0, first=True)
            with pool.Fori(2, TILES - 1) as i:
                embed(i + 1)
                gather(i - 1)
            gather(TILES - 2)
            gather(TILES - 1)

        @block.tensor
        def _(pe):
            def front(n, first=False):
                pe.wait_ge(x_ready, n + 1)
                if not first:
                    pe.wait_ge(key_top, 4 * n)
                pe.transpose(G[3][:, 0:P], x_tok[:, :], ident[:, :]).then_inc(x_turned, 1)
                pe.wait_ge(x_t_ready, n + 1)
                for k in range(K):
                    m = pe.matmul(G[0][:, k * P:(k + 1) * P], w_q[:, k * P:(k + 1) * P], x_t[:, :],
                                  start=(k == 0), stop=True, skip_group_check=True)
                m.then_inc(qkv_done, 1)
                for k in range(K):
                    m = pe.matmul(G[1][:, k * P:(k + 1) * P], w_k[:, k * P:(k + 1) * P], x_t[:, :],
                                  start=(k == 0), stop=True, skip_group_check=True)
                m.then_inc(qkv_done, 1)
                pe.matmul(G[2][:, :], x_t[:, :], w_v[:, :], start=True, stop=True).then_inc(qkv_done, 1)
                for half in range(2):
                    s0 = 4 * half
                    rzv = rz_bank[half][:, :].rearrange("p (s g k b) -> p s g k b", s=4, g=2, k=K)
                    nv = n_bank[half][:, :].rearrange("p (s g k b) -> p s g k b", s=4, g=2, k=K)
                    for k in range(K):
                        for g in range(GATES):
                            c = (k * GATES + g) * P
                            out = rzv[:, :, g, k, :] if g < 2 else nv[:, :, 0, k, :]
                            pe.matmul(out, gru_bias[:, c:c + P], bias_rows[:, 0 if g < 2 else 1, :],
                                      start=(k == 0 and g in (0, 2)), stop=False, skip_group_check=True)
                            pe.matmul(out, w_ih[:, c:c + P], x_t[:, s0 * B:(s0 + 4) * B],
                                      start=False, stop=False, skip_group_check=True)
                        pe.matmul(nv[:, :, 1, k, :], gru_bias[:, c:c + P], bias_rows[:, 2, :],
                                  start=False, stop=False, skip_group_check=True)
                pe.wait_ge(qkv_ready, 3 * n + 2)
                for k in range(K):
                    m = pe.matmul(G[k // 2][:, (k % 2) * 256:(k % 2 + 1) * 256], q_t[:, k, :], k_t[:, k, :, :],
                                  start=(k % 2 == 0), stop=True, skip_group_check=True)
                m.then_inc(win_scores, 1)
                pe.wait_ge(win_probs, 4 * (n + 1))
                pe.wait_ge(qkv_ready, 3 * n + 3)
                for half in range(2):
                    for k in range(K):
                        m = pe.transpose(G[2 + half][:, k * P:(k + 1) * P], sm[:, k, half * P:(half + 1) * P], ident[:, :])
                    m.then_inc(win_turned, 1)
                pe.wait_ge(win_t_ready, 2 * (n + 1))
                for k in range(K):
                    pe.matmul(G[0][:, k * P:(k + 1) * P], v_prev[:, k, :], p_t[:, 0, k, :],
                              start=(k == 0), stop=False, skip_group_check=True)
                    m = pe.matmul(G[0][:, k * P:(k + 1) * P], v_cur[:, k, :], p_t[:, 1, k, :],
                                  start=False, stop=True, skip_group_check=True)
                m.then_inc(ao_done, 1)

            def gru_step(n, s):
                pe.wait_ge(h_ready, STEPS * n + s + 1)
                prev = (s - 1) % STEPS
                for g in range(2):
                    for k in range(K):
                        c = (k * GATES + g) * P
                        m = pe.matmul(rz(s)[:, (g * K + k) * B:(g * K + k + 1) * B], w_hh[:, c:c + P],
                                      h_t[:, k, prev, :], start=False, stop=True, skip_group_check=True)
                m.then_inc(rz_ready, 1)
                for k in range(K):
                    c = (k * GATES + 2) * P
                    m = pe.matmul(n_hid(s)[:, k * B:(k + 1) * B], w_hh[:, c:c + P],
                                  h_t[:, k, prev, :], start=False, stop=True, skip_group_check=True)
                m.then_inc(hn_ready, 1)

            def mix(n):
                pe.wait_ge(h_ready, STEPS * (n + 1) + 1)
                pe.wait_ge(ao_ready, n + 1)
                for k in range(K):
                    pe.matmul(G[1][:, k * P:(k + 1) * P], h_t[:, k, :, :], w_beat[:, k, 0, :],
                              start=(k == 0), stop=False, skip_group_check=True)
                    m = pe.matmul(G[1][:, k * P:(k + 1) * P], ao_t[:, k, :], w_beat[:, k, 1, :],
                                  start=False, stop=True, skip_group_check=True)
                m.then_inc(beat_done, 1)
                pe.wait_ge(thr_ready, n + 1)
                for k in range(K):
                    m = pe.transpose(G[2][:, k * P:(k + 1) * P], thr[:, k * P:(k + 1) * P], ident[:, :])
                m.then_inc(thr_turned, 1)
                pe.wait_ge(thr_t_ready, n + 1)
                for k in range(K):
                    m = pe.matmul(G[3][:, 0:P], thr_t[:, k, :], w_mix[:, k, :], start=(k == 0), stop=(k == K - 1))
                m.then_inc(mix_done, 1)

            def choose(n):
                pe.wait_ge(q_ready, n + 1)
                pe.transpose(G[0][:, 0:P], q_tok[:, :], ident[:, :]).then_inc(q_turned, 1)
                pe.wait_ge(qk_ready, n + 1)
                for h in range(H):
                    m = pe.matmul(G[1 + h // 4][:, (h % 4) * P:(h % 4 + 1) * P], key_wq[:, h * P:(h + 1) * P],
                                  qk_t[:, :], start=(h % 4 == 0), stop=True, skip_group_check=True)
                    if h % 4 == 3:
                        m.then_inc(qh_done, 1)
                for g in range(4):
                    c = g % 2
                    pe.wait_ge(qh_ready, H * n + 4 * (g // 2 + 1))
                    for j in range(4):
                        m = pe.matmul(G[(3 + g) % 4][:, j * P:(j + 1) * P],
                                      qh_t[c * HALF:(c + 1) * HALF, 4 * (g // 2) + j, :],
                                      keys[c * HALF:(c + 1) * HALF, 4 * (g // 2) + j, :],
                                      start=(j == 0), stop=True, skip_group_check=True)
                    m.then_inc(key_scores, 1)

            def round_(n, last=False):
                for s in range(STEPS):
                    gru_step(n, s)
                mix(n)
                choose(n)
                if not last:
                    front(n + 1)

            pe.wait_ge(weights_in, LOADS)
            pe.wait_ge(zeroed, 3)
            front(0, first=True)
            round_(0)
            with pe.Fori(1, TILES - 1) as i:
                round_(i)
            round_(TILES - 1, last=True)

        @block.scalar
        def _(act):
            own = Steps(act, act_step)

            def front(n):
                act.wait_ge(emb_in, 16 * (n + 1))
                nc.scalar.copy(res[:, :], emb[:, :]).then_inc(emb_used, 1)
                act.wait_ge(x_turned, n + 1)
                nc.scalar.copy(x_t[:, :], G[3][:, 0:P]).then_inc(x_t_ready, 1)
                nc.scalar.copy(v_prev[:, :, :], v_cur[:, :, :]).then_inc(act_step, 1)
                own.n += 1
                own.then(nc.scalar.copy(k_t[:, :, 0, :], k_t[:, :, 1, :]))
                act.wait_ge(qkv_done, 3 * n + 1)
                nc.scalar.copy(q_t[:, :, :], G[0][:, :].rearrange("p (k t) -> p k t", k=K)).then_inc(qkv_ready, 1)
                act.wait_ge(qkv_done, 3 * n + 2)
                nc.scalar.copy(k_t[:, :, 1, :], G[1][:, :].rearrange("p (k t) -> p k t", k=K)).then_inc(qkv_ready, 1)
                act.wait_ge(qkv_done, 3 * n + 3)
                nc.scalar.copy(v_cur[:, :, :], G[2][:, :].rearrange("p (k t) -> p k t", k=K)).then_inc(qkv_ready, 1)
                act.wait_ge(win_max, n + 1)
                for k in range(K):
                    own.mark(nc.scalar.activation(sm[:, k, :], sm[:, k, :], ACT.Exp, bias=neg_max[:, k:k + 1],
                                                  accum_out=p_sum[:, k:k + 1]))
                own.wait()
                act.sem_inc(win_exp, 1)
                act.wait_ge(win_inv, n + 1)
                for k in range(K):
                    nc.scalar.activation(sm[:, k, :], sm[:, k, :], ACT.Copy, scale=p_inv[:, k:k + 1]).then_inc(win_probs, 1)
                for half in range(2):
                    act.wait_ge(win_turned, 2 * n + half + 1)
                    nc.scalar.copy(p_t[:, half, :, :], G[2 + half][:, :].rearrange("p (k t) -> p k t", k=K)
                                   ).then_inc(win_t_ready, 1)
                act.wait_ge(ao_done, n + 1)
                nc.scalar.copy(ao_t[:, :, :], G[0][:, :].rearrange("p (k t) -> p k t", k=K)).then_inc(ao_ready, 1)

            def gru_step(n, s):
                act.wait_ge(rz_ready, STEPS * n + s + 1)
                nc.scalar.activation(th_rz[:, :, :], rz(s).rearrange("p (g c) -> p g c", g=2), ACT.Tanh, scale=0.5
                                     ).then_inc(rz_tanh, 1)
                act.wait_ge(n_pre, STEPS * n + s + 1)
                nc.scalar.activation(nn[:, :], np2[:, :], ACT.Tanh).then_inc(n_tanh, 1)

            def mix(n):
                act.wait_ge(thr_turned, n + 1)
                nc.scalar.copy(thr_t[:, :, :], G[2][:, :].rearrange("p (k t) -> p k t", k=K)).then_inc(thr_t_ready, 1)

            def choose(n):
                act.wait_ge(q_turned, n + 1)
                nc.scalar.copy(qk_t[:, :], G[0][:, 0:P]).then_inc(qk_ready, 1)
                for h in range(H):
                    if h % 4 == 0:
                        act.wait_ge(qh_done, 2 * n + h // 4 + 1)
                    nc.scalar.activation(qh_t[:, h, :], G[1 + h // 4][:, (h % 4) * P:(h % 4 + 1) * P], ACT.Identity,
                                         bias=key_bq[:, h:h + 1]).then_inc(qh_ready, 1)
                act.wait_ge(best_ready, n + 1)
                nc.scalar.activation(best_e[:, :, :], best_e[:, :, :], ACT.Exp).then_inc(best_exp, 1)

            def experts(n, g):
                act.wait_ge(gelu_in, GROUPS * n + g + 1)
                nc.scalar.activation(g3[:, :], g2[:, :], ACT.Tanh).then_inc(gelu_tanh, 1)

            def finish(n, first=False):
                act.wait_ge(group_used, GROUPS * (n + 1))
                if not first:
                    act.wait_ge(stored, 16 * n)
                nc.scalar.copy(h_out[:, :], h_acc[:, :]).then_inc(h_out_ready, 1)

            def round_(n, first=False, last=False):
                own.restart()
                for s in range(4):
                    gru_step(n, s)
                if not first:
                    experts(n - 1, 0)
                for s in range(4, STEPS):
                    gru_step(n, s)
                if not first:
                    experts(n - 1, 1)
                mix(n)
                choose(n)
                if not first:
                    experts(n - 1, 2)
                if not last:
                    front(n + 1)
                if not first:
                    experts(n - 1, 3)
                    finish(n - 1, first=(isinstance(n, int) and n == 1))

            nc.scalar.preload_act_table_set("exp_and_others")
            act.wait_ge(zeroed, 3)
            front(0)
            round_(0, first=True)
            round_(1)
            with act.Fori(2, TILES - 1) as i:
                round_(i)
            round_(TILES - 1, last=True)
            for g in range(GROUPS):
                experts(TILES - 1, g)
            finish(TILES - 1)

        @block.vector
        def _(dve):
            own = Steps(dve, dve_step)
            V = nc.vector

            def norm_stats(x, k):
                own.then(V.bn_stats(stats[:, k, :], x))
                own.then(V.bn_aggr(mv[:, k, :], stats[:, k, :]))

            def front(n):
                dve.wait_ge(emb_in, 16 * (n + 1))
                norm_stats(emb[:, :], 0)
                rsqrt(nc, own, rstd[:, 0:1], mv[:, 0, 1:2], nt, 1, LN_EPS)
                V.tensor_scalar(x_tok[:, :], emb[:, :], mv[:, 0, 0:1], rstd[:, 0:1], ALU.subtract, ALU.mult
                                ).then_inc(emb_used, 1)
                dve.wait_ge(emb_used, 2 * (n + 1))
                dve.wait_ge(pe_in, 16 * (n + 1))
                V.tensor_tensor(x_tok[:, :], x_tok[:, :], pe_rows[:, :], ALU.add).then_inc(x_ready, 1)
                dve.wait_ge(win_scores, n + 1)
                for j in range(2):
                    own.mark(V.scalar_tensor_tensor(sm[:, 2 * j:2 * j + 2, :], G[j][:, :].rearrange("p (k t) -> p k t", k=2),
                                                    float(D) ** -0.5, mask[:, 2 * j:2 * j + 2, :], ALU.mult, ALU.add))
                own.wait()
                V.tensor_reduce(neg_max[:, :], sm[:, :, :], AX, ALU.max, negate=True).then_inc(win_max, 1)
                dve.wait_ge(win_exp, n + 1)
                V.reciprocal(p_inv[:, :], p_sum[:, :]).then_inc(win_inv, 1)

            def gru_step(n, s):
                t = STEPS * n + s
                dve.wait_ge(rz_tanh, t + 1)
                dve.wait_ge(hn_ready, t + 1)
                prev = h_t[:, :, (s - 1) % STEPS, :]
                own.then(V.scalar_tensor_tensor(np1[:, :], th_rz[:, 0, :], 1.0, n_hid(s), ALU.add, ALU.mult))
                V.scalar_tensor_tensor(np2[:, :], np1[:, :], 0.5, n_in(s), ALU.mult, ALU.add).then_inc(n_pre, 1)
                own.mark(V.tensor_scalar(zp[:, :], th_rz[:, 1, :], 0.5, 0.5, ALU.mult, ALU.add))
                own.mark(V.tensor_scalar(zm[:, :], th_rz[:, 1, :], -0.5, 0.5, ALU.mult, ALU.add))
                own.wait()
                own.mark(V.tensor_tensor(zh[:, :].rearrange("p (k b) -> p k b", k=K),
                                         zp[:, :].rearrange("p (k b) -> p k b", k=K), prev, ALU.mult))
                dve.wait_ge(n_tanh, t + 1)
                own.then(V.tensor_tensor(nz[:, :], nn[:, :], zm[:, :], ALU.mult))
                V.tensor_tensor(h_t[:, :, s, :], nz[:, :].rearrange("p (k b) -> p k b", k=K),
                                zh[:, :].rearrange("p (k b) -> p k b", k=K), ALU.add).then_inc(h_ready, 1)

            def mix(n):
                dve.wait_ge(beat_done, n + 1)
                own.then(V.tensor_tensor(thr[:, :].rearrange("p (k c) -> p k c", k=K),
                                         G[1][:, :].rearrange("p (k c) -> p k c", k=K),
                                         x_tok[:, :].unsqueeze(1).to_broadcast([P, K, P]), ALU.add))
                for k in range(K):
                    own.mark(V.bn_stats(stats[:, k, :], thr[:, k * P:(k + 1) * P]))
                own.wait()
                for k in range(K):
                    own.mark(V.bn_aggr(mv[:, k, :], stats[:, k, :]))
                own.wait()
                rsqrt(nc, own, rstd[:, :], mv[:, :, 1], nt, K, LN_EPS)
                for k in range(K):
                    own.mark(V.tensor_scalar(thr[:, k * P:(k + 1) * P], thr[:, k * P:(k + 1) * P], mv[:, k, 0:1],
                                             rstd[:, k:k + 1], ALU.subtract, ALU.mult))
                own.wait()
                own.then(V.tensor_tensor(thr[:, :], thr[:, :], norm_g[:, :], ALU.mult))
                V.tensor_tensor(thr[:, :], thr[:, :], norm_b[:, :], ALU.add).then_inc(thr_ready, 1)
                dve.wait_ge(mix_done, n + 1)
                own.then(V.tensor_tensor(mixed[:, :], G[3][:, 0:P], x_tok[:, :], ALU.add))
                norm_stats(mixed[:, :], 0)
                rsqrt(nc, own, rstd[:, 0:1], mv[:, 0, 1:2], nt, 1, LN_EPS)
                own.then(V.tensor_scalar(mixed[:, :], mixed[:, :], mv[:, 0, 0:1], rstd[:, 0:1], ALU.subtract, ALU.mult))
                own.then(V.tensor_tensor(mixed[:, :], mixed[:, :], bn_g[:, :], ALU.mult))
                own.then(V.tensor_tensor(mixed[:, :], mixed[:, :], bn_b[:, :], ALU.add))
                own.then(V.tensor_tensor(h1[:, :], mixed[:, :], res[:, :], ALU.add))

            def choose(n):
                norm_stats(h1[:, :], 0)
                rsqrt(nc, own, rstd[:, 0:1], mv[:, 0, 1:2], nt, 1, LN_EPS)
                V.tensor_scalar(q_tok[:, :], h1[:, :], mv[:, 0, 0:1], rstd[:, 0:1], ALU.subtract, ALU.mult
                                ).then_inc(q_ready, 1)
                for g in range(4):
                    src = G[(3 + g) % 4]
                    wait_apart(dve, (zeroed, 3), (key_scores, 4 * n + g + 1))
                    for j in range(4):
                        own.mark(V.max(top_s[:, 4 * (g // 2) + j, g % 2, :], src[:, j * P:(j + 1) * P]))
                    own.wait()
                    for j in range(4):
                        m = V.max_index(top_i[:, 4 * (g // 2) + j, g % 2, :], top_s[:, 4 * (g // 2) + j, g % 2, :],
                                        src[:, j * P:(j + 1) * P])
                        if j < 3:
                            own.mark(m)
                    m.then_inc(key_top, 1)
                own.then(V.tensor_tensor(pairs[:, :, :].rearrange("p h (i j) -> p h i j", i=TOP), top_s[:, :, 0, :].unsqueeze(3).to_broadcast([P, H, TOP, TOP]),
                                         top_s[:, :, 1, :].unsqueeze(2).to_broadcast([P, H, TOP, TOP]), ALU.add))
                for h in range(H):
                    own.mark(V.max(best[:, h, :], pairs[:, h, :]))
                own.wait()
                V.tensor_tensor(best_e[:, :, :], best[:, :, :], best[:, :, 0:1].to_broadcast([P, H, TOP]), ALU.subtract
                                ).then_inc(best_ready, 1)
                for h in range(H):
                    own.mark(V.max_index(pos[:, h * TOP:(h + 1) * TOP], best[:, h, :], pairs[:, h, :]))
                own.wait()
                own.mark(V.tensor_scalar(pos_hi[:, :], pos[:, :], 3, None, ALU.logical_shift_right))
                own.mark(V.tensor_scalar(pos_lo[:, :], pos[:, :], 7, None, ALU.bitwise_and))
                own.wait()
                dve.wait_ge(key_top, 4 * (n + 1))
                for c, (p_, oh, r) in enumerate(((pos_hi, onehot, row_i), (pos_lo, onehot2, row_j))):
                    own.then(V.tensor_tensor(oh[:, :, :], p_[:, :].unsqueeze(2).to_broadcast([P, SLOTS, TOP]),
                                             iota8[:, :].unsqueeze(1).to_broadcast([P, SLOTS, TOP]), ALU.is_equal))
                    own.then(V.tensor_tensor(oh[:, :, :].rearrange("p (h k) e -> p h k e", h=H),
                                             oh[:, :, :].rearrange("p (h k) e -> p h k e", h=H),
                                             top_i[:, :, c, :].unsqueeze(2).to_broadcast([P, H, TOP, TOP]), ALU.mult))
                    own.then(V.tensor_reduce(r[:, :], oh[:, :, :], AX, ALU.add))
                if not (isinstance(n, int) and n == 0):
                    dve.wait_ge(idx_copied, n)
                V.scalar_tensor_tensor(idx_next[:, :], row_i[:, :], float(EXPERTS), row_j[:, :], ALU.mult, ALU.add
                                       ).then_inc(idx_ready, 1)
                dve.wait_ge(best_exp, n + 1)
                own.then(V.tensor_reduce(e_sum[:, :], best_e[:, :, :], AX, ALU.add))
                own.then(V.reciprocal(e_inv[:, :], e_sum[:, :]))
                own.then(V.tensor_tensor(prob[:, :].rearrange("p (h k) -> p h k", h=H), best_e[:, :, :],
                                         e_inv[:, :].unsqueeze(2).to_broadcast([P, H, TOP]), ALU.mult))

            def take_over(n, first=False):
                if not first:
                    dve.wait_ge(h_out_ready, n)
                own.mark(V.tensor_copy(q_exp[:, :], q_tok[:, :]))
                own.mark(V.tensor_copy(prob_exp[:, :], prob[:, :]))
                own.mark(V.tensor_copy(h_acc[:, :], h1[:, :]))
                own.wait()

            def experts(n, g):
                dve.wait_ge(rows_in[g], 16 * GS * (n + 1))
                for j in range(GS):
                    down = rows[:, g * GS + j, 0:P]
                    own.mark(V.tensor_tensor_reduce(down, down, q_exp[:, :], 1.0, 0.0, ALU.mult, ALU.add, xd[:, j:j + 1]))
                own.wait()
                own.then(V.tensor_tensor(g1[:, :], xd[:, :], xd[:, :], ALU.mult))
                own.then(V.tensor_scalar(g1[:, :], g1[:, :], GELU_B, GELU_A, ALU.mult, ALU.add))
                V.tensor_tensor(g2[:, :], g1[:, :], xd[:, :], ALU.mult).then_inc(gelu_in, 1)
                dve.wait_ge(gelu_tanh, GROUPS * n + g + 1)
                own.then(V.scalar_tensor_tensor(g4[:, :], g3[:, :], 1.0, xd[:, :], ALU.add, ALU.mult))
                own.then(V.scalar_tensor_tensor(val[:, :], g4[:, :], 0.5, prob_exp[:, g * GS:(g + 1) * GS],
                                                ALU.mult, ALU.mult))
                for j in range(GS):
                    m = V.scalar_tensor_tensor(h_acc[:, :], rows[:, g * GS + j, P:2 * P], val[:, j:j + 1], h_acc[:, :],
                                               ALU.mult, ALU.add)
                    if j < GS - 1:
                        own.then(m)
                m.then_inc(group_used, 1)
                dve.wait_ge(group_used, GROUPS * n + g + 1)

            def round_(n, first=False, last=False):
                own.restart()
                if not first:
                    take_over(n - 1, first=(isinstance(n, int) and n == 1))
                for s in range(4):
                    gru_step(n, s)
                if not first:
                    experts(n - 1, 0)
                for s in range(4, STEPS):
                    gru_step(n, s)
                if not first:
                    experts(n - 1, 1)
                mix(n)
                choose(n)
                if not first:
                    experts(n - 1, 2)
                if not last:
                    front(n + 1)
                if not first:
                    experts(n - 1, 3)

            dve.wait_ge(weights_in, LOADS)
            dve.wait_ge(zeroed, 3)
            dve.wait_ge(mask_in, 16)
            V.memset(zh[:, :], 0.0).then_inc(h_ready, 1)
            front(0)
            dve.wait_ge(mask_in, 32)
            round_(0, first=True)
            round_(1)
            with dve.Fori(2, TILES - 1) as i:
                round_(i)
            round_(TILES - 1, last=True)
            own.restart()
            take_over(TILES - 1)
            for g in range(GROUPS):
                experts(TILES - 1, g)



def layer1(nc, d, hidden, out):
    with ExitStack() as ctx:
        def sb(name, shape, dt=F32):
            return ctx.enter_context(nc.sbuf_tensor(name, shape, dt))

        def sem(name):
            return ctx.enter_context(nc.semaphore(name))

        def bank(name):
            return ctx.enter_context(nc.psum_tensor(name, [P, 512], F32))

        w_qkv = sb("w_qkv", [P, 5, T])
        gamma = sb("gamma", [P, 1])
        rope = sb("rope", [P, 4, T])
        w_out = sb("w_out", [P, 4, P])
        ident = sb("ident1", [P, P])
        conv_w = sb("conv_w", [P, 3])
        conv_b = sb("conv_b", [P, 1])
        f_wqkv = sb("f_wqkv", [P, 3, P])
        f_bqk = sb("f_bqk", [P, 2])
        f_bv = sb("f_bv", [P, P])
        f_wo = sb("f_wo", [P, P])
        f_bo = sb("f_bo", [P, P])
        parity = sb("parity", [P, 2])
        h_in = sb("h_in", [P, CH, P])
        h_a = sb("h_a", [P, CH, P])
        u_a = sb("u_a", [P, CH, P])
        sq = sb("sq", [P, P])
        stats = sb("stats1", [P, CH, 6])
        mv = sb("mv1", [P, CH, 2])
        rstd = sb("rstd1", [P, CH])
        ss = sb("ss", [P, CH])
        nt = sb("nt1", [P, 3, CH])
        xn_t = sb("xn_t", [P, T])
        q_t = sb("q_t1", [P, 4, T])
        k_t = sb("k_t1", [P, 4, T])
        v_a = sb("v_a", [P, CH, T])
        turned = sb("turned", [P, 2, T])
        a_nmax = sb("a_nmax", [P, 2])
        a_sum = sb("a_sum", [P, UNITS])
        a_inv = sb("a_inv", [P, H])
        a_p = sb("a_p", [P, 2, T])
        a_pt = sb("a_pt", [P, 2, CH, P])
        a_o = sb("a_o", [P, T])
        a_ot = sb("a_ot", [P, 4, P])
        h1 = sb("h1_1", [P, CH, P])
        h_f = sb("h_f", [P, CH, P])
        u_f = sb("u_f", [P, CH, P])
        u_t = sb("u_t", [P, T + 2])
        x_c = sb("x_c", [P, T])
        x_f = sb("x_f", [P, T])
        q_f = sb("q_f", [P, T])
        k_f = sb("k_f", [P, 2, T])
        v_f = sb("v_f", [P, CH, H, HD + 1])
        top_a = sb("top_a", [P, 2, TOP])
        top_b = sb("top_b", [P, 2, TOP])
        f_nmax = sb("f_nmax", [P, 2])
        f_s = sb("f_s", [P, 2, T])
        f_e = sb("f_e", [P, 2, T])
        f_p = sb("f_p", [P, 2, T])
        f_pt = sb("f_pt", [P, 2, CH, P])
        f_inv = sb("f_inv", [P, H])
        f_o = sb("f_o", [P, P])
        f_ot = sb("f_ot", [P, P])
        f_out = sb("f_out", [P, CH, P])

        A = [bank("A0"), bank("A1")]
        AT, AO = bank("AT"), bank("AO")
        F = [bank("F0"), bank("F1")]
        FT, FO = bank("FT"), bank("FO")

        weights_in = sem("weights_in1")
        weights_ready = sem("weights_ready")
        cleared = sem("cleared1")
        h_loaded = sem("h_loaded")
        h_taken = sem("h_taken")
        squares = sem("squares")
        squares_done = sem("squares_done")
        rope_ready = sem("rope_ready")
        u_scaled = sem("u_scaled")
        xn_turned = sem("xn_turned")
        xn_ready = sem("xn_ready")
        proj = sem("proj")
        proj_used = sem("proj_used")
        v_proj = sem("v_proj")
        v_ready = sem("v_ready")
        a_scores = sem("a_scores")
        a_max = sem("a_max")
        a_exp = sem("a_exp")
        a_turned = sem("a_turned")
        a_t_ready = sem("a_t_ready")
        a_pv = sem("a_pv")
        a_norm = sem("a_norm")
        a_o_turned = sem("a_o_turned")
        a_ot_ready = sem("a_ot_ready")
        a_outed = sem("a_outed")
        h1_ready = sem("h1_ready")
        hf_ready = sem("hf_ready")
        uf_ready = sem("uf_ready")
        uf_turned = sem("uf_turned")
        ut_ready = sem("ut_ready")
        xf_ready = sem("xf_ready")
        f_proj = sem("f_proj")
        qf_ready = sem("qf_ready")
        kf_ready = sem("kf_ready")
        f_vproj = sem("f_vproj")
        vf_ready = sem("vf_ready")
        f_scores = sem("f_scores")
        f_first = sem("f_first")
        f_exp = sem("f_exp")
        f_probs = sem("f_probs")
        f_turned = sem("f_turned")
        f_t_ready = sem("f_t_ready")
        f_pv = sem("f_pv")
        f_norm = sem("f_norm")
        f_o_turned = sem("f_o_turned")
        f_ot_ready = sem("f_ot_ready")
        f_outed = sem("f_outed")
        out_ready = sem("out_ready")
        out_stored = sem("out_stored")
        dve_step = sem("dve_step1")
        pool_step = sem("pool_step1")

        rows_of = hidden.rearrange("n p d -> (n p) d").rearrange("(c p b) d -> b p c d", p=P, b=B)
        out_of = out.rearrange("b (c p) d -> b p c d", p=P)
        consts = [(w_qkv, "qkv1"), (gamma, "gamma"), (rope, "rope"), (w_out, "w_out"), (ident, "ident"),
                  (conv_w, "conv_w"), (conv_b, "conv_b"), (f_wqkv, "f_wqkv"), (f_bqk, "f_bqk"), (f_wo, "f_wo"),
                  (parity, "parity")]
        spread = [(f_bv, "f_bv"), (f_bo, "f_bo")]
        LOADS = 16 * (len(consts) + len(spread))
        block = ctx.enter_context(nc.Block())

        def walk(b, attn, ffn, tasks):
            for t in range(UNITS + 4):
                for branch, ends, lag, f in tasks:
                    if not (attn if branch == "a" else ffn):
                        continue
                    u = t - lag
                    if not 0 <= u < UNITS:
                        continue
                    if not ends:
                        f(b if branch == "a" else b - 1, u)
                    elif u % H == H - 1:
                        f(b if branch == "a" else b - 1, u // H)

        def rounds(eng, pre_a, pre_f, tasks, own=None):
            def one(b, attn, ffn):
                if own:
                    own.restart()
                if attn:
                    pre_a(b)
                if ffn:
                    pre_f(b - 1)
                walk(b, attn, ffn, tasks)

            one(0, True, False)
            one(1, True, True)
            with eng.Fori(2, B) as b:
                one(b, True, True)
            one(B, False, True)

        def is_(b, v):
            return isinstance(b, int) and b == v

        @block.sync
        def _(sync):
            for t, name in consts:
                sync.dma_start(t[tuple(slice(None) for _ in t.shape)], d[name]).then_inc(weights_in, 16)
            for t, name in spread:
                sync.dma_start(t[:, :], d[name].partition_broadcast(P)).then_inc(weights_in, 16)

            def load(b):
                if not is_(b, 0):
                    sync.wait_ge(h_taken, b)
                sync.dma_start(h_in[:, :, :], rows_of[b]).then_inc(h_loaded, 16)

            def store(b):
                sync.wait_ge(out_ready, CH * (b + 1))
                sync.dma_start(out_of[b], f_out[:, :, :]).then_inc(out_stored, 16)

            load(0)
            load(1)
            with sync.Fori(2, B) as b:
                load(b)
                store(b - 2)
            store(B - 2)
            store(B - 1)
            sync.wait_ge(out_stored, 16 * B)

        @block.gpsimd
        def _(pool):
            pool.memset(u_t[:, :], 0.0).then_inc(cleared, 1)
            pool.memset(v_f[:, :, :, :], 1.0).then_inc(cleared, 1)

            def pre_a(b):
                wait_apart(pool, (weights_in, LOADS), (h_loaded, 16 * (b + 1)),
                           *(() if is_(b, 0) else ((h1_ready, CH * b),)))
                pool.tensor_copy(h_a[:, :, :], h_in[:, :, :]).then_inc(h_taken, 1)

            def pre_f(b):
                pool.wait_ge(h1_ready, CH * (b + 1))
                if not is_(b, 0):
                    pool.wait_ge(out_ready, CH * b)
                pool.tensor_tensor(h_f[:, :, :], h1[:, :, :], f_bo[:, :].unsqueeze(1).to_broadcast([P, CH, P]), ALU.add
                                   ).then_inc(hf_ready, 1)

            rounds(pool, pre_a, pre_f, [])

        @block.tensor
        def _(pe):
            def pre_a(b):
                pe.wait_ge(u_scaled, b + 1)
                for c in range(CH):
                    m = pe.transpose(A[0][:, c * P:(c + 1) * P], u_a[:, c, :], ident[:, :])
                m.then_inc(xn_turned, 1)
                pe.wait_ge(xn_ready, b + 1)
                if not is_(b, 0):
                    pe.wait_ge(h1_ready, CH * b)
                banks = [A[1], AT, AO, A[0]]
                n = 0
                for j in range(4):
                    for w in range(4):
                        n += 1
                        if n > 4:
                            pe.wait_ge(proj_used, 16 * b + n - 4)
                        pe.matmul(banks[w][:, :], w_qkv[:, w, j * P:(j + 1) * P], xn_t[:, :], start=True, stop=True
                                  ).then_inc(proj, 1)
                for c in range(CH):
                    if c < 4:
                        pe.wait_ge(proj_used, 16 * b + 13 + c)
                    pe.matmul(banks[c][:, :], xn_t[:, c * P:(c + 1) * P], w_qkv[:, 4, :], start=True, stop=True
                              ).then_inc(v_proj, 1)

            def pre_f(b):
                pe.wait_ge(uf_ready, b + 1)
                if not is_(b, 0):
                    pe.wait_ge(out_ready, CH * b)
                for c in range(CH):
                    m = pe.transpose(FT[:, c * P:(c + 1) * P], u_f[:, c, :], ident[:, :])
                m.then_inc(uf_turned, 1)
                pe.wait_ge(xf_ready, b + 1)
                for w in range(2):
                    pe.matmul(F[w][:, :], f_wqkv[:, w, :], x_f[:, :], start=True, stop=True).then_inc(f_proj, 1)
                for c in range(CH):
                    m = pe.matmul(FO[:, c * P:(c + 1) * P], x_f[:, c * P:(c + 1) * P], f_wqkv[:, 2, :],
                                  start=(c == 0), stop=True, skip_group_check=True)
                m.then_inc(f_vproj, 1)

            def a_s(b, u):
                c, h = divmod(u, H)
                rows = slice((h % 2) * DH, (h % 2 + 1) * DH)
                if u == 0:
                    pe.wait_ge(v_ready, CH * (b + 1))
                    pe.wait_ge(rope_ready, b + 1)
                if u >= 2:
                    pe.wait_ge(a_exp, UNITS * b + u - 1)
                pe.matmul(A[u % 2][:, :], q_t[rows, h // 2, c * P:(c + 1) * P], k_t[rows, h // 2, :],
                          start=True, stop=True).then_inc(a_scores, 1)

            def a_v(b, u):
                c, h = divmod(u, H)
                pe.wait_ge(a_t_ready, UNITS * b + u + 1)
                if h == 0 and u:
                    pe.wait_ge(a_norm, CH * b + c)
                for j in range(CH):
                    m = pe.matmul(AO[:, h * DH:(h + 1) * DH], a_pt[:, u % 2, j, :], v_a[:, j, h * DH:(h + 1) * DH],
                                  start=(h == 0 and j == 0), stop=(j == CH - 1), skip_group_check=True)
                m.then_inc(a_pv, 1)

            def a_turn(b, u):
                pe.wait_ge(a_exp, UNITS * b + u + 1)
                if u:
                    pe.wait_ge(a_t_ready, UNITS * b + u)
                    if u % H == 1 and u > H:
                        pe.wait_ge(a_ot_ready, CH * b + u // H)
                    if u % H == 2 and u > H:
                        pe.wait_ge(h1_ready, CH * b + u // H)
                for j in range(CH):
                    m = pe.transpose(AT[:, j * P:(j + 1) * P], a_p[:, u % 2, j * P:(j + 1) * P], ident[:, :])
                m.then_inc(a_turned, 1)

            def a_end1(b, c):
                pe.wait_ge(a_norm, CH * b + c + 1)
                pe.wait_ge(a_t_ready, UNITS * b + min(H * c + 9, UNITS))
                for j in range(4):
                    m = pe.transpose(AT[:, j * P:(j + 1) * P], a_o[:, j * P:(j + 1) * P], ident[:, :])
                m.then_inc(a_o_turned, 1)

            def a_end2(b, c):
                pe.wait_ge(a_ot_ready, CH * b + c + 1)
                pe.wait_ge(a_t_ready, UNITS * b + min(H * c + 10, UNITS))
                for j in range(4):
                    m = pe.matmul(AT[:, 0:P], a_ot[:, j, :], w_out[:, j, :], start=(j == 0), stop=(j == 3))
                m.then_inc(a_outed, 1)

            def f_sc(b, u):
                c, h = divmod(u, H)
                rows = slice((h // 2) * 32, (h // 2 + 1) * 32)
                if u == 0:
                    pe.wait_ge(qf_ready, b + 1)
                    pe.wait_ge(kf_ready, 2 * (b + 1))
                    pe.wait_ge(vf_ready, b + 1)
                if u >= 2:
                    pe.wait_ge(f_exp, UNITS * b + u - 1)
                pe.matmul(F[u % 2][:, :], q_f[rows, c * P:(c + 1) * P], k_f[rows, h % 2, :], start=True, stop=True
                          ).then_inc(f_scores, 1)

            def f_v(b, u):
                c, h = divmod(u, H)
                pe.wait_ge(f_t_ready, UNITS * b + u + 1)
                if h == 0 and u:
                    pe.wait_ge(f_norm, CH * b + c)
                for j in range(CH):
                    m = pe.matmul(FO[:, h * (HD + 1):(h + 1) * (HD + 1)], f_pt[:, u % 2, j, :], v_f[:, j, h, :],
                                  start=(h == 0 and j == 0), stop=(j == CH - 1), skip_group_check=True)
                m.then_inc(f_pv, 1)

            def f_turn(b, u):
                pe.wait_ge(f_probs, UNITS * b + u + 1)
                if u:
                    pe.wait_ge(f_t_ready, UNITS * b + u)
                    if u % H == 1 and u > H:
                        pe.wait_ge(f_ot_ready, CH * b + u // H)
                    if u % H == 2 and u > H:
                        pe.wait_ge(out_ready, CH * b + u // H)
                for j in range(CH):
                    m = pe.transpose(FT[:, j * P:(j + 1) * P], f_p[:, u % 2, j * P:(j + 1) * P], ident[:, :])
                m.then_inc(f_turned, 1)

            def f_end1(b, c):
                pe.wait_ge(f_norm, CH * b + c + 1)
                pe.wait_ge(f_t_ready, UNITS * b + min(H * c + 9, UNITS))
                pe.transpose(FT[:, 0:P], f_o[:, :], ident[:, :]).then_inc(f_o_turned, 1)

            def f_end2(b, c):
                pe.wait_ge(f_ot_ready, CH * b + c + 1)
                pe.wait_ge(f_t_ready, UNITS * b + min(H * c + 10, UNITS))
                pe.matmul(FT[:, 0:P], f_ot[:, :], f_wo[:, :], start=True, stop=True).then_inc(f_outed, 1)

            pe.wait_ge(weights_in, LOADS)
            pe.wait_ge(weights_ready, 1)
            rounds(pe, pre_a, pre_f, [
                ("a", False, 0, a_s), ("f", False, 0, f_sc), ("a", False, 2, a_v), ("f", False, 2, f_v),
                ("a", True, 3, a_end1), ("f", True, 3, f_end1), ("a", True, 4, a_end2), ("f", True, 4, f_end2),
                ("a", False, 1, a_turn), ("f", False, 1, f_turn)])

        @block.scalar
        def _(act):
            def pre_a(b):
                act.wait_ge(squares, 2 * b + 1)
                for c in range(CH):
                    m = nc.scalar.activation(sq[:, :], u_a[:, c, :], ACT.Square, accum_out=ss[:, c:c + 1])
                    m.then_inc(squares_done, 1)
                    act.wait_ge(squares_done, CH * b + c + 1)
                act.wait_ge(xn_turned, b + 1)
                nc.scalar.copy(xn_t[:, :], A[0][:, :]).then_inc(xn_ready, 1)
                banks = [A[1], AT, AO, A[0]]
                for c in range(CH):
                    act.wait_ge(v_proj, CH * b + c + 1)
                    nc.scalar.copy(v_a[:, c, :], banks[c][:, :]).then_inc(v_ready, 1)

            def pre_f(b):
                act.wait_ge(uf_turned, b + 1)
                act.wait_ge(cleared, 2)
                nc.scalar.copy(u_t[:, 1:T + 1], FT[:, :]).then_inc(ut_ready, 1)
                act.wait_ge(f_proj, 2 * b + 1)
                act.wait_ge(weights_ready, 1)
                nc.scalar.activation(q_f[:, :], F[0][:, :], ACT.Identity, bias=f_bqk[:, 0:1], scale=float(D) ** -0.5
                                     ).then_inc(qf_ready, 1)

            def a_e(b, u):
                act.wait_ge(a_max, UNITS * b + u + 1)
                if u >= 2:
                    act.wait_ge(a_turned, UNITS * b + u - 1)
                nc.scalar.activation(a_p[:, u % 2, :], A[u % 2][:, :], ACT.Exp, bias=a_nmax[:, u % 2:u % 2 + 1],
                                     accum_out=a_sum[:, u:u + 1]).then_inc(a_exp, 1)

            def a_ev(b, u):
                act.wait_ge(a_turned, UNITS * b + u + 1)
                if u >= 2:
                    act.wait_ge(a_pv, UNITS * b + u - 1)
                nc.scalar.copy(a_pt[:, u % 2, :, :], AT[:, :].rearrange("p (j n) -> p j n", j=CH)).then_inc(a_t_ready, 1)

            def a_end(b, c):
                act.wait_ge(a_o_turned, CH * b + c + 1)
                nc.scalar.copy(a_ot[:, :, :], AT[:, :].rearrange("p (j n) -> p j n", j=4)).then_inc(a_ot_ready, 1)

            def f_e_(b, u):
                act.wait_ge(f_first, UNITS * b + u + 1)
                if u >= 2:
                    act.wait_ge(f_probs, UNITS * b + u - 1)
                nc.scalar.activation(f_e[:, u % 2, :], F[u % 2][:, :], ACT.Exp, bias=f_nmax[:, u % 2:u % 2 + 1]
                                     ).then_inc(f_exp, 1)

            def f_ev(b, u):
                act.wait_ge(f_turned, UNITS * b + u + 1)
                if u >= 2:
                    act.wait_ge(f_pv, UNITS * b + u - 1)
                nc.scalar.copy(f_pt[:, u % 2, :, :], FT[:, :].rearrange("p (j n) -> p j n", j=CH)).then_inc(f_t_ready, 1)

            def f_end(b, c):
                act.wait_ge(f_o_turned, CH * b + c + 1)
                nc.scalar.copy(f_ot[:, :], FT[:, 0:P]).then_inc(f_ot_ready, 1)

            nc.scalar.preload_act_table_set("exp_and_others")
            rounds(act, pre_a, pre_f, [
                ("a", False, 0, a_e), ("f", False, 0, f_e_), ("a", True, 3, a_end), ("f", True, 3, f_end),
                ("a", False, 1, a_ev), ("f", False, 1, f_ev)])

        @block.vector
        def _(dve):
            own = Steps(dve, dve_step)
            V = nc.vector

            def norm(src, dst):
                for c in range(CH):
                    own.mark(V.bn_stats(stats[:, c, :], src[:, c, :]))
                own.wait()
                for c in range(CH):
                    own.mark(V.bn_aggr(mv[:, c, :], stats[:, c, :]))
                own.wait()
                rsqrt(nc, own, rstd[:, :], mv[:, :, 1], nt, CH, LN_EPS)
                for c in range(CH):
                    m = V.tensor_scalar(dst[:, c, :], src[:, c, :], mv[:, c, 0:1], rstd[:, c:c + 1],
                                        ALU.subtract, ALU.mult)
                    if c < CH - 1:
                        own.mark(m)
                own.wait()
                return m

            def pre_a(b):
                dve.wait_ge(h_taken, b + 1)
                norm(h_a, u_a).then_inc(squares, 1)
                dve.wait_ge(squares, 2 * b + 1)
                dve.wait_ge(squares_done, CH * (b + 1))
                rsqrt(nc, own, rstd[:, :], ss[:, :], nt, CH, 0.0)
                own.then(V.tensor_scalar(rstd[:, :], rstd[:, :], 1e8, None, ALU.min))
                for c in range(CH):
                    m = V.tensor_scalar(u_a[:, c, :], u_a[:, c, :], rstd[:, c:c + 1], None, ALU.mult)
                    if c < CH - 1:
                        own.mark(m)
                m.then_inc(squares, 1)
                dve.wait_ge(squares, 2 * b + 2)
                own.wait()
                dve.sem_inc(u_scaled, 1)
                banks = [A[1], AT, AO, A[0]]
                for j in range(4):
                    for w in range(4):
                        dst = (q_t if w < 2 else k_t)[:, j, :] if w % 2 == 0 else turned[:, w // 2, :]
                        dve.wait_ge(proj, 16 * b + 4 * j + w + 1)
                        V.tensor_tensor(dst, banks[w][:, :], rope[:, w, :], ALU.mult).then_inc(proj_used, 1)
                    dve.wait_ge(proj_used, 16 * b + 4 * j + 4)
                    own.mark(V.tensor_tensor(q_t[:, j, :], q_t[:, j, :], turned[:, 0, :], ALU.add))
                    own.mark(V.tensor_tensor(k_t[:, j, :], k_t[:, j, :], turned[:, 1, :], ALU.add))
                    own.wait()
                dve.sem_inc(rope_ready, 1)

            def pre_f(b):
                dve.wait_ge(h1_ready, CH * (b + 1))
                norm(h1, u_f).then_inc(uf_ready, 1)
                dve.wait_ge(ut_ready, b + 1)
                own.then(V.tensor_scalar(x_c[:, :], u_t[:, 0:T], conv_w[:, 0:1], conv_b[:, 0:1], ALU.mult, ALU.add))
                own.then(V.scalar_tensor_tensor(x_c[:, :], u_t[:, 1:T + 1], conv_w[:, 1:2], x_c[:, :], ALU.mult, ALU.add))
                own.then(V.scalar_tensor_tensor(x_c[:, :], u_t[:, 2:T + 2], conv_w[:, 2:3], x_c[:, :], ALU.mult, ALU.add))
                V.tensor_tensor(x_f[:, :], x_c[:, :], u_t[:, 1:T + 1], ALU.add).then_inc(xf_ready, 1)
                dve.wait_ge(f_proj, 2 * b + 2)
                for e in range(2):
                    V.tensor_scalar(k_f[:, e, :], F[1][:, :], f_bqk[:, 1:2], parity[:, e:e + 1], ALU.add, ALU.mult
                                    ).then_inc(kf_ready, 1)
                dve.wait_ge(f_vproj, b + 1)
                V.tensor_tensor(v_f[:, :, :, 0:HD], FO[:, :].rearrange("p (c h e) -> p c h e", c=CH, h=H),
                                f_bv[:, :].rearrange("p (h e) -> p h e", h=H).unsqueeze(1).to_broadcast([P, CH, H, HD]),
                                ALU.add).then_inc(vf_ready, 1)

            def a_m(b, u):
                dve.wait_ge(a_scores, UNITS * b + u + 1)
                if u >= 2:
                    dve.wait_ge(a_exp, UNITS * b + u - 1)
                V.tensor_reduce(a_nmax[:, u % 2:u % 2 + 1], A[u % 2][:, :], AX, ALU.max, negate=True).then_inc(a_max, 1)

            def f_top(b, u):
                s, pq = F[u % 2][:, :], u % 2
                wait_apart(dve, (weights_in, LOADS), (f_scores, UNITS * b + u + 1))
                own.then(V.max(top_a[:, pq, :], s))
                own.mark(V.match_replace(f_s[:, pq, :], top_a[:, pq, :], s, NEG))
                if u >= 2:
                    dve.wait_ge(f_exp, UNITS * b + u - 1)
                own.mark(V.tensor_scalar(f_nmax[:, pq:pq + 1], top_a[:, pq, 0:1], -1.0, None, ALU.mult))
                own.wait()
                dve.sem_inc(f_first, 1)
                own.then(V.max(top_b[:, pq, :], f_s[:, pq, :]))
                own.then(V.match_replace(f_s[:, pq, :], top_b[:, pq, :], f_s[:, pq, :], NEG))

            def f_mask(b, u):
                pq = u % 2
                dve.wait_ge(f_exp, UNITS * b + u + 1)
                if u >= 2:
                    dve.wait_ge(f_turned, UNITS * b + u - 1)
                V.scalar_tensor_tensor(f_p[:, pq, :], f_s[:, pq, :], 0.1 * NEG, f_e[:, pq, :], ALU.is_le, ALU.mult
                                       ).then_inc(f_probs, 1)

            def a_n(b, c):
                dve.wait_ge(a_pv, UNITS * b + H * (c + 1))
                own.then(V.reciprocal(a_inv[:, :], a_sum[:, c * H:(c + 1) * H]))
                if not is_(c, 0):
                    dve.wait_ge(a_o_turned, CH * b + c)
                V.tensor_tensor(a_o[:, :].rearrange("p (h e) -> p h e", h=H), AO[:, :].rearrange("p (h e) -> p h e", h=H),
                                a_inv[:, :].unsqueeze(2).to_broadcast([P, H, DH]), ALU.mult).then_inc(a_norm, 1)

            def a_h(b, c):
                dve.wait_ge(a_outed, CH * b + c + 1)
                if c == 0 and not is_(b, 0):
                    dve.wait_ge(hf_ready, b)
                V.tensor_tensor(h1[:, c, :], AT[:, 0:P], h_a[:, c, :], ALU.add).then_inc(h1_ready, 1)

            def f_n(b, c):
                dve.wait_ge(f_pv, UNITS * b + H * (c + 1))
                acc = FO[:, 0:H * (HD + 1)].rearrange("p (h e) -> p h e", h=H)
                own.then(V.reciprocal(f_inv[:, :].unsqueeze(2), acc[:, :, HD:HD + 1]))
                V.tensor_tensor(f_o[:, :].rearrange("p (h e) -> p h e", h=H), acc[:, :, 0:HD],
                                f_inv[:, :].unsqueeze(2).to_broadcast([P, H, HD]), ALU.mult).then_inc(f_norm, 1)

            def f_h(b, c):
                dve.wait_ge(f_outed, CH * b + c + 1)
                if c == 0:
                    dve.wait_ge(hf_ready, b + 1)
                    if not is_(b, 0):
                        dve.wait_ge(out_stored, 16 * b)
                V.tensor_tensor(f_out[:, c, :], FT[:, 0:P], h_f[:, c, :], ALU.add).then_inc(out_ready, 1)

            dve.wait_ge(weights_in, LOADS)
            own.mark(V.tensor_scalar(w_qkv[:, :, :], w_qkv[:, :, :], gamma[:, 0:1], float(D) ** 0.5, ALU.mult, ALU.mult))
            own.mark(V.tensor_scalar(f_bqk[:, 0:1], f_bqk[:, 0:1], float(D) ** -0.5, None, ALU.mult))
            own.wait()
            dve.sem_inc(weights_ready, 1)
            dve.wait_ge(cleared, 2)
            rounds(dve, pre_a, pre_f, [
                ("a", False, 0, a_m), ("f", False, 0, f_top), ("a", True, 4, a_h), ("f", True, 4, f_h),
                ("f", False, 0, f_mask), ("a", True, 2, a_n), ("f", True, 2, f_n)], own)


def build(nc, d, out):
    hidden = nc.dram_tensor("hidden", (TILES, P, D), F32, kind="Internal").ap()
    layer0(nc, d, hidden)
    layer1(nc, d, hidden, out)


def kernel(**inputs):
    import numpy as np
    import concourse.bacc as bacc
    from concourse.bass_utils import run_bass_kernel_spmd as run

    nc = bacc.Bacc("TRN2", target_bir_lowering=False, num_devices=1)
    arrays, d = {}, {}

    def give(name, a):
        a = np.ascontiguousarray(a)
        arrays[f"{name}_dram"] = a
        d[name] = nc.dram_tensor(f"{name}_dram", a.shape, mybir.dt.from_np(a.dtype), kind="ExternalInput").ap()

    v = {k: np.asarray(a) for k, a in inputs.items()}
    give("token_ids", v["x"].reshape(B, TILES, STEPS).transpose(2, 0, 1).reshape(P, TILES))
    give("tok_w", v["L0_tok_W"].T)
    give("w_ih", v["L0_attn_gru_wih"].transpose(2, 0, 1).reshape(P, -1))
    give("w_hh", v["L0_attn_gru_whh"].transpose(2, 0, 1).reshape(P, -1))
    give("gru_bias", np.stack([v["L0_attn_gru_bih"].reshape(-1), v["L0_attn_gru_bhh"].reshape(-1)]))
    for name in ("wq", "wk", "wv"):
        give(f"w_{name[1]}", v[f"L0_attn_{name}"].transpose(2, 0, 1).reshape(P, -1))
    give("w_beat", v["L0_attn_w_beat"].reshape(K, P, 2, P).transpose(3, 0, 2, 1))
    give("w_mix", v["L0_attn_w_mix"].reshape(P, K, P).transpose(2, 1, 0))
    give("norm_g", v["L0_attn_norm_g"].reshape(-1))
    give("norm_b", v["L0_attn_norm_b"].reshape(-1))
    give("bn_g", v["L0_attn_bn_g"])
    give("bn_b", v["L0_attn_bn_b"])
    give("key_wq", v["L0_ffn_Wq"].T)
    give("key_bq", v["L0_ffn_bq"].reshape(H, P).T)
    give("keys", v["L0_ffn_keys"].transpose(1, 3, 0, 2).reshape(P, H, EXPERTS))
    give("experts", np.concatenate([v["L0_ffn_w_down_embed"], v["L0_ffn_w_up_embed"]], axis=1))
    pairs = v["L1_attn_w_qkv"].reshape(D, 3, H * DH // 2, 2)
    plain, swapped = pairs.reshape(D, 3, -1), pairs[..., ::-1].reshape(D, 3, -1)
    give("qkv1", np.stack([plain[:, 0], swapped[:, 0], plain[:, 1], swapped[:, 1], plain[:, 2]], axis=1))
    give("gamma", v["L1_attn_gamma"].reshape(P, 1))
    give("w_out", v["L1_attn_w_out"].reshape(4, P, D).transpose(1, 0, 2))
    give("conv_w", v["L1_ffn_pos_w"].reshape(P, 3))
    give("conv_b", v["L1_ffn_pos_b"].reshape(P, 1))
    give("f_wqkv", v["L1_ffn_qkv_w"].reshape(3, P, D).transpose(2, 0, 1))
    give("f_bqk", v["L1_ffn_qkv_b"][:2 * D].reshape(2, P).T)
    give("f_bv", v["L1_ffn_qkv_b"][2 * D:])
    give("f_wo", v["L1_ffn_wo_w"].T)
    give("f_bo", v["L1_ffn_wo_b"])
    for name, a in shape_constants().items():
        give(name, a)
    out = nc.dram_tensor("out", (B, T, D), F32, kind="ExternalOutput").ap()
    build(nc, d, out)
    r = run(nc, [arrays], core_ids=[0])
    return r.results[0]["out"]


def shape_constants():
    import math

    pos = np.arange(T, dtype=np.float32)[:, None]
    div = np.exp(np.arange(0, D, 2, dtype=np.float32) * (-math.log(10000.0) / D))
    pe = np.zeros((T, D), np.float32)
    pe[:, 0::2] = np.sin(pos * div)
    pe[:, 1::2] = np.cos(pos * div)
    tala = np.zeros((T, D), np.float32)
    slots = D // 4
    half = slots // 2
    harm = np.arange(1, half + 1, dtype=np.float32)
    for n, c in enumerate(CYCLES):
        phase = pos % c / c * 2.0 * math.pi
        tala[:, n * slots:n * slots + half] = np.sin(phase * harm)
        tala[:, n * slots + half:(n + 1) * slots] = np.cos(phase * harm)
    table = (0.5 * pe + 0.5 * tala).astype(np.float32)
    step, seq = np.arange(P) // B, np.arange(P) % B
    mask = np.full((P, K, 2, P), NEG, np.float32)
    for k, c in enumerate(CYCLES):
        for half_ in range(2):
            diff = step[:, None] - (step[None, :] - STEPS * (1 - half_))
            ok = (seq[:, None] == seq[None, :]) & (diff >= 0) & (diff < c)
            mask[:, k, half_, :][ok] = 0.0
    first = mask.copy()
    first[:, :, 0, :] = NEG
    rows = np.zeros((2, 3, 64), np.float32)
    rows[:, 0], rows[0, 1], rows[1, 2] = 1.0, 1.0, 1.0
    inv_freq = (1.0 / ROPE_THETA ** (np.arange(0, DH, 2, dtype=np.float32) / np.float32(DH))).astype(np.float32)
    angle = np.repeat(np.arange(T, dtype=np.float32)[:, None] * inv_freq[None, :], 2, axis=-1).T
    cos, sin = np.cos(angle), np.sin(angle)
    sin[0::2] *= -1.0
    rope = np.stack([cos * DH ** -0.5, sin * DH ** -0.5, cos, sin], axis=1).astype(np.float32)
    head = np.arange(P) // HD
    return {
        "rope": np.tile(rope, (2, 1, 1)),
        "parity": np.stack([head % 2 == 0, head % 2 == 1], axis=1).astype(np.float32),
        "pe": np.repeat(table.reshape(TILES, STEPS, 1, D), B, axis=2).reshape(TILES, P, D),
        "mask": mask.reshape(P, K, 2 * P),
        "mask_first": first.reshape(P, K, 2 * P),
        "bias_rows": rows,
        "ident": np.eye(P, dtype=np.float32),
        "iota8": np.tile(np.arange(TOP, dtype=np.float32), (P, 1)),
    }
```

```python
from contextlib import ExitStack

import numpy as np
import concourse.bass as bass
from concourse import mybir

ALU = mybir.AluOpType
ACT = mybir.ActivationFunctionType
AX = mybir.AxisListType.X
F32 = mybir.dt.float32
I32 = mybir.dt.int32
U32 = mybir.dt.uint32

P = 128
B, T, D = 16, 512, 128
VOCAB = 50257
STEPS = P // B
TILES = T // STEPS
K = 4
CYCLES = (5, 6, 7, 8)
GATES = 3
KB = K * B
NEG = -1e30
LN_EPS = 1e-5
H = 8
TOP = 8
EXPERTS = 128
HALF = 64
SLOTS = H * TOP
GROUPS = 4
GS = SLOTS // GROUPS
GELU_A = 0.7978845608028654
GELU_B = GELU_A * 0.044715
CH = T // P
UNITS = CH * H
DH, HD = 64, 16
ROPE_THETA = 10000.0
RSQRT_SEED = float(0x5F3759DF)


def wait_apart(eng, met, *waits):
    values = [v if isinstance(v, int) else eng.to_reg(v) for _, v in waits]
    eng.wait_ge(*met)
    for (sem, _), value in zip(waits, values):
        eng.wait_ge(sem, value)


class Steps:

    def __init__(self, eng, sem):
        self.eng, self.sem, self.n = eng, sem, 0

    def restart(self):
        self.eng.sem_clear(self.sem)
        self.n = 0

    def then(self, ins):
        ins.then_inc(self.sem, 1)
        self.n += 1
        self.eng.wait_ge(self.sem, self.n)

    def mark(self, ins):
        ins.then_inc(self.sem, 1)
        self.n += 1

    def wait(self):
        self.wait_lag(0)

    def wait_lag(self, lag):
        if self.n > lag:
            self.eng.wait_ge(self.sem, self.n - lag)


def rsqrt(nc, own, out, var, tmp, width, eps):
    v, a, b = (tmp[:, j, 0:width] for j in range(3))
    own.then(nc.vector.tensor_scalar(v, var, eps, None, ALU.add))
    own.then(nc.vector.tensor_scalar(a.bitcast(I32), v.bitcast(I32), 1, None, ALU.logical_shift_right))
    own.then(nc.vector.tensor_scalar(out.bitcast(I32), a.bitcast(I32), -1.0, RSQRT_SEED, ALU.mult, ALU.add))
    for _ in range(3):
        own.then(nc.vector.tensor_tensor(a, out, out, ALU.mult))
        own.then(nc.vector.scalar_tensor_tensor(b, a, -0.5, v, ALU.mult, ALU.mult))
        own.then(nc.vector.scalar_tensor_tensor(out, b, 1.5, out, ALU.add, ALU.mult))


def layer0(nc, d, hidden):
    with ExitStack() as ctx:
        def sb(name, shape, dt=F32):
            return ctx.enter_context(nc.sbuf_tensor(name, shape, dt))

        def pair(name, shape, dt=F32):
            return [sb(f"{name}_of{j}", shape, dt) for j in range(2)]

        def sem(name):
            return ctx.enter_context(nc.semaphore(name))

        w_ih = sb("w_ih", [P, K * GATES * P])
        w_hh = sb("w_hh", [P, K * GATES * P])
        b_in = sb("b_in", [P, K, GATES])
        b_hid = sb("b_hid", [P, K, GATES])
        b_hn = sb("b_hn", [P, K, B])
        w_q = sb("w_q", [P, K * P])
        w_k = sb("w_k", [P, K * P])
        w_v = sb("w_v", [P, K * P])
        w_beat = sb("w_beat", [P, K, 2, P])
        w_mix = sb("w_mix", [P, K, P])
        norm_g = sb("norm_g", [P, K])
        norm_b = sb("norm_b", [P, K])
        bn_g = sb("bn_g", [P, P])
        bn_b = sb("bn_b", [P, P])
        key_wq = sb("key_wq", [P, H * P])
        key_bq = sb("key_bq", [P, H])
        keys = sb("keys", [P, H, 2, EXPERTS])
        ident = sb("ident", [P, P])
        iota8 = sb("iota8", [P, TOP])
        mask = sb("mask", [P, K, 3, P])
        token_ids = sb("token_ids", [P, TILES], I32)
        tile_ids = sb("tile_ids", [P, 1], I32)
        emb = sb("emb", [P, P])
        res = pair("res", [P, P])
        pe_rows = sb("pe_rows", [P, P])
        x_tok = pair("x_tok", [P, P])
        x_t = sb("x_t", [P, P])
        x_gates = pair("x_gates", [P, STEPS, GATES, K, B])
        q_t = sb("q_t", [P, K, P])
        k_t = sb("k_t", [P, K, 2, P])
        v_tok = sb("v_tok", [P, 2, K, P])
        sm = sb("sm", [P, K, 2 * P])
        neg_max = sb("neg_max", [P, K])
        p_sum = sb("p_sum", [P, K])
        p_inv = sb("p_inv", [P, K])
        p_t = sb("p_t", [P, 2, K, P])
        ao_t = sb("ao_t", [P, K, P])
        h_t = pair("h_t", [P, K, STEPS, B])
        r_in = sb("r_in", [P, K, B])
        z_in = sb("z_in", [P, K, B])
        hn_b = sb("hn_b", [P, K, B])
        tr = sb("tr", [P, K, B])
        tz = sb("tz", [P, K, B])
        np1 = sb("np1", [P, K, B])
        np2 = sb("np2", [P, K, B])
        nn = sb("nn", [P, K, B])
        h_n = sb("h_n", [P, K, B])
        zd = sb("zd", [P, K, B])
        thr = sb("thr", [P, K, P])
        thr_t = sb("thr_t", [P, K, P])
        mixed = sb("mixed", [P, P])
        h1 = pair("h1", [P, P])
        stats = sb("stats", [P, K, 6])
        mv = sb("mv", [P, K, 2])
        rstd = sb("rstd", [P, K])
        shift = sb("shift", [P, K])
        nt = sb("nt", [P, 3, K])
        q_tok = pair("q_tok", [P, P])
        qk_t = sb("qk_t", [P, P])
        qh_t = sb("qh_t", [P, H, P])
        top_s = sb("top_s", [P, H, 2, TOP])
        top_i = sb("top_i", [P, H, 2, TOP], U32)
        pairs = sb("pairs", [P, H, TOP * TOP])
        best = sb("best", [P, H, TOP])
        pos = sb("pos", [P, SLOTS], U32)
        pos_hi = sb("pos_hi", [P, SLOTS], U32)
        pos_lo = sb("pos_lo", [P, SLOTS], U32)
        onehot = sb("onehot", [P, SLOTS, TOP])
        onehot2 = sb("onehot2", [P, SLOTS, TOP])
        row_i = sb("row_i", [P, SLOTS])
        row_j = sb("row_j", [P, SLOTS])
        idx = pair("idx", [P, SLOTS], I32)
        best_e = sb("best_e", [P, H, TOP])
        e_sum = sb("e_sum", [P, H])
        e_inv = sb("e_inv", [P, H])
        prob = pair("prob", [P, SLOTS])
        rows = sb("rows", [P, SLOTS, 2 * P])
        h_odd = sb("h_odd", [P, P])
        xd = sb("xd", [P, SLOTS])
        g1 = sb("g1", [P, GS])
        g2 = sb("g2", [P, GS])
        g3 = sb("g3", [P, GS])
        g4 = sb("g4", [P, GS])
        val = sb("val", [P, GS])

        def bank(name):
            return ctx.enter_context(nc.psum_tensor(name, [P, 512], F32))

        nr_bank, z_bank = bank("nr_bank"), bank("z_bank")
        S = [bank(f"S{i}") for i in range(6)]
        KEY_BANKS = [S[1], S[4], S[0], S[5]]
        GATE_BANKS = [S[1], S[4], S[5]]

        def by_thread(ap):
            return ap.rearrange("p (k c) -> p k c", k=K)

        weights_in = sem("weights_in")
        keys_in = sem("keys_in")
        mask_in = sem("mask_in")
        zeroed = sem("zeroed")
        bias_ready = sem("bias_ready")
        id_copied = sem("id_copied")
        emb_in = sem("emb_in")
        pe_in = sem("pe_in")
        emb_used = sem("emb_used")
        x_scaled = sem("x_scaled")
        x_ready = sem("x_ready")
        x_turned = sem("x_turned")
        x_t_ready = sem("x_t_ready")
        xg_done = sem("xg_done")
        xg_ready = sem("xg_ready")
        qkv_done = sem("qkv_done")
        qkv_ready = sem("qkv_ready")
        win_scores = sem("win_scores")
        win_max = sem("win_max")
        win_exp = sem("win_exp")
        win_inv = sem("win_inv")
        win_probs = sem("win_probs")
        win_turned = sem("win_turned")
        win_t_ready = sem("win_t_ready")
        ao_done = sem("ao_done")
        ao_ready = sem("ao_ready")
        nr_ready = sem("nr_ready")
        z_ready = sem("z_ready")
        r_pre = sem("r_pre")
        n_pre = sem("n_pre")
        z_pre = sem("z_pre")
        r_tanh = sem("r_tanh")
        n_tanh = sem("n_tanh")
        z_tanh = sem("z_tanh")
        h_ready = sem("h_ready")
        beat_done = sem("beat_done")
        thr_stats = sem("thr_stats")
        thr_ready = sem("thr_ready")
        thr_turned = sem("thr_turned")
        thr_t_ready = sem("thr_t_ready")
        mix_done = sem("mix_done")
        q_ready = sem("q_ready")
        q_turned = sem("q_turned")
        qk_ready = sem("qk_ready")
        qh_done = sem("qh_done")
        qh_ready = sem("qh_ready")
        key_scores = sem("key_scores")
        key_top = sem("key_top")
        best_ready = sem("best_ready")
        best_exp = sem("best_exp")
        idx_ready = sem("idx_ready")
        rows_in = [sem(f"rows_in{g}") for g in range(GROUPS)]
        gelu_in = sem("gelu_in")
        gelu_tanh = sem("gelu_tanh")
        group_used = sem("group_used")
        stored = sem("stored")
        dve_step = sem("dve_step")
        act_step = sem("act_step")

        consts = [(w_ih, "w_ih"), (w_hh, "w_hh"), (b_in, "b_in"), (b_hid, "b_hid"),
                  (w_q, "w_q"), (w_k, "w_k"), (w_v, "w_v"), (w_beat, "w_beat"), (w_mix, "w_mix"),
                  (norm_g, "norm_g"), (norm_b, "norm_b"),
                  (key_wq, "key_wq"), (key_bq, "key_bq"), (ident, "ident"),
                  (iota8, "iota8"), (token_ids, "token_ids")]
        spread = [(bn_g, "bn_g"), (bn_b, "bn_b")]
        LOADS = 16 * (len(consts) + len(spread))
        XG = GATES * K

        block = ctx.enter_context(nc.Block())

        def rounds(eng, round_):
            round_(0, 0, mixing=False, experts=False)
            round_(1, 1, experts=False)
            with eng.Fori(1, TILES // 2 - 1) as i:
                round_(2 * i, 0)
                round_(2 * i + 1, 1)
            round_(TILES - 2, 0)
            round_(TILES - 1, 1, inputs=False)
            round_(TILES, 0, gru=False, inputs=False)
            round_(TILES + 1, 1, gru=False, inputs=False, mixing=False)

        def at_least(n, v):
            return not isinstance(n, int) or n >= v

        @block.sync
        def _(sync):
            sync.dma_start(mask[:, :, :, :], d["mask_first"]).then_inc(mask_in, 16)
            for t, name in consts:
                sync.dma_start(t[tuple(slice(None) for _ in t.shape)], d[name]).then_inc(weights_in, 16)
            for t, name in spread:
                sync.dma_start(t[:, :], d[name].partition_broadcast(P)).then_inc(weights_in, 16)
            sync.wait_ge(zeroed, 4)
            for c in range(2):
                sync.dma_start(keys[c * HALF:(c + 1) * HALF, :, c, :], d["keys"][c * HALF:(c + 1) * HALF]
                               ).then_inc(keys_in, 16)

            def load_pe(t):
                if at_least(t, 1):
                    sync.wait_ge(x_ready, t)
                sync.dma_start(pe_rows[:, :], d["pe"][t]).then_inc(pe_in, 16)

            load_pe(0)
            load_pe(1)
            sync.wait_ge(win_max, 1)
            sync.dma_start(mask[:, :, :, :], d["mask"]).then_inc(mask_in, 16)

            def round_(n, par, gru=True, inputs=True, mixing=True, experts=True):
                if inputs and not (isinstance(n, int) and n == TILES - 2):
                    load_pe(n + 2)
                if experts:
                    sync.wait_ge(group_used, GROUPS * (n - 1))
                    sync.dma_start(hidden[n - 2], h1[par][:, :]).then_inc(stored, 16)

            rounds(sync, round_)
            sync.wait_ge(stored, 16 * TILES)

        @block.gpsimd
        def _(pool):
            pool.memset(h_t[1][:, :, :, :], 0.0).then_inc(zeroed, 1)
            pool.memset(k_t[:, :, :, :], 0.0).then_inc(zeroed, 1)
            pool.memset(v_tok[:, :, :, :], 0.0).then_inc(zeroed, 1)
            pool.memset(keys[:, :, :, :], 0.0).then_inc(zeroed, 1)
            pool.wait_ge(weights_in, LOADS)

            def embed(t):
                if at_least(t, 1):
                    pool.wait_ge(emb_used, 2 * t)
                    pool.wait_ge(emb_in, 16 * t)
                pool.tensor_copy(tile_ids[:, :], token_ids[:, bass.ds(t, 1)]).then_inc(id_copied, 1)
                wait_apart(pool, (weights_in, LOADS), (id_copied, t + 1))
                pool.indirect_dma_start(out=emb[:, :], out_offset=None, in_=d["tok_w"],
                                        in_offset=bass.IndirectOffsetOnAxis(ap=tile_ids[:, :].bitcast(U32), axis=0)
                                        ).then_inc(emb_in, 16)

            def gather(t, par):
                wait_apart(pool, (weights_in, LOADS), (idx_ready, t + 1))
                for g in range(GROUPS):
                    if at_least(t, 1):
                        wait_apart(pool, (weights_in, LOADS), (group_used, GROUPS * (t - 1) + g + 1))
                    for j in range(g * GS, (g + 1) * GS):
                        pool.indirect_dma_start(out=rows[:, j, :], out_offset=None, in_=d["experts"],
                                                in_offset=bass.IndirectOffsetOnAxis(ap=idx[par][:, j:j + 1].bitcast(U32), axis=0)
                                                ).then_inc(rows_in[g], 16)

            for t in range(3):
                embed(t)
            for t in range(2):
                embed(t + 3)
                gather(t, t % 2)
            with pool.Fori(1, TILES // 2 - 2) as i:
                embed(2 * i + 3)
                gather(2 * i, 0)
                embed(2 * i + 4)
                gather(2 * i + 1, 1)
            embed(TILES - 1)
            for t in range(TILES - 4, TILES):
                gather(t, t % 2)

        @block.tensor
        def _(pe):
            def turn_x(t, par):
                pe.wait_ge(x_ready, t + 1)
                if at_least(t, 1):
                    pe.wait_ge(win_t_ready, 2 * t)
                pe.transpose(S[3][:, 0:P], x_tok[par][:, :], ident[:, :]).then_inc(x_turned, 1)

            def input_gates(t):
                pe.wait_ge(x_t_ready, t + 1)
                if at_least(t, 1):
                    pe.wait_ge(qkv_ready, 3 * t)
                if at_least(t, 2):
                    pe.wait_ge(key_top, 4 * (t - 1))
                for g in range(GATES):
                    for k in range(K):
                        c = (k * GATES + g) * P
                        m = pe.matmul(GATE_BANKS[g][:, k * P:(k + 1) * P], w_ih[:, c:c + P], x_t[:, :],
                                      start=(k == 0), stop=True, skip_group_check=True)
                    m.then_inc(xg_done, 1)

            def gru_step(n, s, par):
                if at_least(n, 1) or s:
                    pe.wait_ge(h_ready, STEPS * n + s)
                prev = h_t[par][:, :, s - 1, :] if s else h_t[1 - par][:, :, STEPS - 1, :]
                for out, g in ((nr_bank[:, 0:KB], 2), (nr_bank[:, KB:2 * KB], 0), (z_bank[:, 0:KB], 1)):
                    for k in range(K):
                        c = (k * GATES + g) * P
                        m = pe.matmul(out[:, k * B:(k + 1) * B], w_hh[:, c:c + P], prev[:, k, :],
                                      start=(k == 0 and g != 0), stop=True, skip_group_check=True)
                    if g == 0:
                        m.then_inc(nr_ready, 1)
                m.then_inc(z_ready, 1)

            def beat(n, par):
                pe.wait_ge(h_ready, STEPS * (n + 1))
                pe.wait_ge(ao_ready, n + 1)
                if at_least(n, 1):
                    pe.wait_ge(key_top, 4 * n)
                for k in range(K):
                    pe.matmul(S[0][:, k * P:(k + 1) * P], h_t[par][:, k, :, :], w_beat[:, k, 0, :],
                              start=(k == 0), stop=False, skip_group_check=True)
                    m = pe.matmul(S[0][:, k * P:(k + 1) * P], ao_t[:, k, :], w_beat[:, k, 1, :],
                                  start=False, stop=True, skip_group_check=True)
                m.then_inc(beat_done, 1)

            def turn_thr(n):
                pe.wait_ge(thr_ready, 4 * (n + 1))
                last = min(n + 1, TILES - 1) if isinstance(n, int) else n + 1
                pe.wait_ge(xg_ready, XG * (last + 1))
                for k in range(K):
                    m = pe.transpose(S[1][:, k * P:(k + 1) * P], thr[:, k, :], ident[:, :])
                m.then_inc(thr_turned, 1)

            def mix(n):
                pe.wait_ge(thr_t_ready, 4 * (n + 1))
                for k in range(K):
                    m = pe.matmul(S[0][:, 0:P], thr_t[:, k, :], w_mix[:, k, :], start=(k == 0), stop=(k == K - 1))
                m.then_inc(mix_done, 1)

            def window_qkv(n, par):
                pe.wait_ge(x_t_ready, n + 1)
                pe.wait_ge(xg_ready, XG * (n + 1))
                if at_least(n, 1):
                    pe.wait_ge(ao_ready, n)
                for b, w in ((2, w_q), (3, w_k)):
                    for k in range(K):
                        m = pe.matmul(S[b][:, k * P:(k + 1) * P], w[:, k * P:(k + 1) * P], x_t[:, :],
                                      start=(k == 0), stop=True, skip_group_check=True)
                    m.then_inc(qkv_done, 1)
                pe.matmul(S[4][:, :], x_t[:, :], w_v[:, :], start=True, stop=True).then_inc(qkv_done, 1)

            def window_scores(n):
                pe.wait_ge(qkv_ready, 3 * n + 2)
                for k in range(K):
                    m = pe.matmul(S[2 + k // 2][:, (k % 2) * 256:(k % 2 + 1) * 256], q_t[:, k, :], k_t[:, k, :, :],
                                  start=(k % 2 == 0), stop=True, skip_group_check=True)
                m.then_inc(win_scores, 1)

            def window_turn(n):
                pe.wait_ge(win_probs, 4 * (n + 1))
                for slot in range(2):
                    for k in range(K):
                        m = pe.transpose(S[2 + slot][:, k * P:(k + 1) * P], sm[:, k, slot * P:(slot + 1) * P], ident[:, :])
                    m.then_inc(win_turned, 1)

            def window_rows(n):
                pe.wait_ge(win_t_ready, 2 * (n + 1))
                pe.wait_ge(qkv_ready, 3 * (n + 1))
                for k in range(K):
                    for slot in range(2):
                        m = pe.matmul(S[2][:, k * P:(k + 1) * P], v_tok[:, slot, k, :], p_t[:, slot, k, :],
                                      start=(k == 0 and slot == 0), stop=(slot == 1), skip_group_check=True)
                m.then_inc(ao_done, 1)

            def turn_q(n, par):
                pe.wait_ge(q_ready, n + 1)
                pe.transpose(S[1][:, 0:P], q_tok[par][:, :], ident[:, :]).then_inc(q_turned, 1)

            def key_queries(n):
                pe.wait_ge(qk_ready, n + 1)
                for h in range(H):
                    m = pe.matmul(S[0 if h < 4 else 5][:, (h % 4) * P:(h % 4 + 1) * P], key_wq[:, h * P:(h + 1) * P],
                                  qk_t[:, :], start=(h % 4 == 0), stop=True, skip_group_check=True)
                    if h % 4 == 3:
                        m.then_inc(qh_done, 1)

            def key_products(n, window):
                if window:
                    pe.wait_ge(qkv_ready, 3 * (n + 2))
                for g in range(4):
                    pe.wait_ge(qh_ready, H * n + 2 * g + 2)
                    for j in range(2):
                        m = pe.matmul(KEY_BANKS[g][:, j * 256:(j + 1) * 256], qh_t[:, 2 * g + j, :],
                                      keys[:, 2 * g + j, :, :], start=(j == 0), stop=True, skip_group_check=True)
                    m.then_inc(key_scores, 1)

            def round_(n, par, gru=True, inputs=True, mixing=True, experts=True):
                odd = 1 - par
                if gru:
                    gru_step(n, 0, par)
                if mixing:
                    beat(n - 1, odd)
                if gru:
                    gru_step(n, 1, par)
                if mixing:
                    turn_thr(n - 1)
                if gru:
                    window_qkv(n, par)
                if mixing:
                    mix(n - 1)
                if gru:
                    gru_step(n, 2, par)
                if mixing:
                    turn_q(n - 1, odd)
                if gru:
                    window_scores(n)
                if mixing:
                    key_queries(n - 1)
                if gru:
                    gru_step(n, 3, par)
                if mixing:
                    key_products(n - 1, gru)
                if gru:
                    gru_step(n, 4, par)
                    window_turn(n)
                    gru_step(n, 5, par)
                if inputs:
                    turn_x(n + 1, odd)
                if gru:
                    window_rows(n)
                    gru_step(n, 6, par)
                if inputs:
                    input_gates(n + 1)
                if gru:
                    gru_step(n, 7, par)

            pe.wait_ge(weights_in, LOADS)
            pe.wait_ge(keys_in, 32)
            pe.wait_ge(zeroed, 4)
            turn_x(0, 0)
            input_gates(0)
            rounds(pe, round_)

        @block.scalar
        def _(act):
            own = Steps(act, act_step)

            def keep_rows(t, par):
                act.wait_ge(emb_in, 16 * (t + 1))
                if at_least(t, 2):
                    act.wait_ge(q_ready, t - 1)
                nc.scalar.copy(res[par][:, :], emb[:, :]).then_inc(emb_used, 1)

            def turn_x(t):
                act.wait_ge(x_turned, t + 1)
                if at_least(t, 1):
                    act.wait_ge(qkv_done, 3 * t)
                nc.scalar.copy(x_t[:, :], S[3][:, 0:P]).then_inc(x_t_ready, 1)

            def input_gates(t, par):
                for g in range(GATES):
                    act.wait_ge(xg_done, GATES * t + g + 1)
                    for k in range(K):
                        nc.scalar.activation(x_gates[par][:, :, g, k, :],
                                             GATE_BANKS[g][:, k * P:(k + 1) * P].rearrange("p (s b) -> p s b", s=STEPS),
                                             ACT.Identity, bias=b_in[:, k, g:g + 1]).then_inc(xg_ready, 1)

            def gru_step(n, s):
                t = STEPS * n + s + 1
                act.wait_ge(r_pre, t)
                nc.scalar.activation(tr[:, :, :], r_in[:, :, :], ACT.Tanh, scale=0.5).then_inc(r_tanh, 1)
                act.wait_ge(n_pre, t)
                nc.scalar.activation(nn[:, :, :], np2[:, :, :], ACT.Tanh).then_inc(n_tanh, 1)
                act.wait_ge(z_pre, t)
                nc.scalar.activation(tz[:, :, :], z_in[:, :, :], ACT.Tanh, scale=0.5).then_inc(z_tanh, 1)

            def scale_thr(n):
                act.wait_ge(thr_stats, n + 1)
                for k in range(K):
                    nc.scalar.activation(thr[:, k, :], thr[:, k, :], ACT.Identity, scale=rstd[:, k:k + 1],
                                         bias=shift[:, k:k + 1]).then_inc(thr_ready, 1)

            def turn_thr(n):
                act.wait_ge(thr_turned, n + 1)
                for k in range(K):
                    nc.scalar.activation(thr_t[:, k, :], S[1][:, k * P:(k + 1) * P], ACT.Identity,
                                         scale=norm_g[:, k:k + 1], bias=norm_b[:, k:k + 1]).then_inc(thr_t_ready, 1)

            def window_qkv(n, par):
                for w, (dst, b) in enumerate(((q_t[:, :, :], 2), (k_t[:, :, par, :], 3), (v_tok[:, par, :, :], 4))):
                    act.wait_ge(qkv_done, 3 * n + w + 1)
                    nc.scalar.copy(dst, by_thread(S[b][:, :])).then_inc(qkv_ready, 1)

            def window_exp(n):
                act.wait_ge(win_max, n + 1)
                for k in range(K):
                    nc.scalar.activation(sm[:, k, :], sm[:, k, :], ACT.Exp, bias=neg_max[:, k:k + 1],
                                         accum_out=p_sum[:, k:k + 1]).then_inc(win_exp, 1)

            def window_probs(n):
                act.wait_ge(win_inv, n + 1)
                for k in range(K):
                    nc.scalar.activation(sm[:, k, :], sm[:, k, :], ACT.Copy, scale=p_inv[:, k:k + 1]).then_inc(win_probs, 1)

            def window_turn(n):
                for slot in range(2):
                    act.wait_ge(win_turned, 2 * n + slot + 1)
                    nc.scalar.copy(p_t[:, slot, :, :], by_thread(S[2 + slot][:, :])).then_inc(win_t_ready, 1)

            def window_rows(n):
                act.wait_ge(ao_done, n + 1)
                nc.scalar.copy(ao_t[:, :, :], by_thread(S[2][:, :])).then_inc(ao_ready, 1)

            def turn_q(n):
                act.wait_ge(q_turned, n + 1)
                nc.scalar.copy(qk_t[:, :], S[1][:, 0:P]).then_inc(qk_ready, 1)

            def key_queries(n):
                for h in range(H):
                    if h % 4 == 0:
                        act.wait_ge(qh_done, 2 * n + h // 4 + 1)
                    nc.scalar.activation(qh_t[:, h, :], S[0 if h < 4 else 5][:, (h % 4) * P:(h % 4 + 1) * P],
                                         ACT.Identity, bias=key_bq[:, h:h + 1]).then_inc(qh_ready, 1)

            def best_weights(n):
                act.wait_ge(best_ready, n + 1)
                nc.scalar.activation(best_e[:, :, :], best_e[:, :, :], ACT.Exp).then_inc(best_exp, 1)

            def gelu(n, g):
                act.wait_ge(gelu_in, GROUPS * n + g + 1)
                nc.scalar.activation(g3[:, :], g2[:, :], ACT.Tanh).then_inc(gelu_tanh, 1)

            def round_(n, par, gru=True, inputs=True, mixing=True, experts=True):
                odd = 1 - par
                if gru:
                    gru_step(n, 0)
                if mixing:
                    scale_thr(n - 1)
                if gru:
                    gru_step(n, 1)
                if mixing:
                    turn_thr(n - 1)
                if gru:
                    window_qkv(n, par)
                    gru_step(n, 2)
                if mixing:
                    turn_q(n - 1)
                if experts:
                    gelu(n - 2, 0)
                if mixing:
                    key_queries(n - 1)
                if gru:
                    window_exp(n)
                    gru_step(n, 3)
                    window_probs(n)
                if inputs:
                    keep_rows(n + 1, odd)
                if gru:
                    gru_step(n, 4)
                if experts:
                    gelu(n - 2, 1)
                if gru:
                    window_turn(n)
                    gru_step(n, 5)
                if inputs:
                    turn_x(n + 1)
                if gru:
                    window_rows(n)
                if mixing:
                    best_weights(n - 1)
                if gru:
                    gru_step(n, 6)
                if experts:
                    gelu(n - 2, 2)
                if inputs:
                    input_gates(n + 1, odd)
                if gru:
                    gru_step(n, 7)
                if experts:
                    gelu(n - 2, 3)

            nc.scalar.preload_act_table_set("exp_and_others")
            act.wait_ge(zeroed, 4)
            act.wait_ge(bias_ready, 1)
            keep_rows(0, 0)
            turn_x(0)
            input_gates(0, 0)
            rounds(act, round_)

        @block.vector
        def _(dve):
            own = Steps(dve, dve_step)
            V = nc.vector

            def norm_stats(x, k):
                own.then(V.bn_stats(stats[:, k, :], x))
                own.then(V.bn_aggr(mv[:, k, :], stats[:, k, :]))

            def make_x(t, par):
                dve.wait_ge(emb_in, 16 * (t + 1))
                norm_stats(emb[:, :], 0)
                rsqrt(nc, own, rstd[:, 0:1], mv[:, 0, 1:2], nt, 1, LN_EPS)
                V.tensor_scalar(x_tok[par][:, :], emb[:, :], mv[:, 0, 0:1], rstd[:, 0:1], ALU.subtract, ALU.mult
                                ).then_inc(emb_used, 1)
                dve.wait_ge(emb_used, 2 * (t + 1))
                dve.wait_ge(pe_in, 16 * (t + 1))
                V.tensor_tensor(x_tok[par][:, :], x_tok[par][:, :], pe_rows[:, :], ALU.add).then_inc(x_ready, 1)

            def window_mask(n, par):
                dve.wait_ge(win_scores, n + 1)
                own.wait()
                for j in range(2):
                    own.mark(V.scalar_tensor_tensor(
                        sm[:, 2 * j:2 * j + 2, :].rearrange("p k (s t) -> p k s t", s=2),
                        S[2 + j][:, :].rearrange("p (k s t) -> p k s t", k=2, s=2), float(D) ** -0.5,
                        mask[:, 2 * j:2 * j + 2, 1 - par:3 - par, :], ALU.mult, ALU.add))
                own.wait()
                V.tensor_reduce(neg_max[:, :], sm[:, :, :], AX, ALU.max, negate=True).then_inc(win_max, 1)

            def window_inv(n):
                dve.wait_ge(win_exp, 4 * (n + 1))
                V.reciprocal(p_inv[:, :], p_sum[:, :]).then_inc(win_inv, 1)

            def gru_step(n, s, par, dots=None):
                t = STEPS * n + s + 1
                x_of = x_gates[par][:, s, :, :, :]
                prev = h_t[par][:, :, s - 1, :] if s else h_t[1 - par][:, :, STEPS - 1, :]
                if s == 0:
                    dve.wait_ge(xg_ready, XG * (n + 1))
                dve.wait_ge(nr_ready, t)
                V.tensor_tensor(r_in[:, :, :], by_thread(nr_bank[:, KB:2 * KB]), x_of[:, 0, :, :], ALU.add).then_inc(r_pre, 1)
                own.mark(V.tensor_tensor(hn_b[:, :, :], by_thread(nr_bank[:, 0:KB]), b_hn[:, :, :], ALU.add))
                if dots:
                    dots(0)
                own.wait()
                dve.wait_ge(r_tanh, t)
                own.then(V.scalar_tensor_tensor(np1[:, :, :], tr[:, :, :], 1.0, hn_b[:, :, :], ALU.add, ALU.mult))
                V.scalar_tensor_tensor(np2[:, :, :], np1[:, :, :], 0.5, x_of[:, 2, :, :], ALU.mult, ALU.add).then_inc(n_pre, 1)
                if dots:
                    dots(1)
                dve.wait_ge(z_ready, t)
                V.tensor_tensor(z_in[:, :, :], by_thread(z_bank[:, 0:KB]), x_of[:, 1, :, :], ALU.add).then_inc(z_pre, 1)
                dve.wait_ge(n_tanh, t)
                own.mark(V.tensor_tensor(h_n[:, :, :], prev, nn[:, :, :], ALU.subtract))
                if dots:
                    dots(2)
                own.wait()
                dve.wait_ge(z_tanh, t)
                own.then(V.scalar_tensor_tensor(zd[:, :, :], tz[:, :, :], 1.0, h_n[:, :, :], ALU.add, ALU.mult))
                V.scalar_tensor_tensor(h_t[par][:, :, s, :], zd[:, :, :], 0.5, nn[:, :, :], ALU.mult, ALU.add
                                       ).then_inc(h_ready, 1)

            def norm_threads(n, par):
                dve.wait_ge(beat_done, n + 1)
                own.then(V.tensor_tensor(thr[:, :, :], by_thread(S[0][:, :]),
                                         x_tok[par][:, :].unsqueeze(1).to_broadcast([P, K, P]), ALU.add))
                for k in range(K):
                    own.mark(V.bn_stats(stats[:, k, :], thr[:, k, :]))
                own.wait()
                for k in range(K):
                    own.mark(V.bn_aggr(mv[:, k, :], stats[:, k, :]))
                own.wait()
                rsqrt(nc, own, rstd[:, :], mv[:, :, 1], nt, K, LN_EPS)
                V.scalar_tensor_tensor(shift[:, :], mv[:, :, 0], -1.0, rstd[:, :], ALU.mult, ALU.mult).then_inc(thr_stats, 1)

            def norm_mixture(n, par):
                dve.wait_ge(mix_done, n + 1)
                own.then(V.tensor_tensor(mixed[:, :], S[0][:, 0:P], x_tok[par][:, :], ALU.add))
                norm_stats(mixed[:, :], 0)
                rsqrt(nc, own, rstd[:, 0:1], mv[:, 0, 1:2], nt, 1, LN_EPS)
                own.then(V.tensor_scalar(mixed[:, :], mixed[:, :], mv[:, 0, 0:1], rstd[:, 0:1], ALU.subtract, ALU.mult))
                own.then(V.tensor_tensor(mixed[:, :], mixed[:, :], bn_g[:, :], ALU.mult))
                own.then(V.tensor_tensor(mixed[:, :], mixed[:, :], bn_b[:, :], ALU.add))
                if at_least(n, 2):
                    dve.wait_ge(stored, 16 * (n - 1))
                own.then(V.tensor_tensor(h1[par][:, :], mixed[:, :], res[par][:, :], ALU.add))
                norm_stats(h1[par][:, :], 0)
                rsqrt(nc, own, rstd[:, 0:1], mv[:, 0, 1:2], nt, 1, LN_EPS)
                V.tensor_scalar(q_tok[par][:, :], h1[par][:, :], mv[:, 0, 0:1], rstd[:, 0:1], ALU.subtract, ALU.mult
                                ).then_inc(q_ready, 1)
                dve.wait_ge(q_ready, n + 1)

            def key_tops(n, g):
                wait_apart(dve, (zeroed, 4), (key_scores, 4 * n + g + 1))
                cuts = [(2 * g + j, c, KEY_BANKS[g][:, (2 * j + c) * P:(2 * j + c + 1) * P])
                        for j in range(2) for c in range(2)]
                for h, c, src in cuts:
                    own.mark(V.max(top_s[:, h, c, :], src))
                own.wait()
                for h, c, src in cuts[:-1]:
                    own.mark(V.max_index(top_i[:, h, c, :], top_s[:, h, c, :], src))
                h, c, src = cuts[-1]
                V.max_index(top_i[:, h, c, :], top_s[:, h, c, :], src).then_inc(key_top, 1)

            def best_pairs(n):
                own.then(V.tensor_tensor(pairs[:, :, :].rearrange("p h (i j) -> p h i j", i=TOP),
                                         top_s[:, :, 0, :].unsqueeze(3).to_broadcast([P, H, TOP, TOP]),
                                         top_s[:, :, 1, :].unsqueeze(2).to_broadcast([P, H, TOP, TOP]), ALU.add))
                for h in range(H):
                    own.mark(V.max(best[:, h, :], pairs[:, h, :]))
                own.wait()
                V.tensor_tensor(best_e[:, :, :], best[:, :, :], best[:, :, 0:1].to_broadcast([P, H, TOP]), ALU.subtract
                                ).then_inc(best_ready, 1)
                for h in range(H):
                    own.mark(V.max_index(pos[:, h * TOP:(h + 1) * TOP], best[:, h, :], pairs[:, h, :]))
                own.wait()

            def expert_rows(n, par):
                own.mark(V.tensor_scalar(pos_hi[:, :], pos[:, :], 3, None, ALU.logical_shift_right))
                own.mark(V.tensor_scalar(pos_lo[:, :], pos[:, :], 7, None, ALU.bitwise_and))
                own.wait()
                dve.wait_ge(key_top, 4 * (n + 1))
                sides = ((pos_hi, onehot, row_i, 0), (pos_lo, onehot2, row_j, 1))
                for p_, oh, r, c in sides:
                    own.mark(V.tensor_tensor(oh[:, :, :], p_[:, :].unsqueeze(2).to_broadcast([P, SLOTS, TOP]),
                                             iota8[:, :].unsqueeze(1).to_broadcast([P, SLOTS, TOP]), ALU.is_equal))
                for p_, oh, r, c in sides:
                    own.wait_lag(1)
                    own.mark(V.tensor_tensor(oh[:, :, :].rearrange("p (h k) e -> p h k e", h=H),
                                             oh[:, :, :].rearrange("p (h k) e -> p h k e", h=H),
                                             top_i[:, :, c, :].unsqueeze(2).to_broadcast([P, H, TOP, TOP]), ALU.mult))
                for p_, oh, r, c in sides:
                    own.wait_lag(1)
                    own.mark(V.tensor_reduce(r[:, :], oh[:, :, :], AX, ALU.add))
                own.wait()
                V.scalar_tensor_tensor(idx[par][:, :], row_i[:, :], float(EXPERTS), row_j[:, :], ALU.mult, ALU.add
                                       ).then_inc(idx_ready, 1)

            def expert_probs(n, par):
                dve.wait_ge(best_exp, n + 1)
                own.then(V.tensor_reduce(e_sum[:, :], best_e[:, :, :], AX, ALU.add))
                own.then(V.reciprocal(e_inv[:, :], e_sum[:, :]))
                own.then(V.tensor_tensor(prob[par][:, :].rearrange("p (h k) -> p h k", h=H), best_e[:, :, :],
                                         e_inv[:, :].unsqueeze(2).to_broadcast([P, H, TOP]), ALU.mult))

            def down(n, g, par, js):
                if js[0] == 0:
                    dve.wait_ge(rows_in[g], 16 * GS * (n + 1))
                for j in js:
                    row = rows[:, g * GS + j, 0:P]
                    own.mark(V.tensor_tensor_reduce(row, row, q_tok[par][:, :], 1.0, 0.0, ALU.mult, ALU.add,
                                                    xd[:, g * GS + j:g * GS + j + 1]))

            def gelu_in_(n, g):
                x = xd[:, g * GS:(g + 1) * GS]
                own.wait()
                own.then(V.tensor_tensor(g1[:, :], x, x, ALU.mult))
                own.then(V.tensor_scalar(g1[:, :], g1[:, :], GELU_B, GELU_A, ALU.mult, ALU.add))
                V.tensor_tensor(g2[:, :], g1[:, :], x, ALU.mult).then_inc(gelu_in, 1)

            def up(n, g, par):
                x = xd[:, g * GS:(g + 1) * GS]
                dve.wait_ge(gelu_tanh, GROUPS * n + g + 1)
                own.then(V.scalar_tensor_tensor(g4[:, :], g3[:, :], 1.0, x, ALU.add, ALU.mult))
                own.then(V.scalar_tensor_tensor(val[:, :], g4[:, :], 0.5, prob[par][:, g * GS:(g + 1) * GS],
                                                ALU.mult, ALU.mult))
                for j in range(GS):
                    row, w = rows[:, g * GS + j, P:2 * P], val[:, j:j + 1]
                    if j > 1:
                        own.wait_lag(1)
                    acc = h_odd if j % 2 else h1[par]
                    if g == 0 and j == 1:
                        own.mark(V.tensor_scalar(acc[:, :], row, w, None, ALU.mult))
                    else:
                        own.mark(V.scalar_tensor_tensor(acc[:, :], row, w, acc[:, :], ALU.mult, ALU.add))
                own.wait()
                if g < GROUPS - 1:
                    dve.sem_inc(group_used, 1)
                else:
                    V.tensor_tensor(h1[par][:, :], h1[par][:, :], h_odd[:, :], ALU.add).then_inc(group_used, 1)

            DOTS = {1: (0, (range(0, 3), range(3, 6), range(6, 8))), 2: (0, (range(8, 11), range(11, 14), range(14, 16))),
                    3: (1, (range(0, 3), range(3, 6), range(6, 8))), 4: (1, (range(8, 11), range(11, 14), range(14, 16))),
                    5: (2, (range(0, 3), range(3, 6), range(6, 8))), 6: (2, (range(8, 11), range(11, 14), range(14, 16))),
                    7: (3, (range(0, 5), range(5, 11), range(11, 16)))}

            def round_(n, par, gru=True, inputs=True, mixing=True, experts=True):
                odd = 1 - par
                own.wait()
                own.restart()

                def step(s):
                    g, gaps = DOTS.get(s, (None, None))

                    def dots(i):
                        down(n - 2, g, par, gaps[i])

                    use = dots if experts and gaps else None
                    if gru:
                        gru_step(n, s, par, use)
                    elif use:
                        for i in range(3):
                            use(i)

                step(0)
                if mixing:
                    norm_threads(n - 1, odd)
                step(1)
                if mixing:
                    norm_mixture(n - 1, odd)
                step(2)
                if experts:
                    gelu_in_(n - 2, 0)
                if gru:
                    if isinstance(n, int) and n == 1:
                        dve.wait_ge(mask_in, 32)
                    window_mask(n, par)
                if experts:
                    up(n - 2, 0, par)
                step(3)
                if gru:
                    window_inv(n)
                if mixing:
                    key_tops(n - 1, 0)
                    key_tops(n - 1, 1)
                if inputs:
                    make_x(n + 1, odd)
                step(4)
                if experts:
                    gelu_in_(n - 2, 1)
                if mixing:
                    key_tops(n - 1, 2)
                    key_tops(n - 1, 3)
                if experts:
                    up(n - 2, 1, par)
                step(5)
                if mixing:
                    best_pairs(n - 1)
                step(6)
                if experts:
                    gelu_in_(n - 2, 2)
                if mixing:
                    expert_rows(n - 1, odd)
                if experts:
                    up(n - 2, 2, par)
                step(7)
                if experts:
                    gelu_in_(n - 2, 3)
                if mixing:
                    expert_probs(n - 1, odd)
                if experts:
                    up(n - 2, 3, par)

            dve.wait_ge(weights_in, LOADS)
            dve.wait_ge(zeroed, 4)
            dve.wait_ge(mask_in, 16)
            own.mark(V.tensor_tensor(b_in[:, :, 0:2], b_in[:, :, 0:2], b_hid[:, :, 0:2], ALU.add))
            own.mark(V.tensor_copy(b_hn[:, :, :], b_hid[:, :, 2:3].to_broadcast([P, K, B])))
            own.wait()
            dve.sem_inc(bias_ready, 1)
            make_x(0, 0)
            rounds(dve, round_)


def layer1(nc, d, hidden, out):
    with ExitStack() as ctx:
        def sb(name, shape, dt=F32):
            return ctx.enter_context(nc.sbuf_tensor(name, shape, dt))

        def sem(name):
            return ctx.enter_context(nc.semaphore(name))

        def bank(name):
            return ctx.enter_context(nc.psum_tensor(name, [P, 512], F32))

        w_qkv = sb("w_qkv", [P, 5, T])
        gamma = sb("gamma", [P, 1])
        rope = sb("rope", [P, 4, T])
        w_out = sb("w_out", [P, 4, P])
        ident = sb("ident1", [P, P])
        conv_w = sb("conv_w", [P, 3])
        conv_b = sb("conv_b", [P, 1])
        f_wqkv = sb("f_wqkv", [P, 3, P])
        f_bqk = sb("f_bqk", [P, 2])
        f_bv = sb("f_bv", [P, P])
        f_wo = sb("f_wo", [P, P])
        f_bo = sb("f_bo", [P, P])
        parity = sb("parity", [P, 2])
        h_in = sb("h_in", [P, CH, P])
        h_a = sb("h_a", [P, CH, P])
        u_a = sb("u_a", [P, CH, P])
        sq = sb("sq", [P, P])
        stats = sb("stats1", [P, CH, 6])
        mv = sb("mv1", [P, CH, 2])
        rstd = sb("rstd1", [P, CH])
        ss = sb("ss", [P, CH])
        nt = sb("nt1", [P, 3, CH])
        xn_t = sb("xn_t", [P, T])
        q_t = sb("q_t1", [P, 4, T])
        k_t = sb("k_t1", [P, 4, T])
        v_a = sb("v_a", [P, CH, T])
        turned = sb("turned", [P, 2, T])
        a_nmax = sb("a_nmax", [P, 2])
        a_sum = sb("a_sum", [P, UNITS])
        a_inv = sb("a_inv", [P, H])
        a_p = sb("a_p", [P, 2, T])
        a_pt = sb("a_pt", [P, 2, CH, P])
        a_o = sb("a_o", [P, T])
        a_ot = sb("a_ot", [P, 4, P])
        h1 = sb("h_mid", [P, CH, P])
        h_f = sb("h_f", [P, CH, P])
        u_f = sb("u_f", [P, CH, P])
        u_t = sb("u_t", [P, T + 2])
        x_c = sb("x_c", [P, T])
        x_f = sb("x_f", [P, T])
        q_f = sb("q_f", [P, T])
        k_f = sb("k_f", [P, 2, T])
        v_f = sb("v_f", [P, CH, H, HD + 1])
        top_a = sb("top_a", [P, 2, TOP])
        top_b = sb("top_b", [P, 2, TOP])
        f_nmax = sb("f_nmax", [P, 2])
        f_s = sb("f_s", [P, 2, T])
        f_e = sb("f_e", [P, 2, T])
        f_p = sb("f_p", [P, 2, T])
        f_pt = sb("f_pt", [P, 2, CH, P])
        f_inv = sb("f_inv", [P, H])
        f_o = sb("f_o", [P, P])
        f_ot = sb("f_ot", [P, P])
        f_out = sb("f_out", [P, CH, P])

        A = [bank("A0"), bank("A1")]
        AT, AO = bank("AT"), bank("AO")
        F = [bank("F0"), bank("F1")]
        FT, FO = bank("FT"), bank("FO")

        weights_in = sem("weights_in1")
        weights_ready = sem("weights_ready")
        cleared = sem("cleared1")
        h_loaded = sem("h_loaded")
        h_taken = sem("h_taken")
        squares = sem("squares")
        squares_done = sem("squares_done")
        rope_ready = sem("rope_ready")
        u_scaled = sem("u_scaled")
        xn_turned = sem("xn_turned")
        xn_ready = sem("xn_ready")
        proj = sem("proj")
        proj_used = sem("proj_used")
        v_proj = sem("v_proj")
        v_ready = sem("v_ready")
        a_scores = sem("a_scores")
        a_max = sem("a_max")
        a_exp = sem("a_exp")
        a_turned = sem("a_turned")
        a_t_ready = sem("a_t_ready")
        a_pv = sem("a_pv")
        a_norm = sem("a_norm")
        a_o_turned = sem("a_o_turned")
        a_ot_ready = sem("a_ot_ready")
        a_outed = sem("a_outed")
        h1_ready = sem("h1_ready")
        hf_ready = sem("hf_ready")
        uf_ready = sem("uf_ready")
        uf_turned = sem("uf_turned")
        ut_ready = sem("ut_ready")
        xf_ready = sem("xf_ready")
        f_proj = sem("f_proj")
        qf_ready = sem("qf_ready")
        kf_ready = sem("kf_ready")
        f_vproj = sem("f_vproj")
        vf_ready = sem("vf_ready")
        f_scores = sem("f_scores")
        f_first = sem("f_first")
        f_exp = sem("f_exp")
        f_probs = sem("f_probs")
        f_turned = sem("f_turned")
        f_t_ready = sem("f_t_ready")
        f_pv = sem("f_pv")
        f_norm = sem("f_norm")
        f_o_turned = sem("f_o_turned")
        f_ot_ready = sem("f_ot_ready")
        f_outed = sem("f_outed")
        out_ready = sem("out_ready")
        out_stored = sem("out_stored")
        dve_step = sem("dve_step1")
        pool_step = sem("pool_step1")

        rows_of = hidden.rearrange("n p d -> (n p) d").rearrange("(c p b) d -> b p c d", p=P, b=B)
        out_of = out.rearrange("b (c p) d -> b p c d", p=P)
        consts = [(w_qkv, "qkv1"), (gamma, "gamma"), (rope, "rope"), (w_out, "w_out"), (ident, "ident"),
                  (conv_w, "conv_w"), (conv_b, "conv_b"), (f_wqkv, "f_wqkv"), (f_bqk, "f_bqk"), (f_wo, "f_wo"),
                  (parity, "parity")]
        spread = [(f_bv, "f_bv"), (f_bo, "f_bo")]
        LOADS = 16 * (len(consts) + len(spread))
        block = ctx.enter_context(nc.Block())

        def walk(b, attn, ffn, tasks):
            for t in range(UNITS + 4):
                for branch, ends, lag, f in tasks:
                    if not (attn if branch == "a" else ffn):
                        continue
                    u = t - lag
                    if not 0 <= u < UNITS:
                        continue
                    if not ends:
                        f(b if branch == "a" else b - 1, u)
                    elif u % H == H - 1:
                        f(b if branch == "a" else b - 1, u // H)

        def rounds(eng, pre_a, pre_f, tasks, own=None):
            def one(b, attn, ffn):
                if own:
                    own.restart()
                if attn:
                    pre_a(b)
                if ffn:
                    pre_f(b - 1)
                walk(b, attn, ffn, tasks)

            one(0, True, False)
            one(1, True, True)
            with eng.Fori(2, B) as b:
                one(b, True, True)
            one(B, False, True)

        def is_(b, v):
            return isinstance(b, int) and b == v

        @block.sync
        def _(sync):
            for t, name in consts:
                sync.dma_start(t[tuple(slice(None) for _ in t.shape)], d[name]).then_inc(weights_in, 16)
            for t, name in spread:
                sync.dma_start(t[:, :], d[name].partition_broadcast(P)).then_inc(weights_in, 16)

            def load(b):
                if not is_(b, 0):
                    sync.wait_ge(h_taken, b)
                sync.dma_start(h_in[:, :, :], rows_of[b]).then_inc(h_loaded, 16)

            def store(b):
                sync.wait_ge(out_ready, CH * (b + 1))
                sync.dma_start(out_of[b], f_out[:, :, :]).then_inc(out_stored, 16)

            load(0)
            load(1)
            with sync.Fori(2, B) as b:
                load(b)
                store(b - 2)
            store(B - 2)
            store(B - 1)
            sync.wait_ge(out_stored, 16 * B)

        @block.gpsimd
        def _(pool):
            pool.memset(u_t[:, :], 0.0).then_inc(cleared, 1)
            pool.memset(v_f[:, :, :, :], 1.0).then_inc(cleared, 1)

            def pre_a(b):
                wait_apart(pool, (weights_in, LOADS), (h_loaded, 16 * (b + 1)),
                           *(() if is_(b, 0) else ((h1_ready, CH * b),)))
                pool.tensor_copy(h_a[:, :, :], h_in[:, :, :]).then_inc(h_taken, 1)

            def pre_f(b):
                pool.wait_ge(h1_ready, CH * (b + 1))
                if not is_(b, 0):
                    pool.wait_ge(out_ready, CH * b)
                pool.tensor_tensor(h_f[:, :, :], h1[:, :, :], f_bo[:, :].unsqueeze(1).to_broadcast([P, CH, P]), ALU.add
                                   ).then_inc(hf_ready, 1)

            rounds(pool, pre_a, pre_f, [])

        @block.tensor
        def _(pe):
            def pre_a(b):
                pe.wait_ge(u_scaled, b + 1)
                for c in range(CH):
                    m = pe.transpose(A[0][:, c * P:(c + 1) * P], u_a[:, c, :], ident[:, :])
                m.then_inc(xn_turned, 1)
                pe.wait_ge(xn_ready, b + 1)
                if not is_(b, 0):
                    pe.wait_ge(h1_ready, CH * b)
                banks = [A[1], AT, AO, A[0]]
                n = 0
                for j in range(4):
                    for w in range(4):
                        n += 1
                        if n > 4:
                            pe.wait_ge(proj_used, 16 * b + n - 4)
                        pe.matmul(banks[w][:, :], w_qkv[:, w, j * P:(j + 1) * P], xn_t[:, :], start=True, stop=True
                                  ).then_inc(proj, 1)
                for c in range(CH):
                    if c < 4:
                        pe.wait_ge(proj_used, 16 * b + 13 + c)
                    pe.matmul(banks[c][:, :], xn_t[:, c * P:(c + 1) * P], w_qkv[:, 4, :], start=True, stop=True
                              ).then_inc(v_proj, 1)

            def pre_f(b):
                pe.wait_ge(uf_ready, b + 1)
                if not is_(b, 0):
                    pe.wait_ge(out_ready, CH * b)
                for c in range(CH):
                    m = pe.transpose(FT[:, c * P:(c + 1) * P], u_f[:, c, :], ident[:, :])
                m.then_inc(uf_turned, 1)
                pe.wait_ge(xf_ready, b + 1)
                for w in range(2):
                    pe.matmul(F[w][:, :], f_wqkv[:, w, :], x_f[:, :], start=True, stop=True).then_inc(f_proj, 1)
                for c in range(CH):
                    m = pe.matmul(FO[:, c * P:(c + 1) * P], x_f[:, c * P:(c + 1) * P], f_wqkv[:, 2, :],
                                  start=(c == 0), stop=True, skip_group_check=True)
                m.then_inc(f_vproj, 1)

            def a_s(b, u):
                c, h = divmod(u, H)
                rows = slice((h % 2) * DH, (h % 2 + 1) * DH)
                if u == 0:
                    pe.wait_ge(v_ready, CH * (b + 1))
                    pe.wait_ge(rope_ready, b + 1)
                if u >= 2:
                    pe.wait_ge(a_exp, UNITS * b + u - 1)
                pe.matmul(A[u % 2][:, :], q_t[rows, h // 2, c * P:(c + 1) * P], k_t[rows, h // 2, :],
                          start=True, stop=True).then_inc(a_scores, 1)

            def a_v(b, u):
                c, h = divmod(u, H)
                pe.wait_ge(a_t_ready, UNITS * b + u + 1)
                if h == 0 and u:
                    pe.wait_ge(a_norm, CH * b + c)
                for j in range(CH):
                    m = pe.matmul(AO[:, h * DH:(h + 1) * DH], a_pt[:, u % 2, j, :], v_a[:, j, h * DH:(h + 1) * DH],
                                  start=(h == 0 and j == 0), stop=(j == CH - 1), skip_group_check=True)
                m.then_inc(a_pv, 1)

            def a_turn(b, u):
                pe.wait_ge(a_exp, UNITS * b + u + 1)
                if u:
                    pe.wait_ge(a_t_ready, UNITS * b + u)
                    if u % H == 1 and u > H:
                        pe.wait_ge(a_ot_ready, CH * b + u // H)
                    if u % H == 2 and u > H:
                        pe.wait_ge(h1_ready, CH * b + u // H)
                for j in range(CH):
                    m = pe.transpose(AT[:, j * P:(j + 1) * P], a_p[:, u % 2, j * P:(j + 1) * P], ident[:, :])
                m.then_inc(a_turned, 1)

            def a_end1(b, c):
                pe.wait_ge(a_norm, CH * b + c + 1)
                pe.wait_ge(a_t_ready, UNITS * b + min(H * c + 9, UNITS))
                for j in range(4):
                    m = pe.transpose(AT[:, j * P:(j + 1) * P], a_o[:, j * P:(j + 1) * P], ident[:, :])
                m.then_inc(a_o_turned, 1)

            def a_end2(b, c):
                pe.wait_ge(a_ot_ready, CH * b + c + 1)
                pe.wait_ge(a_t_ready, UNITS * b + min(H * c + 10, UNITS))
                for j in range(4):
                    m = pe.matmul(AT[:, 0:P], a_ot[:, j, :], w_out[:, j, :], start=(j == 0), stop=(j == 3))
                m.then_inc(a_outed, 1)

            def f_sc(b, u):
                c, h = divmod(u, H)
                rows = slice((h // 2) * 32, (h // 2 + 1) * 32)
                if u == 0:
                    pe.wait_ge(qf_ready, b + 1)
                    pe.wait_ge(kf_ready, 2 * (b + 1))
                    pe.wait_ge(vf_ready, b + 1)
                if u >= 2:
                    pe.wait_ge(f_exp, UNITS * b + u - 1)
                pe.matmul(F[u % 2][:, :], q_f[rows, c * P:(c + 1) * P], k_f[rows, h % 2, :], start=True, stop=True
                          ).then_inc(f_scores, 1)

            def f_v(b, u):
                c, h = divmod(u, H)
                pe.wait_ge(f_t_ready, UNITS * b + u + 1)
                if h == 0 and u:
                    pe.wait_ge(f_norm, CH * b + c)
                for j in range(CH):
                    m = pe.matmul(FO[:, h * (HD + 1):(h + 1) * (HD + 1)], f_pt[:, u % 2, j, :], v_f[:, j, h, :],
                                  start=(h == 0 and j == 0), stop=(j == CH - 1), skip_group_check=True)
                m.then_inc(f_pv, 1)

            def f_turn(b, u):
                pe.wait_ge(f_probs, UNITS * b + u + 1)
                if u:
                    pe.wait_ge(f_t_ready, UNITS * b + u)
                    if u % H == 1 and u > H:
                        pe.wait_ge(f_ot_ready, CH * b + u // H)
                    if u % H == 2 and u > H:
                        pe.wait_ge(out_ready, CH * b + u // H)
                for j in range(CH):
                    m = pe.transpose(FT[:, j * P:(j + 1) * P], f_p[:, u % 2, j * P:(j + 1) * P], ident[:, :])
                m.then_inc(f_turned, 1)

            def f_end1(b, c):
                pe.wait_ge(f_norm, CH * b + c + 1)
                pe.wait_ge(f_t_ready, UNITS * b + min(H * c + 9, UNITS))
                pe.transpose(FT[:, 0:P], f_o[:, :], ident[:, :]).then_inc(f_o_turned, 1)

            def f_end2(b, c):
                pe.wait_ge(f_ot_ready, CH * b + c + 1)
                pe.wait_ge(f_t_ready, UNITS * b + min(H * c + 10, UNITS))
                pe.matmul(FT[:, 0:P], f_ot[:, :], f_wo[:, :], start=True, stop=True).then_inc(f_outed, 1)

            pe.wait_ge(weights_in, LOADS)
            pe.wait_ge(weights_ready, 1)
            rounds(pe, pre_a, pre_f, [
                ("a", False, 0, a_s), ("f", False, 0, f_sc), ("a", False, 2, a_v), ("f", False, 2, f_v),
                ("a", True, 3, a_end1), ("f", True, 3, f_end1), ("a", True, 4, a_end2), ("f", True, 4, f_end2),
                ("a", False, 1, a_turn), ("f", False, 1, f_turn)])

        @block.scalar
        def _(act):
            def pre_a(b):
                act.wait_ge(squares, 2 * b + 1)
                for c in range(CH):
                    m = nc.scalar.activation(sq[:, :], u_a[:, c, :], ACT.Square, accum_out=ss[:, c:c + 1])
                    m.then_inc(squares_done, 1)
                    act.wait_ge(squares_done, CH * b + c + 1)
                act.wait_ge(xn_turned, b + 1)
                nc.scalar.copy(xn_t[:, :], A[0][:, :]).then_inc(xn_ready, 1)
                banks = [A[1], AT, AO, A[0]]
                for c in range(CH):
                    act.wait_ge(v_proj, CH * b + c + 1)
                    nc.scalar.copy(v_a[:, c, :], banks[c][:, :]).then_inc(v_ready, 1)

            def pre_f(b):
                act.wait_ge(uf_turned, b + 1)
                act.wait_ge(cleared, 2)
                nc.scalar.copy(u_t[:, 1:T + 1], FT[:, :]).then_inc(ut_ready, 1)
                act.wait_ge(f_proj, 2 * b + 1)
                act.wait_ge(weights_ready, 1)
                nc.scalar.activation(q_f[:, :], F[0][:, :], ACT.Identity, bias=f_bqk[:, 0:1], scale=float(D) ** -0.5
                                     ).then_inc(qf_ready, 1)

            def a_e(b, u):
                act.wait_ge(a_max, UNITS * b + u + 1)
                if u >= 2:
                    act.wait_ge(a_turned, UNITS * b + u - 1)
                nc.scalar.activation(a_p[:, u % 2, :], A[u % 2][:, :], ACT.Exp, bias=a_nmax[:, u % 2:u % 2 + 1],
                                     accum_out=a_sum[:, u:u + 1]).then_inc(a_exp, 1)

            def a_ev(b, u):
                act.wait_ge(a_turned, UNITS * b + u + 1)
                if u >= 2:
                    act.wait_ge(a_pv, UNITS * b + u - 1)
                nc.scalar.copy(a_pt[:, u % 2, :, :], AT[:, :].rearrange("p (j n) -> p j n", j=CH)).then_inc(a_t_ready, 1)

            def a_end(b, c):
                act.wait_ge(a_o_turned, CH * b + c + 1)
                nc.scalar.copy(a_ot[:, :, :], AT[:, :].rearrange("p (j n) -> p j n", j=4)).then_inc(a_ot_ready, 1)

            def f_e_(b, u):
                act.wait_ge(f_first, UNITS * b + u + 1)
                if u >= 2:
                    act.wait_ge(f_probs, UNITS * b + u - 1)
                nc.scalar.activation(f_e[:, u % 2, :], F[u % 2][:, :], ACT.Exp, bias=f_nmax[:, u % 2:u % 2 + 1]
                                     ).then_inc(f_exp, 1)

            def f_ev(b, u):
                act.wait_ge(f_turned, UNITS * b + u + 1)
                if u >= 2:
                    act.wait_ge(f_pv, UNITS * b + u - 1)
                nc.scalar.copy(f_pt[:, u % 2, :, :], FT[:, :].rearrange("p (j n) -> p j n", j=CH)).then_inc(f_t_ready, 1)

            def f_end(b, c):
                act.wait_ge(f_o_turned, CH * b + c + 1)
                nc.scalar.copy(f_ot[:, :], FT[:, 0:P]).then_inc(f_ot_ready, 1)

            nc.scalar.preload_act_table_set("exp_and_others")
            rounds(act, pre_a, pre_f, [
                ("a", False, 0, a_e), ("f", False, 0, f_e_), ("a", True, 3, a_end), ("f", True, 3, f_end),
                ("a", False, 1, a_ev), ("f", False, 1, f_ev)])

        @block.vector
        def _(dve):
            own = Steps(dve, dve_step)
            V = nc.vector

            def norm(src, dst):
                for c in range(CH):
                    own.mark(V.bn_stats(stats[:, c, :], src[:, c, :]))
                own.wait()
                for c in range(CH):
                    own.mark(V.bn_aggr(mv[:, c, :], stats[:, c, :]))
                own.wait()
                rsqrt(nc, own, rstd[:, :], mv[:, :, 1], nt, CH, LN_EPS)
                for c in range(CH):
                    m = V.tensor_scalar(dst[:, c, :], src[:, c, :], mv[:, c, 0:1], rstd[:, c:c + 1],
                                        ALU.subtract, ALU.mult)
                    if c < CH - 1:
                        own.mark(m)
                own.wait()
                return m

            def pre_a(b):
                dve.wait_ge(h_taken, b + 1)
                norm(h_a, u_a).then_inc(squares, 1)
                dve.wait_ge(squares, 2 * b + 1)
                dve.wait_ge(squares_done, CH * (b + 1))
                rsqrt(nc, own, rstd[:, :], ss[:, :], nt, CH, 0.0)
                own.then(V.tensor_scalar(rstd[:, :], rstd[:, :], 1e8, None, ALU.min))
                for c in range(CH):
                    m = V.tensor_scalar(u_a[:, c, :], u_a[:, c, :], rstd[:, c:c + 1], None, ALU.mult)
                    if c < CH - 1:
                        own.mark(m)
                m.then_inc(squares, 1)
                dve.wait_ge(squares, 2 * b + 2)
                own.wait()
                dve.sem_inc(u_scaled, 1)
                banks = [A[1], AT, AO, A[0]]
                for j in range(4):
                    for w in range(4):
                        dst = (q_t if w < 2 else k_t)[:, j, :] if w % 2 == 0 else turned[:, w // 2, :]
                        dve.wait_ge(proj, 16 * b + 4 * j + w + 1)
                        V.tensor_tensor(dst, banks[w][:, :], rope[:, w, :], ALU.mult).then_inc(proj_used, 1)
                    dve.wait_ge(proj_used, 16 * b + 4 * j + 4)
                    own.mark(V.tensor_tensor(q_t[:, j, :], q_t[:, j, :], turned[:, 0, :], ALU.add))
                    own.mark(V.tensor_tensor(k_t[:, j, :], k_t[:, j, :], turned[:, 1, :], ALU.add))
                    own.wait()
                dve.sem_inc(rope_ready, 1)

            def pre_f(b):
                dve.wait_ge(h1_ready, CH * (b + 1))
                norm(h1, u_f).then_inc(uf_ready, 1)
                dve.wait_ge(ut_ready, b + 1)
                own.then(V.tensor_scalar(x_c[:, :], u_t[:, 0:T], conv_w[:, 0:1], conv_b[:, 0:1], ALU.mult, ALU.add))
                own.then(V.scalar_tensor_tensor(x_c[:, :], u_t[:, 1:T + 1], conv_w[:, 1:2], x_c[:, :], ALU.mult, ALU.add))
                own.then(V.scalar_tensor_tensor(x_c[:, :], u_t[:, 2:T + 2], conv_w[:, 2:3], x_c[:, :], ALU.mult, ALU.add))
                V.tensor_tensor(x_f[:, :], x_c[:, :], u_t[:, 1:T + 1], ALU.add).then_inc(xf_ready, 1)
                dve.wait_ge(f_proj, 2 * b + 2)
                for e in range(2):
                    V.tensor_scalar(k_f[:, e, :], F[1][:, :], f_bqk[:, 1:2], parity[:, e:e + 1], ALU.add, ALU.mult
                                    ).then_inc(kf_ready, 1)
                dve.wait_ge(f_vproj, b + 1)
                V.tensor_tensor(v_f[:, :, :, 0:HD], FO[:, :].rearrange("p (c h e) -> p c h e", c=CH, h=H),
                                f_bv[:, :].rearrange("p (h e) -> p h e", h=H).unsqueeze(1).to_broadcast([P, CH, H, HD]),
                                ALU.add).then_inc(vf_ready, 1)

            def a_m(b, u):
                dve.wait_ge(a_scores, UNITS * b + u + 1)
                if u >= 2:
                    dve.wait_ge(a_exp, UNITS * b + u - 1)
                V.tensor_reduce(a_nmax[:, u % 2:u % 2 + 1], A[u % 2][:, :], AX, ALU.max, negate=True).then_inc(a_max, 1)

            def f_top(b, u):
                s, pq = F[u % 2][:, :], u % 2
                wait_apart(dve, (weights_in, LOADS), (f_scores, UNITS * b + u + 1))
                own.then(V.max(top_a[:, pq, :], s))
                own.mark(V.match_replace(f_s[:, pq, :], top_a[:, pq, :], s, NEG))
                if u >= 2:
                    dve.wait_ge(f_exp, UNITS * b + u - 1)
                own.mark(V.tensor_scalar(f_nmax[:, pq:pq + 1], top_a[:, pq, 0:1], -1.0, None, ALU.mult))
                own.wait()
                dve.sem_inc(f_first, 1)
                own.then(V.max(top_b[:, pq, :], f_s[:, pq, :]))
                own.then(V.match_replace(f_s[:, pq, :], top_b[:, pq, :], f_s[:, pq, :], NEG))

            def f_mask(b, u):
                pq = u % 2
                dve.wait_ge(f_exp, UNITS * b + u + 1)
                if u >= 2:
                    dve.wait_ge(f_turned, UNITS * b + u - 1)
                V.scalar_tensor_tensor(f_p[:, pq, :], f_s[:, pq, :], 0.1 * NEG, f_e[:, pq, :], ALU.is_le, ALU.mult
                                       ).then_inc(f_probs, 1)

            def a_n(b, c):
                dve.wait_ge(a_pv, UNITS * b + H * (c + 1))
                own.then(V.reciprocal(a_inv[:, :], a_sum[:, c * H:(c + 1) * H]))
                if not is_(c, 0):
                    dve.wait_ge(a_o_turned, CH * b + c)
                V.tensor_tensor(a_o[:, :].rearrange("p (h e) -> p h e", h=H), AO[:, :].rearrange("p (h e) -> p h e", h=H),
                                a_inv[:, :].unsqueeze(2).to_broadcast([P, H, DH]), ALU.mult).then_inc(a_norm, 1)

            def a_h(b, c):
                dve.wait_ge(a_outed, CH * b + c + 1)
                if c == 0 and not is_(b, 0):
                    dve.wait_ge(hf_ready, b)
                V.tensor_tensor(h1[:, c, :], AT[:, 0:P], h_a[:, c, :], ALU.add).then_inc(h1_ready, 1)

            def f_n(b, c):
                dve.wait_ge(f_pv, UNITS * b + H * (c + 1))
                acc = FO[:, 0:H * (HD + 1)].rearrange("p (h e) -> p h e", h=H)
                own.then(V.reciprocal(f_inv[:, :].unsqueeze(2), acc[:, :, HD:HD + 1]))
                V.tensor_tensor(f_o[:, :].rearrange("p (h e) -> p h e", h=H), acc[:, :, 0:HD],
                                f_inv[:, :].unsqueeze(2).to_broadcast([P, H, HD]), ALU.mult).then_inc(f_norm, 1)

            def f_h(b, c):
                dve.wait_ge(f_outed, CH * b + c + 1)
                if c == 0:
                    dve.wait_ge(hf_ready, b + 1)
                    if not is_(b, 0):
                        dve.wait_ge(out_stored, 16 * b)
                V.tensor_tensor(f_out[:, c, :], FT[:, 0:P], h_f[:, c, :], ALU.add).then_inc(out_ready, 1)

            dve.wait_ge(weights_in, LOADS)
            own.mark(V.tensor_scalar(w_qkv[:, :, :], w_qkv[:, :, :], gamma[:, 0:1], float(D) ** 0.5, ALU.mult, ALU.mult))
            own.mark(V.tensor_scalar(f_bqk[:, 0:1], f_bqk[:, 0:1], float(D) ** -0.5, None, ALU.mult))
            own.wait()
            dve.sem_inc(weights_ready, 1)
            dve.wait_ge(cleared, 2)
            rounds(dve, pre_a, pre_f, [
                ("a", False, 0, a_m), ("f", False, 0, f_top), ("a", True, 4, a_h), ("f", True, 4, f_h),
                ("f", False, 0, f_mask), ("a", True, 2, a_n), ("f", True, 2, f_n)], own)


def build(nc, d, out):
    hidden = nc.dram_tensor("hidden", (TILES, P, D), F32, kind="Internal").ap()
    layer0(nc, d, hidden)
    layer1(nc, d, hidden, out)


def kernel(**inputs):
    import numpy as np
    import concourse.bacc as bacc
    from concourse.bass_utils import run_bass_kernel_spmd as run

    nc = bacc.Bacc("TRN2", target_bir_lowering=False, num_devices=1)
    arrays, d = {}, {}

    def give(name, a):
        a = np.ascontiguousarray(a)
        arrays[f"{name}_dram"] = a
        d[name] = nc.dram_tensor(f"{name}_dram", a.shape, mybir.dt.from_np(a.dtype), kind="ExternalInput").ap()

    v = {k: np.asarray(a) for k, a in inputs.items()}
    give("token_ids", v["x"].reshape(B, TILES, STEPS).transpose(2, 0, 1).reshape(P, TILES))
    give("tok_w", v["L0_tok_W"].T)
    give("w_ih", v["L0_attn_gru_wih"].transpose(2, 0, 1).reshape(P, -1))
    give("w_hh", v["L0_attn_gru_whh"].transpose(2, 0, 1).reshape(P, -1))
    give("b_in", v["L0_attn_gru_bih"].reshape(K, GATES, P).transpose(2, 0, 1))
    give("b_hid", v["L0_attn_gru_bhh"].reshape(K, GATES, P).transpose(2, 0, 1))
    for name in ("wq", "wk", "wv"):
        give(f"w_{name[1]}", v[f"L0_attn_{name}"].transpose(2, 0, 1).reshape(P, -1))
    give("w_beat", v["L0_attn_w_beat"].reshape(K, P, 2, P).transpose(3, 0, 2, 1))
    give("w_mix", v["L0_attn_w_mix"].reshape(P, K, P).transpose(2, 1, 0))
    give("norm_g", v["L0_attn_norm_g"].reshape(K, P).T)
    give("norm_b", v["L0_attn_norm_b"].reshape(K, P).T)
    give("bn_g", v["L0_attn_bn_g"])
    give("bn_b", v["L0_attn_bn_b"])
    give("key_wq", v["L0_ffn_Wq"].T)
    give("key_bq", v["L0_ffn_bq"].reshape(H, P).T)
    give("keys", v["L0_ffn_keys"].transpose(1, 3, 0, 2).reshape(P, H, EXPERTS))
    give("experts", np.concatenate([v["L0_ffn_w_down_embed"], v["L0_ffn_w_up_embed"]], axis=1))
    pairs = v["L1_attn_w_qkv"].reshape(D, 3, H * DH // 2, 2)
    plain, swapped = pairs.reshape(D, 3, -1), pairs[..., ::-1].reshape(D, 3, -1)
    give("qkv1", np.stack([plain[:, 0], swapped[:, 0], plain[:, 1], swapped[:, 1], plain[:, 2]], axis=1))
    give("gamma", v["L1_attn_gamma"].reshape(P, 1))
    give("w_out", v["L1_attn_w_out"].reshape(4, P, D).transpose(1, 0, 2))
    give("conv_w", v["L1_ffn_pos_w"].reshape(P, 3))
    give("conv_b", v["L1_ffn_pos_b"].reshape(P, 1))
    give("f_wqkv", v["L1_ffn_qkv_w"].reshape(3, P, D).transpose(2, 0, 1))
    give("f_bqk", v["L1_ffn_qkv_b"][:2 * D].reshape(2, P).T)
    give("f_bv", v["L1_ffn_qkv_b"][2 * D:])
    give("f_wo", v["L1_ffn_wo_w"].T)
    give("f_bo", v["L1_ffn_wo_b"])
    for name, a in shape_constants().items():
        give(name, a)
    out = nc.dram_tensor("out", (B, T, D), F32, kind="ExternalOutput").ap()
    build(nc, d, out)
    r = run(nc, [arrays], core_ids=[0])
    return r.results[0]["out"]


def shape_constants():
    import math

    pos = np.arange(T, dtype=np.float32)[:, None]
    div = np.exp(np.arange(0, D, 2, dtype=np.float32) * (-math.log(10000.0) / D))
    pe = np.zeros((T, D), np.float32)
    pe[:, 0::2] = np.sin(pos * div)
    pe[:, 1::2] = np.cos(pos * div)
    tala = np.zeros((T, D), np.float32)
    slots = D // 4
    half = slots // 2
    harm = np.arange(1, half + 1, dtype=np.float32)
    for n, c in enumerate(CYCLES):
        phase = pos % c / c * 2.0 * math.pi
        tala[:, n * slots:n * slots + half] = np.sin(phase * harm)
        tala[:, n * slots + half:(n + 1) * slots] = np.cos(phase * harm)
    table = (0.5 * pe + 0.5 * tala).astype(np.float32)
    step, seq = np.arange(P) // B, np.arange(P) % B
    mask = np.full((P, K, 2, P), NEG, np.float32)
    for k, c in enumerate(CYCLES):
        for half_ in range(2):
            diff = step[:, None] - (step[None, :] - STEPS * (1 - half_))
            ok = (seq[:, None] == seq[None, :]) & (diff >= 0) & (diff < c)
            mask[:, k, half_, :][ok] = 0.0
    mask = np.concatenate([mask, mask[:, :, :1]], axis=2)
    first = mask.copy()
    first[:, :, 0::2, :] = NEG
    inv_freq = (1.0 / ROPE_THETA ** (np.arange(0, DH, 2, dtype=np.float32) / np.float32(DH))).astype(np.float32)
    angle = np.repeat(np.arange(T, dtype=np.float32)[:, None] * inv_freq[None, :], 2, axis=-1).T
    cos, sin = np.cos(angle), np.sin(angle)
    sin[0::2] *= -1.0
    rope = np.stack([cos * DH ** -0.5, sin * DH ** -0.5, cos, sin], axis=1).astype(np.float32)
    head = np.arange(P) // HD
    return {
        "rope": np.tile(rope, (2, 1, 1)),
        "parity": np.stack([head % 2 == 0, head % 2 == 1], axis=1).astype(np.float32),
        "pe": np.repeat(table.reshape(TILES, STEPS, 1, D), B, axis=2).reshape(TILES, P, D),
        "mask": mask,
        "mask_first": first,
        "ident": np.eye(P, dtype=np.float32),
        "iota8": np.tile(np.arange(TOP, dtype=np.float32), (P, 1)),
    }
```

```python
from contextlib import ExitStack

import numpy as np
import concourse.bass as bass
from concourse import mybir

ALU = mybir.AluOpType
ACT = mybir.ActivationFunctionType
AX = mybir.AxisListType.X
F32 = mybir.dt.float32
I32 = mybir.dt.int32
U32 = mybir.dt.uint32

P = 128
B, T, D = 16, 512, 128
VOCAB = 50257
STEPS = P // B
TILES = T // STEPS
K = 4
CYCLES = (5, 6, 7, 8)
GATES = 3
KB = K * B
NEG = -1e30
LN_EPS = 1e-5
H = 8
TOP = 8
EXPERTS = 128
HALF = 64
SLOTS = H * TOP
GROUPS = 4
GS = SLOTS // GROUPS
UP_GROUPS = 3
GELU_A = 0.7978845608028654
GELU_B = GELU_A * 0.044715
CH = T // P
UNITS = CH * H
DH, HD = 64, 16
F_LAG = 10
ROPE_THETA = 10000.0
RSQRT_SEED = float(0x5F3759DF)


def wait_apart(eng, met, *waits):
    values = [v if isinstance(v, int) else eng.to_reg(v) for _, v in waits]
    eng.wait_ge(*met)
    for (sem, _), value in zip(waits, values):
        eng.wait_ge(sem, value)


class Steps:

    def __init__(self, eng, sem):
        self.eng, self.sem, self.n = eng, sem, 0

    def restart(self):
        self.eng.sem_clear(self.sem)
        self.n = 0

    def then(self, ins):
        ins.then_inc(self.sem, 1)
        self.n += 1
        self.eng.wait_ge(self.sem, self.n)

    def mark(self, ins):
        ins.then_inc(self.sem, 1)
        self.n += 1

    def wait(self):
        self.wait_lag(0)

    def wait_lag(self, lag):
        if self.n > lag:
            self.eng.wait_ge(self.sem, self.n - lag)


def rsqrt_start(nc, own, out, var, tmp, width, eps):
    v, a, _ = (tmp[:, j, 0:width] for j in range(3))
    own.then(nc.vector.tensor_scalar(v, var, eps, None, ALU.add))
    own.then(nc.vector.tensor_scalar(a.bitcast(I32), v.bitcast(I32), 1, None, ALU.logical_shift_right))
    own.then(nc.vector.tensor_scalar(out.bitcast(I32), a.bitcast(I32), -1.0, RSQRT_SEED, ALU.mult, ALU.add))
    if width == 1:
        own.then(nc.vector.tensor_scalar(v, v, -0.5, None, ALU.mult))


def rsqrt_steps(nc, own, out, tmp, width, steps):
    v, a, b = (tmp[:, j, 0:width] for j in range(3))
    for _ in range(steps):
        if width == 1:
            own.then(nc.vector.tensor_scalar(b, out, out, v, ALU.mult, ALU.mult))
            own.then(nc.vector.tensor_scalar(out, b, 1.5, out, ALU.add, ALU.mult))
        else:
            own.then(nc.vector.tensor_tensor(a, out, out, ALU.mult))
            own.then(nc.vector.scalar_tensor_tensor(b, a, -0.5, v, ALU.mult, ALU.mult))
            own.then(nc.vector.scalar_tensor_tensor(out, b, 1.5, out, ALU.add, ALU.mult))


def rsqrt(nc, own, out, var, tmp, width, eps):
    rsqrt_start(nc, own, out, var, tmp, width, eps)
    rsqrt_steps(nc, own, out, tmp, width, 3)


def layer0(nc, d, hidden):
    with ExitStack() as ctx:
        def sb(name, shape, dt=F32):
            return ctx.enter_context(nc.sbuf_tensor(name, shape, dt))

        def pair(name, shape, dt=F32):
            return [sb(f"{name}_of{j}", shape, dt) for j in range(2)]

        def sem(name):
            return ctx.enter_context(nc.semaphore(name))

        w_ih = sb("w_ih", [P, K * GATES * P])
        w_hh = sb("w_hh", [P, K * GATES * P])
        b_in = sb("b_in", [P, K, GATES])
        b_hid = sb("b_hid", [P, K, GATES])
        b_hn = sb("b_hn", [P, K, B])
        w_q = sb("w_q", [P, K * P])
        w_k = sb("w_k", [P, K * P])
        w_v = sb("w_v", [P, K * P])
        w_beat = sb("w_beat", [P, K, 2, P])
        w_mix = sb("w_mix", [P, K, P])
        norm_g = sb("norm_g", [P, K])
        norm_b = sb("norm_b", [P, K])
        bn_g = sb("bn_g", [P, P])
        bn_b = sb("bn_b", [P, P])
        key_wq = sb("key_wq", [P, H * P])
        key_bq = sb("key_bq", [P, H])
        keys = sb("keys", [P, H, 2, EXPERTS])
        ident = sb("ident", [P, P])
        iota8 = sb("iota8", [P, TOP])
        mask = sb("mask", [P, K, 3, P])
        token_ids = sb("token_ids", [P, TILES], I32)
        tile_ids = sb("tile_ids", [P, 1], I32)
        emb = sb("emb", [P, P])
        res = pair("res", [P, P])
        pe_rows = sb("pe_rows", [P, P])
        x_tok = pair("x_tok", [P, P])
        x_t = sb("x_t", [P, P])
        x_gates = pair("x_gates", [P, STEPS, GATES, K, B])
        q_t = sb("q_t", [P, K, P])
        k_t = sb("k_t", [P, K, 2, P])
        v_tok = sb("v_tok", [P, 2, K, P])
        sm = sb("sm", [P, K, 2 * P])
        neg_max = sb("neg_max", [P, K])
        p_sum = sb("p_sum", [P, K])
        p_inv = sb("p_inv", [P, K])
        p_t = sb("p_t", [P, 2, K, P])
        ao_t = sb("ao_t", [P, K, P])
        h_t = pair("h_t", [P, K, STEPS, B])
        r_in = sb("r_in", [P, K, B])
        z_in = sb("z_in", [P, K, B])
        hn_b = sb("hn_b", [P, K, B])
        tr = sb("tr", [P, K, B])
        tz = sb("tz", [P, K, B])
        np1 = sb("np1", [P, K, B])
        np2 = sb("np2", [P, K, B])
        nn = sb("nn", [P, K, B])
        h_n = sb("h_n", [P, K, B])
        zd = sb("zd", [P, K, B])
        thr = sb("thr", [P, K, P])
        thr_t = sb("thr_t", [P, K, P])
        mixed = sb("mixed", [P, P])
        h1 = pair("h1", [P, P])
        stats = sb("stats", [P, K + 1, 6])
        mv = sb("mv", [P, K + 1, 2])
        rstd = sb("rstd", [P, K + 1])
        shift = sb("shift", [P, K])
        nt = sb("nt", [P, 3, K + 1])
        q_tok = pair("q_tok", [P, P])
        qk_t = sb("qk_t", [P, P])
        qh_t = sb("qh_t", [P, H, P])
        top_s = sb("top_s", [P, H, 2, TOP])
        top_i = sb("top_i", [P, H, 2, TOP], U32)
        pairs = sb("pairs", [P, H, TOP * TOP])
        best = sb("best", [P, H, TOP])
        pos = sb("pos", [P, SLOTS], U32)
        pos_hi = sb("pos_hi", [P, SLOTS], U32)
        pos_lo = sb("pos_lo", [P, SLOTS], U32)
        onehot = sb("onehot", [P, SLOTS, TOP])
        onehot2 = sb("onehot2", [P, SLOTS, TOP])
        row_i = sb("row_i", [P, SLOTS])
        row_j = sb("row_j", [P, SLOTS])
        idx = pair("idx", [P, SLOTS], I32)
        best_e = sb("best_e", [P, H, TOP])
        e_sum = sb("e_sum", [P, H])
        e_inv = sb("e_inv", [P, H])
        prob = pair("prob", [P, SLOTS])
        rows = sb("rows", [P, SLOTS, 2 * P])
        h_odd = sb("h_odd", [P, P])
        xd = sb("xd", [P, SLOTS])
        g1 = sb("g1", [P, GS])
        g2 = sb("g2", [P, GS])
        g3 = sb("g3", [P, GS])
        g4 = sb("g4", [P, GS])
        val = sb("val", [P, SLOTS])
        weights_diag = pair("weights_diag", [P, GS, P])

        def bank(name):
            return ctx.enter_context(nc.psum_tensor(name, [P, 512], F32))

        nr_bank, z_bank = bank("nr_bank"), bank("z_bank")
        S = [bank(f"S{i}") for i in range(6)]
        KEY_BANKS = [S[1], S[0], S[4], S[5]]
        GATE_BANKS = [S[1], S[4], S[5]]

        def by_thread(ap):
            return ap.rearrange("p (k c) -> p k c", k=K)

        weights_in = sem("weights_in")
        keys_in = sem("keys_in")
        mask_in = sem("mask_in")
        zeroed = sem("zeroed")
        bias_ready = sem("bias_ready")
        id_copied = sem("id_copied")
        emb_in = sem("emb_in")
        pe_in = sem("pe_in")
        emb_used = sem("emb_used")
        x_scaled = sem("x_scaled")
        x_ready = sem("x_ready")
        x_turned = sem("x_turned")
        x_t_ready = sem("x_t_ready")
        xg_done = sem("xg_done")
        xg_ready = sem("xg_ready")
        qkv_done = sem("qkv_done")
        qkv_ready = sem("qkv_ready")
        win_scores = sem("win_scores")
        win_max = sem("win_max")
        win_exp = sem("win_exp")
        win_inv = sem("win_inv")
        win_probs = sem("win_probs")
        win_turned = sem("win_turned")
        win_t_ready = sem("win_t_ready")
        ao_done = sem("ao_done")
        ao_ready = sem("ao_ready")
        nr_ready = sem("nr_ready")
        z_ready = sem("z_ready")
        r_pre = sem("r_pre")
        n_pre = sem("n_pre")
        z_pre = sem("z_pre")
        r_tanh = sem("r_tanh")
        n_tanh = sem("n_tanh")
        z_tanh = sem("z_tanh")
        h_ready = sem("h_ready")
        beat_done = sem("beat_done")
        thr_stats = sem("thr_stats")
        thr_ready = sem("thr_ready")
        thr_turned = sem("thr_turned")
        thr_t_ready = sem("thr_t_ready")
        mix_done = sem("mix_done")
        q_ready = sem("q_ready")
        q_turned = sem("q_turned")
        qk_ready = sem("qk_ready")
        qh_done = sem("qh_done")
        qh_ready = sem("qh_ready")
        key_scores = sem("key_scores")
        key_top = sem("key_top")
        best_ready = sem("best_ready")
        best_exp = sem("best_exp")
        idx_ready = sem("idx_ready")
        rows_in = [sem(f"rows_in{g}") for g in range(GROUPS)]
        gelu_in = sem("gelu_in")
        gelu_tanh = sem("gelu_tanh")
        val_ready = sem("val_ready")
        diag_ready = sem("diag_ready")
        group_added = sem("group_added")
        tile_added = sem("tile_added")
        stored = sem("stored")
        dve_step = sem("dve_step")
        act_step = sem("act_step")

        consts = [(w_ih, "w_ih"), (w_hh, "w_hh"), (b_in, "b_in"), (b_hid, "b_hid"),
                  (w_q, "w_q"), (w_k, "w_k"), (w_v, "w_v"), (w_beat, "w_beat"), (w_mix, "w_mix"),
                  (norm_g, "norm_g"), (norm_b, "norm_b"),
                  (key_wq, "key_wq"), (key_bq, "key_bq"), (ident, "ident"),
                  (iota8, "iota8"), (token_ids, "token_ids")]
        spread = [(bn_g, "bn_g"), (bn_b, "bn_b")]
        LOADS = 16 * (len(consts) + len(spread))
        XG = GATES * K

        block = ctx.enter_context(nc.Block())

        def rounds(eng, round_):
            round_(0, 0, mixing=False, experts=False)
            round_(1, 1, experts=False)
            with eng.Fori(1, TILES // 2 - 1) as i:
                round_(2 * i, 0)
                round_(2 * i + 1, 1)
            round_(TILES - 2, 0)
            round_(TILES - 1, 1, inputs=False)
            round_(TILES, 0, gru=False, inputs=False)
            round_(TILES + 1, 1, gru=False, inputs=False, mixing=False)

        def at_least(n, v):
            return not isinstance(n, int) or n >= v

        @block.sync
        def _(sync):
            sync.dma_start(mask[:, :, :, :], d["mask_first"]).then_inc(mask_in, 16)
            for t, name in consts:
                sync.dma_start(t[tuple(slice(None) for _ in t.shape)], d[name]).then_inc(weights_in, 16)
            for t, name in spread:
                sync.dma_start(t[:, :], d[name].partition_broadcast(P)).then_inc(weights_in, 16)
            sync.wait_ge(zeroed, 4)
            for c in range(2):
                sync.dma_start(keys[c * HALF:(c + 1) * HALF, :, c, :], d["keys"][c * HALF:(c + 1) * HALF]
                               ).then_inc(keys_in, 16)

            def load_pe(t):
                if at_least(t, 1):
                    sync.wait_ge(x_ready, t)
                sync.dma_start(pe_rows[:, :], d["pe"][t]).then_inc(pe_in, 16)

            load_pe(0)
            load_pe(1)
            sync.wait_ge(win_max, 1)
            sync.dma_start(mask[:, :, :, :], d["mask"]).then_inc(mask_in, 16)

            def round_(n, par, gru=True, inputs=True, mixing=True, experts=True):
                if inputs and not (isinstance(n, int) and n == TILES - 2):
                    load_pe(n + 2)
                if experts:
                    sync.wait_ge(tile_added, n - 1)
                    sync.dma_start(hidden[n - 2], h1[par][:, :]).then_inc(stored, 16)

            rounds(sync, round_)
            sync.wait_ge(stored, 16 * TILES)

        @block.gpsimd
        def _(pool):
            pool.memset(h_t[1][:, :, :, :], 0.0).then_inc(zeroed, 1)
            pool.memset(k_t[:, :, :, :], 0.0).then_inc(zeroed, 1)
            pool.memset(v_tok[:, :, :, :], 0.0).then_inc(zeroed, 1)
            pool.memset(keys[:, :, :, :], 0.0).then_inc(zeroed, 1)
            pool.wait_ge(weights_in, LOADS)

            def embed(t):
                if at_least(t, 1):
                    pool.wait_ge(emb_used, 2 * t)
                    pool.wait_ge(emb_in, 16 * t)
                pool.tensor_copy(tile_ids[:, :], token_ids[:, bass.ds(t, 1)]).then_inc(id_copied, 1)
                wait_apart(pool, (weights_in, LOADS), (id_copied, t + 1))
                pool.indirect_dma_start(out=emb[:, :], out_offset=None, in_=d["tok_w"],
                                        in_offset=bass.IndirectOffsetOnAxis(ap=tile_ids[:, :].bitcast(U32), axis=0)
                                        ).then_inc(emb_in, 16)

            def gather(t, par):
                wait_apart(pool, (weights_in, LOADS), (idx_ready, t + 1))
                for g in range(GROUPS):
                    if at_least(t, 1):
                        wait_apart(pool, (weights_in, LOADS), (group_added, UP_GROUPS * (t - 1) + g + 1)
                                   if g < UP_GROUPS else (tile_added, t))
                    for j in range(g * GS, (g + 1) * GS):
                        pool.indirect_dma_start(out=rows[:, j, :], out_offset=None, in_=d["experts"],
                                                in_offset=bass.IndirectOffsetOnAxis(ap=idx[par][:, j:j + 1].bitcast(U32), axis=0)
                                                ).then_inc(rows_in[g], 16)

            for t in range(3):
                embed(t)
            for t in range(2):
                embed(t + 3)
                gather(t, t % 2)
            with pool.Fori(1, TILES // 2 - 2) as i:
                embed(2 * i + 3)
                gather(2 * i, 0)
                embed(2 * i + 4)
                gather(2 * i + 1, 1)
            embed(TILES - 1)
            for t in range(TILES - 4, TILES):
                gather(t, t % 2)

        @block.tensor
        def _(pe):
            def turn_x(t, par):
                pe.wait_ge(x_ready, t + 1)
                if at_least(t, 1):
                    pe.wait_ge(win_t_ready, 2 * t)
                pe.transpose(S[3][:, 0:P], x_tok[par][:, :], ident[:, :]).then_inc(x_turned, 1)

            def input_gates(t):
                pe.wait_ge(x_t_ready, t + 1)
                if at_least(t, 1):
                    pe.wait_ge(qkv_ready, 3 * t)
                if at_least(t, 2):
                    pe.wait_ge(key_top, 4 * (t - 1))
                for g in range(GATES):
                    for k in range(K):
                        c = (k * GATES + g) * P
                        m = pe.matmul(GATE_BANKS[g][:, k * P:(k + 1) * P], w_ih[:, c:c + P], x_t[:, :],
                                      start=(k == 0), stop=True, skip_group_check=True)
                    m.then_inc(xg_done, 1)

            def gru_step(n, s, par):
                if at_least(n, 1) or s:
                    pe.wait_ge(h_ready, STEPS * n + s)
                prev = h_t[par][:, :, s - 1, :] if s else h_t[1 - par][:, :, STEPS - 1, :]
                for out, g in ((nr_bank[:, 0:KB], 2), (nr_bank[:, KB:2 * KB], 0), (z_bank[:, 0:KB], 1)):
                    for k in range(K):
                        c = (k * GATES + g) * P
                        m = pe.matmul(out[:, k * B:(k + 1) * B], w_hh[:, c:c + P], prev[:, k, :],
                                      start=(k == 0 and g != 0), stop=True, skip_group_check=True)
                    if g == 0:
                        m.then_inc(nr_ready, 1)
                m.then_inc(z_ready, 1)

            def beat(n, par):
                pe.wait_ge(h_ready, STEPS * (n + 1))
                pe.wait_ge(ao_ready, n + 1)
                if at_least(n, 1):
                    pe.wait_ge(key_top, 4 * n)
                if at_least(n, 2):
                    pe.wait_ge(tile_added, n - 1)
                for k in range(K):
                    pe.matmul(S[0][:, k * P:(k + 1) * P], h_t[par][:, k, :, :], w_beat[:, k, 0, :],
                              start=(k == 0), stop=False, skip_group_check=True)
                    m = pe.matmul(S[0][:, k * P:(k + 1) * P], ao_t[:, k, :], w_beat[:, k, 1, :],
                                  start=False, stop=True, skip_group_check=True)
                m.then_inc(beat_done, 1)

            def turn_thr(n):
                pe.wait_ge(thr_ready, 4 * (n + 1))
                last = min(n + 1, TILES - 1) if isinstance(n, int) else n + 1
                pe.wait_ge(xg_ready, XG * (last + 1))
                for k in range(K):
                    m = pe.transpose(S[1][:, k * P:(k + 1) * P], thr[:, k, :], ident[:, :])
                m.then_inc(thr_turned, 1)

            def mix(n):
                pe.wait_ge(thr_t_ready, 4 * (n + 1))
                for k in range(K):
                    m = pe.matmul(S[0][:, 0:P], thr_t[:, k, :], w_mix[:, k, :], start=(k == 0), stop=(k == K - 1))
                m.then_inc(mix_done, 1)

            def window_qkv(n, par, mixing):
                pe.wait_ge(x_t_ready, n + 1)
                pe.wait_ge(xg_ready, XG * (n + 1))
                if at_least(n, 1):
                    pe.wait_ge(ao_ready, n)
                for b, w in ((2, w_q), (3, w_k)):
                    for k in range(K):
                        m = pe.matmul(S[b][:, k * P:(k + 1) * P], w[:, k * P:(k + 1) * P], x_t[:, :],
                                      start=(k == 0), stop=True, skip_group_check=True)
                    m.then_inc(qkv_done, 1)
                    if b == 2 and mixing:
                        mix(n - 1)
                pe.matmul(S[4][:, :], x_t[:, :], w_v[:, :], start=True, stop=True).then_inc(qkv_done, 1)

            def window_scores(n):
                pe.wait_ge(qkv_ready, 3 * n + 2)
                for k in range(K):
                    m = pe.matmul(S[2 + k // 2][:, (k % 2) * 256:(k % 2 + 1) * 256], q_t[:, k, :], k_t[:, k, :, :],
                                  start=(k % 2 == 0), stop=True, skip_group_check=True)
                m.then_inc(win_scores, 1)

            def window_turn(n):
                pe.wait_ge(win_probs, 4 * (n + 1))
                for slot in range(2):
                    for k in range(K):
                        m = pe.transpose(S[2 + slot][:, k * P:(k + 1) * P], sm[:, k, slot * P:(slot + 1) * P], ident[:, :])
                    m.then_inc(win_turned, 1)

            def window_rows(n):
                pe.wait_ge(win_t_ready, 2 * (n + 1))
                pe.wait_ge(qkv_ready, 3 * (n + 1))
                for k in range(K):
                    for slot in range(2):
                        m = pe.matmul(S[2][:, k * P:(k + 1) * P], v_tok[:, slot, k, :], p_t[:, slot, k, :],
                                      start=(k == 0 and slot == 0), stop=(slot == 1), skip_group_check=True)
                m.then_inc(ao_done, 1)

            def turn_q(n, par):
                pe.wait_ge(q_ready, n + 1)
                pe.transpose(S[1][:, 0:P], q_tok[par][:, :], ident[:, :]).then_inc(q_turned, 1)

            def key_queries(n):
                pe.wait_ge(qk_ready, n + 1)
                for h in range(H):
                    m = pe.matmul(S[0 if h < 4 else 5][:, (h % 4) * P:(h % 4 + 1) * P], key_wq[:, h * P:(h + 1) * P],
                                  qk_t[:, :], start=(h % 4 == 0), stop=True, skip_group_check=True)
                    if h % 4 == 3:
                        m.then_inc(qh_done, 1)

            def key_products(n, window):
                if window:
                    pe.wait_ge(qkv_ready, 3 * (n + 2))
                for g in range(4):
                    pe.wait_ge(qh_ready, H * n + 2 * g + 2)
                    for j in range(2):
                        m = pe.matmul(KEY_BANKS[g][:, j * 256:(j + 1) * 256], qh_t[:, 2 * g + j, :],
                                      keys[:, 2 * g + j, :, :], start=(j == 0), stop=True, skip_group_check=True)
                    m.then_inc(key_scores, 1)

            def add_up(n, g, mixing):
                if mixing:
                    pe.wait_ge(key_top, 4 * (n + 1) + 2)
                pe.wait_ge(diag_ready, GS * (UP_GROUPS * n + g + 1))
                for j in range(GS):
                    m = pe.matmul(S[0][:, 0:P], weights_diag[g % 2][:, j, :], rows[:, g * GS + j, P:2 * P],
                                  start=(g == 0 and j == 0), stop=(g == UP_GROUPS - 1 and j == GS - 1))
                m.then_inc(group_added, 1)

            def round_(n, par, gru=True, inputs=True, mixing=True, experts=True):
                odd = 1 - par
                if gru:
                    gru_step(n, 0, par)
                if mixing:
                    beat(n - 1, odd)
                if gru:
                    gru_step(n, 1, par)
                if mixing:
                    turn_thr(n - 1)
                if gru:
                    window_qkv(n, par, mixing)
                elif mixing:
                    mix(n - 1)
                if gru:
                    gru_step(n, 2, par)
                if mixing:
                    turn_q(n - 1, odd)
                if gru:
                    window_scores(n)
                if mixing:
                    key_queries(n - 1)
                if gru:
                    gru_step(n, 3, par)
                if mixing:
                    key_products(n - 1, gru)
                if gru:
                    gru_step(n, 4, par)
                    window_turn(n)
                if experts:
                    add_up(n - 2, 0, mixing)
                if gru:
                    gru_step(n, 5, par)
                if inputs:
                    turn_x(n + 1, odd)
                if gru:
                    window_rows(n)
                if experts:
                    add_up(n - 2, 1, mixing)
                if gru:
                    gru_step(n, 6, par)
                if inputs:
                    input_gates(n + 1)
                if gru:
                    gru_step(n, 7, par)
                if experts:
                    add_up(n - 2, 2, mixing)

            pe.wait_ge(weights_in, LOADS)
            pe.wait_ge(keys_in, 32)
            pe.wait_ge(zeroed, 4)
            turn_x(0, 0)
            input_gates(0)
            rounds(pe, round_)

        @block.scalar
        def _(act):
            own = Steps(act, act_step)

            def keep_rows(t, par):
                act.wait_ge(emb_in, 16 * (t + 1))
                if at_least(t, 2):
                    act.wait_ge(q_ready, t - 1)
                nc.scalar.copy(res[par][:, :], emb[:, :]).then_inc(emb_used, 1)

            def turn_x(t):
                act.wait_ge(x_turned, t + 1)
                if at_least(t, 1):
                    act.wait_ge(qkv_done, 3 * t)
                nc.scalar.copy(x_t[:, :], S[3][:, 0:P]).then_inc(x_t_ready, 1)

            def input_gates(t, par):
                for g in range(GATES):
                    act.wait_ge(xg_done, GATES * t + g + 1)
                    for k in range(K):
                        nc.scalar.activation(x_gates[par][:, :, g, k, :],
                                             GATE_BANKS[g][:, k * P:(k + 1) * P].rearrange("p (s b) -> p s b", s=STEPS),
                                             ACT.Identity, bias=b_in[:, k, g:g + 1]).then_inc(xg_ready, 1)

            def gru_step(n, s):
                t = STEPS * n + s + 1
                act.wait_ge(r_pre, t)
                nc.scalar.activation(tr[:, :, :], r_in[:, :, :], ACT.Tanh, scale=0.5).then_inc(r_tanh, 1)
                act.wait_ge(n_pre, t)
                nc.scalar.activation(nn[:, :, :], np2[:, :, :], ACT.Tanh).then_inc(n_tanh, 1)
                act.wait_ge(z_pre, t)
                nc.scalar.activation(tz[:, :, :], z_in[:, :, :], ACT.Tanh, scale=0.5).then_inc(z_tanh, 1)

            def scale_thr(n):
                act.wait_ge(thr_stats, n + 1)
                for k in range(K):
                    nc.scalar.activation(thr[:, k, :], thr[:, k, :], ACT.Identity, scale=rstd[:, k:k + 1],
                                         bias=shift[:, k:k + 1]).then_inc(thr_ready, 1)

            def turn_thr(n):
                act.wait_ge(thr_turned, n + 1)
                for k in range(K):
                    nc.scalar.activation(thr_t[:, k, :], S[1][:, k * P:(k + 1) * P], ACT.Identity,
                                         scale=norm_g[:, k:k + 1], bias=norm_b[:, k:k + 1]).then_inc(thr_t_ready, 1)

            def window_qkv(n, par):
                for w, (dst, b) in enumerate(((q_t[:, :, :], 2), (k_t[:, :, par, :], 3), (v_tok[:, par, :, :], 4))):
                    act.wait_ge(qkv_done, 3 * n + w + 1)
                    nc.scalar.copy(dst, by_thread(S[b][:, :])).then_inc(qkv_ready, 1)

            def window_exp(n):
                act.wait_ge(win_max, n + 1)
                for k in range(K):
                    nc.scalar.activation(sm[:, k, :], sm[:, k, :], ACT.Exp, bias=neg_max[:, k:k + 1],
                                         accum_out=p_sum[:, k:k + 1]).then_inc(win_exp, 1)

            def window_probs(n):
                act.wait_ge(win_inv, n + 1)
                for k in range(K):
                    nc.scalar.activation(sm[:, k, :], sm[:, k, :], ACT.Copy, scale=p_inv[:, k:k + 1]).then_inc(win_probs, 1)

            def window_turn(n):
                for slot in range(2):
                    act.wait_ge(win_turned, 2 * n + slot + 1)
                    nc.scalar.copy(p_t[:, slot, :, :], by_thread(S[2 + slot][:, :])).then_inc(win_t_ready, 1)

            def window_rows(n):
                act.wait_ge(ao_done, n + 1)
                nc.scalar.copy(ao_t[:, :, :], by_thread(S[2][:, :])).then_inc(ao_ready, 1)

            def turn_q(n):
                act.wait_ge(q_turned, n + 1)
                nc.scalar.copy(qk_t[:, :], S[1][:, 0:P]).then_inc(qk_ready, 1)

            def key_queries(n):
                for h in range(H):
                    if h % 4 == 0:
                        act.wait_ge(qh_done, 2 * n + h // 4 + 1)
                    nc.scalar.activation(qh_t[:, h, :], S[0 if h < 4 else 5][:, (h % 4) * P:(h % 4 + 1) * P],
                                         ACT.Identity, bias=key_bq[:, h:h + 1]).then_inc(qh_ready, 1)

            def best_weights(n):
                act.wait_ge(best_ready, n + 1)
                nc.scalar.activation(best_e[:, :, :], best_e[:, :, :], ACT.Exp).then_inc(best_exp, 1)

            def gelu(n, g):
                act.wait_ge(gelu_in, GROUPS * n + g + 1)
                nc.scalar.activation(g3[:, :], g2[:, :], ACT.Tanh).then_inc(gelu_tanh, 1)

            def spread_weights(n, g):
                act.wait_ge(val_ready, UP_GROUPS * n + g + 1)
                if g > 1 or at_least(n, 1):
                    act.wait_ge(group_added, UP_GROUPS * n + max(g - 1, 0))
                for j in range(g * GS, (g + 1) * GS):
                    nc.scalar.activation(weights_diag[g % 2][:, j % GS, :], ident[:, :], ACT.Copy, scale=val[:, j:j + 1]
                                         ).then_inc(diag_ready, 1)

            def round_(n, par, gru=True, inputs=True, mixing=True, experts=True):
                odd = 1 - par
                if gru:
                    gru_step(n, 0)
                if mixing:
                    scale_thr(n - 1)
                if gru:
                    gru_step(n, 1)
                if mixing:
                    turn_thr(n - 1)
                if gru:
                    window_qkv(n, par)
                    gru_step(n, 2)
                if mixing:
                    turn_q(n - 1)
                if experts:
                    gelu(n - 2, 0)
                if mixing:
                    key_queries(n - 1)
                if gru:
                    window_exp(n)
                    gru_step(n, 3)
                    window_probs(n)
                if inputs:
                    keep_rows(n + 1, odd)
                if experts:
                    spread_weights(n - 2, 0)
                if gru:
                    gru_step(n, 4)
                if experts:
                    gelu(n - 2, 1)
                if gru:
                    window_turn(n)
                if experts:
                    spread_weights(n - 2, 1)
                if gru:
                    gru_step(n, 5)
                if inputs:
                    turn_x(n + 1)
                if gru:
                    window_rows(n)
                if mixing:
                    best_weights(n - 1)
                if gru:
                    gru_step(n, 6)
                if experts:
                    gelu(n - 2, 2)
                    spread_weights(n - 2, 2)
                if inputs:
                    input_gates(n + 1, odd)
                if gru:
                    gru_step(n, 7)
                if experts:
                    gelu(n - 2, 3)

            nc.scalar.preload_act_table_set("exp_and_others")
            act.wait_ge(zeroed, 4)
            act.wait_ge(bias_ready, 1)
            keep_rows(0, 0)
            turn_x(0)
            input_gates(0, 0)
            rounds(act, round_)

        @block.vector
        def _(dve):
            own = Steps(dve, dve_step)
            V = nc.vector

            def norm_stats(x, k):
                own.then(V.bn_stats(stats[:, k, :], x))
                own.then(V.bn_aggr(mv[:, k, :], stats[:, k, :]))

            def moments_of_emb(t):
                dve.wait_ge(emb_in, 16 * (t + 1))
                norm_stats(emb[:, :], K)
                rsqrt(nc, own, rstd[:, K:K + 1], mv[:, K, 1:2], nt, 1, LN_EPS)

            def make_x(t, par):
                V.tensor_scalar(x_tok[par][:, :], emb[:, :], mv[:, K, 0:1], rstd[:, K:K + 1], ALU.subtract, ALU.mult
                                ).then_inc(emb_used, 1)
                dve.wait_ge(emb_used, 2 * (t + 1))
                dve.wait_ge(pe_in, 16 * (t + 1))
                V.tensor_tensor(x_tok[par][:, :], x_tok[par][:, :], pe_rows[:, :], ALU.add).then_inc(x_ready, 1)

            def window_mask(n, par):
                dve.wait_ge(win_scores, n + 1)
                own.wait()
                for j in range(2):
                    own.mark(V.scalar_tensor_tensor(
                        sm[:, 2 * j:2 * j + 2, :].rearrange("p k (s t) -> p k s t", s=2),
                        S[2 + j][:, :].rearrange("p (k s t) -> p k s t", k=2, s=2), float(D) ** -0.5,
                        mask[:, 2 * j:2 * j + 2, 1 - par:3 - par, :], ALU.mult, ALU.add))
                own.wait()
                V.tensor_reduce(neg_max[:, :], sm[:, :, :], AX, ALU.max, negate=True).then_inc(win_max, 1)

            def window_inv(n):
                dve.wait_ge(win_exp, 4 * (n + 1))
                V.reciprocal(p_inv[:, :], p_sum[:, :]).then_inc(win_inv, 1)

            def gru_step(n, s, par, dots=None):
                t = STEPS * n + s + 1
                x_of = x_gates[par][:, s, :, :, :]
                prev = h_t[par][:, :, s - 1, :] if s else h_t[1 - par][:, :, STEPS - 1, :]
                if s == 0:
                    dve.wait_ge(xg_ready, XG * (n + 1))
                dve.wait_ge(nr_ready, t)
                V.tensor_tensor(r_in[:, :, :], by_thread(nr_bank[:, KB:2 * KB]), x_of[:, 0, :, :], ALU.add).then_inc(r_pre, 1)
                own.mark(V.tensor_tensor(hn_b[:, :, :], by_thread(nr_bank[:, 0:KB]), b_hn[:, :, :], ALU.add))
                if dots:
                    dots(0)
                own.wait()
                dve.wait_ge(r_tanh, t)
                own.then(V.scalar_tensor_tensor(np1[:, :, :], tr[:, :, :], 1.0, hn_b[:, :, :], ALU.add, ALU.mult))
                V.scalar_tensor_tensor(np2[:, :, :], np1[:, :, :], 0.5, x_of[:, 2, :, :], ALU.mult, ALU.add).then_inc(n_pre, 1)
                if dots:
                    dots(1)
                dve.wait_ge(z_ready, t)
                V.tensor_tensor(z_in[:, :, :], by_thread(z_bank[:, 0:KB]), x_of[:, 1, :, :], ALU.add).then_inc(z_pre, 1)
                dve.wait_ge(n_tanh, t)
                own.mark(V.tensor_tensor(h_n[:, :, :], prev, nn[:, :, :], ALU.subtract))
                if dots:
                    dots(2)
                own.wait()
                dve.wait_ge(z_tanh, t)
                own.then(V.scalar_tensor_tensor(zd[:, :, :], tz[:, :, :], 1.0, h_n[:, :, :], ALU.add, ALU.mult))
                V.scalar_tensor_tensor(h_t[par][:, :, s, :], zd[:, :, :], 0.5, nn[:, :, :], ALU.mult, ALU.add
                                       ).then_inc(h_ready, 1)

            def norm_threads(n, par, inputs):
                if inputs:
                    dve.wait_ge(emb_in, 16 * (n + 3))
                    own.mark(V.bn_stats(stats[:, K, :], emb[:, :]))
                dve.wait_ge(beat_done, n + 1)
                own.then(V.tensor_tensor(thr[:, :, :], by_thread(S[0][:, :]),
                                         x_tok[par][:, :].unsqueeze(1).to_broadcast([P, K, P]), ALU.add))
                for k in range(K):
                    own.mark(V.bn_stats(stats[:, k, :], thr[:, k, :]))
                own.wait()
                w = K + 1 if inputs else K
                for k in range(w):
                    own.mark(V.bn_aggr(mv[:, k, :], stats[:, k, :]))
                own.wait()
                rsqrt(nc, own, rstd[:, 0:w], mv[:, 0:w, 1], nt, w, LN_EPS)
                V.scalar_tensor_tensor(shift[:, :], mv[:, 0:K, 0], -1.0, rstd[:, 0:K], ALU.mult, ALU.mult).then_inc(thr_stats, 1)

            def norm_mixture(n, par):
                dve.wait_ge(mix_done, n + 1)
                own.then(V.tensor_tensor(mixed[:, :], S[0][:, 0:P], x_tok[par][:, :], ALU.add))
                norm_stats(mixed[:, :], 0)
                rsqrt(nc, own, rstd[:, 0:1], mv[:, 0, 1:2], nt, 1, LN_EPS)
                own.then(V.scalar_tensor_tensor(mixed[:, :], mixed[:, :], mv[:, 0, 0:1], bn_g[:, :], ALU.subtract, ALU.mult))
                own.then(V.scalar_tensor_tensor(mixed[:, :], mixed[:, :], rstd[:, 0:1], bn_b[:, :], ALU.mult, ALU.add))
                if at_least(n, 2):
                    dve.wait_ge(stored, 16 * (n - 1))
                own.then(V.tensor_tensor(h1[par][:, :], mixed[:, :], res[par][:, :], ALU.add))
                norm_stats(h1[par][:, :], 0)
                rsqrt(nc, own, rstd[:, 0:1], mv[:, 0, 1:2], nt, 1, LN_EPS)
                V.tensor_scalar(q_tok[par][:, :], h1[par][:, :], mv[:, 0, 0:1], rstd[:, 0:1], ALU.subtract, ALU.mult
                                ).then_inc(q_ready, 1)
                dve.wait_ge(q_ready, n + 1)

            def key_tops(n, g):
                wait_apart(dve, (zeroed, 4), (key_scores, 4 * n + g + 1))
                cuts = [(2 * g + j, c, KEY_BANKS[g][:, (2 * j + c) * P:(2 * j + c + 1) * P])
                        for j in range(2) for c in range(2)]
                for h, c, src in cuts:
                    own.mark(V.max(top_s[:, h, c, :], src))
                own.wait()
                for h, c, src in cuts[:-1]:
                    own.mark(V.max_index(top_i[:, h, c, :], top_s[:, h, c, :], src))
                h, c, src = cuts[-1]
                V.max_index(top_i[:, h, c, :], top_s[:, h, c, :], src).then_inc(key_top, 1)

            def best_pairs(n):
                own.then(V.tensor_tensor(pairs[:, :, :].rearrange("p h (i j) -> p h i j", i=TOP),
                                         top_s[:, :, 0, :].unsqueeze(3).to_broadcast([P, H, TOP, TOP]),
                                         top_s[:, :, 1, :].unsqueeze(2).to_broadcast([P, H, TOP, TOP]), ALU.add))
                for h in range(H):
                    own.mark(V.max(best[:, h, :], pairs[:, h, :]))
                own.wait()
                V.tensor_tensor(best_e[:, :, :], best[:, :, :], best[:, :, 0:1].to_broadcast([P, H, TOP]), ALU.subtract
                                ).then_inc(best_ready, 1)
                for h in range(H):
                    own.mark(V.max_index(pos[:, h * TOP:(h + 1) * TOP], best[:, h, :], pairs[:, h, :]))
                own.wait()

            def expert_rows(n, par):
                own.mark(V.tensor_scalar(pos_hi[:, :], pos[:, :], 3, None, ALU.logical_shift_right))
                own.mark(V.tensor_scalar(pos_lo[:, :], pos[:, :], 7, None, ALU.bitwise_and))
                own.wait()
                dve.wait_ge(key_top, 4 * (n + 1))
                sides = ((pos_hi, onehot, row_i, 0), (pos_lo, onehot2, row_j, 1))
                for p_, oh, r, c in sides:
                    own.mark(V.tensor_tensor(oh[:, :, :], p_[:, :].unsqueeze(2).to_broadcast([P, SLOTS, TOP]),
                                             iota8[:, :].unsqueeze(1).to_broadcast([P, SLOTS, TOP]), ALU.is_equal))
                for p_, oh, r, c in sides:
                    own.wait_lag(1)
                    own.mark(V.tensor_tensor(oh[:, :, :].rearrange("p (h k) e -> p h k e", h=H),
                                             oh[:, :, :].rearrange("p (h k) e -> p h k e", h=H),
                                             top_i[:, :, c, :].unsqueeze(2).to_broadcast([P, H, TOP, TOP]), ALU.mult))
                for p_, oh, r, c in sides:
                    own.wait_lag(1)
                    own.mark(V.tensor_reduce(r[:, :], oh[:, :, :], AX, ALU.add))
                own.wait()
                V.scalar_tensor_tensor(idx[par][:, :], row_i[:, :], float(EXPERTS), row_j[:, :], ALU.mult, ALU.add
                                       ).then_inc(idx_ready, 1)

            def expert_probs(n, par):
                dve.wait_ge(best_exp, n + 1)
                own.then(V.tensor_reduce(e_sum[:, :], best_e[:, :, :], AX, ALU.add))
                own.then(V.reciprocal(e_inv[:, :], e_sum[:, :]))
                own.then(V.tensor_tensor(prob[par][:, :].rearrange("p (h k) -> p h k", h=H), best_e[:, :, :],
                                         e_inv[:, :].unsqueeze(2).to_broadcast([P, H, TOP]), ALU.mult))

            def down(n, g, par, js):
                if js[0] == 0:
                    dve.wait_ge(rows_in[g], 16 * GS * (n + 1))
                for j in js:
                    row = rows[:, g * GS + j, 0:P]
                    own.mark(V.tensor_tensor_reduce(row, row, q_tok[par][:, :], 1.0, 0.0, ALU.mult, ALU.add,
                                                    xd[:, g * GS + j:g * GS + j + 1]))

            def gelu_in_(n, g):
                x = xd[:, g * GS:(g + 1) * GS]
                own.wait()
                own.then(V.tensor_tensor(g1[:, :], x, x, ALU.mult))
                own.then(V.tensor_scalar(g1[:, :], g1[:, :], GELU_B, GELU_A, ALU.mult, ALU.add))
                V.tensor_tensor(g2[:, :], g1[:, :], x, ALU.mult).then_inc(gelu_in, 1)

            def weigh(n, g, par):
                cut = slice(g * GS, (g + 1) * GS)
                dve.wait_ge(gelu_tanh, GROUPS * n + g + 1)
                own.then(V.scalar_tensor_tensor(g4[:, :], g3[:, :], 1.0, xd[:, cut], ALU.add, ALU.mult))
                m = V.scalar_tensor_tensor(val[:, cut], g4[:, :], 0.5, prob[par][:, cut], ALU.mult, ALU.mult)
                if g < UP_GROUPS:
                    m.then_inc(val_ready, 1)
                else:
                    own.then(m)

            def add_last_up(n, par):
                for j in range(UP_GROUPS * GS, SLOTS):
                    row, w = rows[:, j, P:2 * P], val[:, j:j + 1]
                    if j > UP_GROUPS * GS + 1:
                        own.wait_lag(1)
                    acc = h_odd if j % 2 else h1[par]
                    if j == UP_GROUPS * GS + 1:
                        own.mark(V.tensor_scalar(acc[:, :], row, w, None, ALU.mult))
                    else:
                        own.mark(V.scalar_tensor_tensor(acc[:, :], row, w, acc[:, :], ALU.mult, ALU.add))
                own.wait()
                own.then(V.tensor_tensor(h1[par][:, :], h1[par][:, :], h_odd[:, :], ALU.add))
                dve.wait_ge(group_added, UP_GROUPS * (n + 1))
                V.tensor_tensor(h1[par][:, :], h1[par][:, :], S[0][:, 0:P], ALU.add).then_inc(tile_added, 1)

            DOTS = {1: (0, (range(0, 3), range(3, 6), range(6, 8))), 2: (0, (range(8, 11), range(11, 14), range(14, 16))),
                    3: (1, (range(0, 3), range(3, 6), range(6, 8))), 4: (1, (range(8, 11), range(11, 14), range(14, 16))),
                    5: (2, (range(0, 3), range(3, 6), range(6, 8))), 6: (2, (range(8, 11), range(11, 14), range(14, 16))),
                    7: (3, (range(0, 5), range(5, 11), range(11, 16)))}

            def round_(n, par, gru=True, inputs=True, mixing=True, experts=True):
                odd = 1 - par
                own.restart()

                def step(s):
                    g, gaps = DOTS.get(s, (None, None))

                    def dots(i):
                        down(n - 2, g, par, gaps[i])

                    use = dots if experts and gaps else None
                    if gru:
                        gru_step(n, s, par, use)
                    elif use:
                        for i in range(3):
                            use(i)

                step(0)
                if mixing:
                    norm_threads(n - 1, odd, inputs)
                elif inputs:
                    moments_of_emb(n + 1)
                step(1)
                if mixing:
                    norm_mixture(n - 1, odd)
                step(2)
                if experts:
                    gelu_in_(n - 2, 0)
                if gru:
                    if isinstance(n, int) and n == 1:
                        dve.wait_ge(mask_in, 32)
                    window_mask(n, par)
                if experts:
                    weigh(n - 2, 0, par)
                step(3)
                if gru:
                    window_inv(n)
                if mixing:
                    key_tops(n - 1, 0)
                    key_tops(n - 1, 1)
                if inputs:
                    make_x(n + 1, odd)
                step(4)
                if experts:
                    gelu_in_(n - 2, 1)
                    weigh(n - 2, 1, par)
                if mixing:
                    key_tops(n - 1, 2)
                    key_tops(n - 1, 3)
                step(5)
                if mixing:
                    best_pairs(n - 1)
                step(6)
                if experts:
                    gelu_in_(n - 2, 2)
                    weigh(n - 2, 2, par)
                if mixing:
                    expert_rows(n - 1, odd)
                step(7)
                if experts:
                    gelu_in_(n - 2, 3)
                if mixing:
                    expert_probs(n - 1, odd)
                if experts:
                    weigh(n - 2, 3, par)
                    add_last_up(n - 2, par)
                own.wait()

            dve.wait_ge(weights_in, LOADS)
            dve.wait_ge(zeroed, 4)
            dve.wait_ge(mask_in, 16)
            own.mark(V.tensor_tensor(b_in[:, :, 0:2], b_in[:, :, 0:2], b_hid[:, :, 0:2], ALU.add))
            own.mark(V.tensor_copy(b_hn[:, :, :], b_hid[:, :, 2:3].to_broadcast([P, K, B])))
            own.wait()
            dve.sem_inc(bias_ready, 1)
            moments_of_emb(0)
            make_x(0, 0)
            own.wait()
            rounds(dve, round_)


def layer1(nc, d, hidden, out):
    with ExitStack() as ctx:
        def sb(name, shape, dt=F32):
            return ctx.enter_context(nc.sbuf_tensor(name, shape, dt))

        def pair(name, shape, dt=F32):
            return [sb(f"{name}_seq{j}", shape, dt) for j in range(2)]

        def sem(name):
            return ctx.enter_context(nc.semaphore(name))

        def bank(name):
            return ctx.enter_context(nc.psum_tensor(name, [P, 512], F32))

        w_qkv = sb("w_qkv", [P, 5, T])
        gamma = sb("gamma", [P, 1])
        rope = sb("rope", [P, 4, T])
        w_out = sb("w_out", [P, 4, P])
        ident = sb("ident1", [P, P])
        conv_w = sb("conv_w", [P, 3])
        conv_b = sb("conv_b", [P, 1])
        f_wqkv = sb("f_wqkv", [P, 3, P])
        f_bqk = sb("f_bqk", [P, 2])
        f_bv = sb("f_bv", [P, P])
        f_wo = sb("f_wo", [P, P])
        f_bo = sb("f_bo", [P, P])
        head_rows = sb("head_rows", [P, H])
        f_bk = sb("f_bk", [P, H])
        h_a = pair("h_a", [P, CH, P])
        u_a = sb("u_a", [P, CH, P])
        sq = sb("sq", [P, P])
        stats = sb("stats1", [P, CH, 6])
        mv_a = sb("mv_a", [P, CH, 2])
        mv_f = sb("mv_f", [P, CH, 2])
        rstd_a = sb("rstd_a", [P, CH])
        rstd_f = sb("rstd_f", [P, CH])
        ss = sb("ss", [P, CH])
        nt_a = sb("nt_a", [P, 3, CH])
        nt_f = sb("nt_f", [P, 3, CH])
        xn_t = sb("xn_t", [P, T])
        q_t = pair("q_t", [P, 4, T])
        k_t = pair("k_t", [P, H, T])
        v_a = pair("v_a", [P, CH, T])
        turned = sb("turned", [P, 3, T])
        a_nmax = sb("a_nmax", [P, 2])
        a_sum = sb("a_sum", [P, UNITS])
        a_inv = sb("a_inv", [P, H])
        a_p = sb("a_p", [P, 2, T])
        a_pt = sb("a_pt", [P, 2, CH, P])
        a_o = sb("a_o", [P, T])
        a_ot = sb("a_ot", [P, 4, P])
        h1 = sb("h_mid", [P, CH, P])
        h_f = pair("h_f", [P, CH, P])
        u_f = sb("u_f", [P, CH, P])
        u_t = sb("u_t", [P, T + 2])
        x_c = sb("x_c", [P, T])
        x_f = sb("x_f", [P, T])
        q_f = pair("q_f", [P, T])
        k_f = pair("k_f", [P, H, T])
        v_f = pair("v_f", [P, CH, H, HD + 1])
        top_a = sb("top_a", [P, 2, TOP])
        top_b = sb("top_b", [P, 2, TOP])
        f_nmax = sb("f_nmax", [P, 2])
        f_s = sb("f_s", [P, 2, T])
        f_e = sb("f_e", [P, 2, T])
        f_p = sb("f_p", [P, 2, T])
        f_pt = sb("f_pt", [P, 2, CH, P])
        f_inv = sb("f_inv", [P, H])
        f_o = sb("f_o", [P, P])
        f_ot = sb("f_ot", [P, P])
        f_out = sb("f_out", [P, CH, P])

        SC = [bank(f"SC{i}") for i in range(3)]
        AT, AO = bank("AT"), bank("AO")
        FT, FO = bank("FT"), bank("FO")
        R = bank("R")

        weights_in = sem("weights_in1")
        weights_ready = sem("weights_ready")
        cleared = sem("cleared1")
        h_loaded = sem("h_loaded")
        squares = sem("squares")
        squares_done = sem("squares_done")
        rope_added = sem("rope_added")
        u_scaled = sem("u_scaled")
        xn_turned = sem("xn_turned")
        xn_ready = sem("xn_ready")
        proj = sem("proj")
        proj_used = sem("proj_used")
        v_proj = sem("v_proj")
        v_ready = sem("v_ready")
        a_scores = sem("a_scores")
        a_max = sem("a_max")
        a_exp = sem("a_exp")
        a_turned = sem("a_turned")
        a_t_ready = sem("a_t_ready")
        a_pv = sem("a_pv")
        a_norm = sem("a_norm")
        a_o_turned = sem("a_o_turned")
        a_ot_ready = sem("a_ot_ready")
        a_outed = sem("a_outed")
        h1_ready = sem("h1_ready")
        hf_ready = sem("hf_ready")
        uf_ready = sem("uf_ready")
        uf_turned = sem("uf_turned")
        ut_ready = sem("ut_ready")
        xf_ready = sem("xf_ready")
        f_proj = sem("f_proj")
        qf_ready = sem("qf_ready")
        kf_ready = sem("kf_ready")
        f_vproj = sem("f_vproj")
        vf_ready = sem("vf_ready")
        f_scores = sem("f_scores")
        f_first = sem("f_first")
        f_exp = sem("f_exp")
        f_probs = sem("f_probs")
        f_turned = sem("f_turned")
        f_t_ready = sem("f_t_ready")
        f_pv = sem("f_pv")
        f_norm = sem("f_norm")
        f_o_turned = sem("f_o_turned")
        f_ot_ready = sem("f_ot_ready")
        f_outed = sem("f_outed")
        out_ready = sem("out_ready")
        out_stored = sem("out_stored")
        dve_step = sem("dve_step1")
        pool_step = sem("pool_step1")

        rows_of = hidden.rearrange("n p d -> (n p) d").rearrange("(c p b) d -> b p c d", p=P, b=B)
        out_of = out.rearrange("b (c p) d -> b p c d", p=P)
        consts = [(w_qkv, "qkv1"), (gamma, "gamma"), (rope, "rope"), (w_out, "w_out"), (ident, "ident"),
                  (conv_w, "conv_w"), (conv_b, "conv_b"), (f_wqkv, "f_wqkv"), (f_bqk, "f_bqk"), (f_wo, "f_wo"),
                  (head_rows, "head_rows")]
        spread = [(f_bv, "f_bv"), (f_bo, "f_bo")]
        LOADS = 16 * (len(consts) + len(spread))
        block = ctx.enter_context(nc.Block())

        def there(s):
            return not isinstance(s, int) or 0 <= s < B

        def rounds(eng, one):
            one(0, 0)
            one(1, 1)
            with eng.Fori(1, B // 2 - 1) as i:
                one(2 * i, 0)
                one(2 * i + 1, 1)
            for b in range(B - 2, B + 2):
                one(b, b % 2)

        def unit_at(b, t, lag):
            back, u = (lag - t + UNITS - 1) // UNITS if t < lag else 0, (t - lag) % UNITS
            return b - back, u, back % 2

        def walk(b, par, tasks, pieces, own=None):
            if own:
                own.restart()
            for t in range(UNITS):
                for task in tasks:
                    if task == "piece":
                        for step, shift, f in pieces:
                            if step == t and there(b + shift):
                                f(b + shift, (par + shift) % 2)
                        continue
                    branch, ends, lag, f = task
                    s, u, odd = unit_at(b, t, lag + (UNITS + F_LAG if branch == "f" else 0))
                    if not there(s) or (ends and u % H != H - 1):
                        continue
                    f(s, u // H if ends else u, (par + odd) % 2)
            if own:
                own.wait()

        def wait(eng, sem, value):
            if not isinstance(value, int) or value > 0:
                eng.wait_ge(sem, value)

        def score_bank(t, branch):
            return SC[(2 * t + (branch == "f")) % 3]

        def bank_before(b, x):
            c = x % 3
            while True:
                x -= 3
                if x < 0:
                    x = max(y for y in range(2 * UNITS) if y % 3 == c)
                    b = b - 1
                    if isinstance(b, int) and b < 0:
                        return None
                s, u, _ = unit_at(b, x // 2, UNITS + F_LAG if x % 2 else 0)
                if there(s):
                    return (f_exp if x % 2 else a_exp), UNITS * s + u + 1

        @block.sync
        def _(sync):
            for t, name in consts:
                sync.dma_start(t[tuple(slice(None) for _ in t.shape)], d[name]).then_inc(weights_in, 16)
            for t, name in spread:
                sync.dma_start(t[:, :], d[name].partition_broadcast(P)).then_inc(weights_in, 16)

            def load(s, par):
                wait_apart(sync, (weights_in, LOADS), *(() if isinstance(s, int) and s < 1 else ((h_loaded, 16 * s),)),
                           *(() if isinstance(s, int) and s < 2 else ((h1_ready, CH * (s - 1)),)))
                sync.dma_start(h_a[par][:, :, :], rows_of[s]).then_inc(h_loaded, 16)

            def one(b, par):
                if there(b + 1):
                    load(b + 1, 1 - par)
                if there(b - 2):
                    sync.wait_ge(out_ready, CH * (b - 1))
                    sync.dma_start(out_of[b - 2], f_out[:, :, :]).then_inc(out_stored, 16)

            load(0, 0)
            rounds(sync, one)
            sync.wait_ge(out_stored, 16 * B)

        @block.gpsimd
        def _(pool):
            pool.memset(u_t[:, :], 0.0).then_inc(cleared, 1)
            for v in v_f:
                pool.memset(v[:, :, :, :], 1.0).then_inc(cleared, 1)
            for v in k_t:
                pool.memset(v[:, :, :], 0.0).then_inc(cleared, 1)
            pool.wait_ge(cleared, 5)

            def residual_f(s, par):
                wait_apart(pool, (weights_in, LOADS), (h1_ready, CH * (s + 1)),
                           *(() if isinstance(s, int) and s < 2 else ((out_ready, CH * (s - 1)),)))
                pool.tensor_tensor(h_f[par][:, :, :], h1[:, :, :], f_bo[:, :].unsqueeze(1).to_broadcast([P, CH, P]), ALU.add
                                   ).then_inc(hf_ready, 1)

            def rope_adds(s, par):
                for j in range(4):
                    wait_apart(pool, (weights_in, LOADS), (proj_used, 16 * s + 4 * j + 2),
                               *(((rope_added, 12 * s + 3 * j),) if j or not isinstance(s, int) or s else ()))
                    pool.tensor_tensor(q_t[par][:, j, :], q_t[par][:, j, :], turned[:, 0, :], ALU.add).then_inc(rope_added, 1)
                    wait_apart(pool, (weights_in, LOADS), (proj_used, 16 * s + 4 * j + 4))
                    for e in range(2):
                        half = slice(e * DH, (e + 1) * DH)
                        wait_apart(pool, (weights_in, LOADS), (rope_added, 12 * s + 3 * j + 1 + e))
                        pool.tensor_tensor(k_t[par][half, 2 * j + e, :], turned[half, 2, :], turned[half, 1, :], ALU.add
                                           ).then_inc(rope_added, 1)

            def one(b, par):
                if there(b - 1):
                    residual_f(b - 1, 1 - par)
                if there(b + 1):
                    rope_adds(b + 1, 1 - par)

            rope_adds(0, 0)
            rounds(pool, one)

        @block.tensor
        def _(pe):
            def turn_a(s, par):
                pe.wait_ge(u_scaled, s + 1)
                wait(pe, v_ready, CH * s)
                wait(pe, vf_ready, s - 1)
                for c in range(CH):
                    m = pe.transpose(R[:, c * P:(c + 1) * P], u_a[:, c, :], ident[:, :])
                m.then_inc(xn_turned, 1)

            def project(j, w):
                def f(s, par):
                    if j == 0 and w == 0:
                        pe.wait_ge(xn_ready, s + 1)
                    else:
                        pe.wait_ge(proj_used, 16 * s + 4 * j + w)
                    pe.matmul(R[:, :], w_qkv[:, w, j * P:(j + 1) * P], xn_t[:, :], start=True, stop=True
                              ).then_inc(proj, 1)
                return f

            def project_v(c):
                def f(s, par):
                    pe.wait_ge(proj_used, 16 * (s + 1))
                    if c:
                        pe.wait_ge(v_ready, CH * s + c)
                    pe.matmul(R[:, :], xn_t[:, c * P:(c + 1) * P], w_qkv[:, 4, :], start=True, stop=True
                              ).then_inc(v_proj, 1)
                return f

            def turn_f(s, par):
                pe.wait_ge(uf_ready, s + 1)
                pe.wait_ge(v_ready, CH * min(s + 2, B) if isinstance(s, int) else CH * (s + 2))
                for c in range(CH):
                    m = pe.transpose(R[:, c * P:(c + 1) * P], u_f[:, c, :], ident[:, :])
                m.then_inc(uf_turned, 1)

            def f_q(s, par):
                pe.wait_ge(xf_ready, s + 1)
                pe.matmul(R[:, :], f_wqkv[:, 0, :], x_f[:, :], start=True, stop=True).then_inc(f_proj, 1)

            def f_k(s, par):
                pe.wait_ge(qf_ready, s + 1)
                pe.matmul(R[:, :], f_wqkv[:, 1, :], x_f[:, :], start=True, stop=True).then_inc(f_proj, 1)

            def f_vals(s, par):
                pe.wait_ge(kf_ready, H * (s + 1))
                for c in range(CH):
                    m = pe.matmul(R[:, c * P:(c + 1) * P], x_f[:, c * P:(c + 1) * P], f_wqkv[:, 2, :],
                                  start=(c == 0), stop=True, skip_group_check=True)
                m.then_inc(f_vproj, 1)

            def a_s(s, u, par):
                c, h = divmod(u, H)
                if u == 0:
                    pe.wait_ge(v_ready, CH * (s + 1))
                    pe.wait_ge(rope_added, 12 * (s + 1))
                before = bank_before(s, 2 * u)
                if before:
                    pe.wait_ge(*before)
                pe.matmul(score_bank(u, "a")[:, :], q_t[par][:, h // 2, c * P:(c + 1) * P], k_t[par][:, h, :],
                          start=True, stop=True).then_inc(a_scores, 1)

            def a_v(s, u, par):
                c, h = divmod(u, H)
                pe.wait_ge(a_t_ready, UNITS * s + u + 1)
                if h == 0:
                    wait(pe, a_norm, CH * s + c)
                for j in range(CH):
                    m = pe.matmul(AO[:, h * DH:(h + 1) * DH], a_pt[:, u % 2, j, :], v_a[par][:, j, h * DH:(h + 1) * DH],
                                  start=(h == 0 and j == 0), stop=(j == CH - 1), skip_group_check=True)
                m.then_inc(a_pv, 1)

            def turn(s, u, bank, src, ready, t_ready, ot_ready, row_ready, turned_):
                pe.wait_ge(ready, UNITS * s + u + 1)
                wait(pe, t_ready, UNITS * s + u)
                if u % H == 1:
                    wait(pe, ot_ready, CH * s + u // H)
                if u % H == 2:
                    wait(pe, row_ready, CH * s + u // H)
                for j in range(CH):
                    m = pe.transpose(bank[:, j * P:(j + 1) * P], src[:, u % 2, j * P:(j + 1) * P], ident[:, :])
                m.then_inc(turned_, 1)

            def a_turn(s, u, par):
                turn(s, u, AT, a_p, a_exp, a_t_ready, a_ot_ready, h1_ready, a_turned)

            def units_by(s, c, n):
                v = UNITS * s + H * c + n
                return min(v, UNITS * B) if isinstance(v, int) else v

            def a_end1(s, c, par):
                pe.wait_ge(a_norm, CH * s + c + 1)
                pe.wait_ge(a_t_ready, units_by(s, c, 9))
                for j in range(4):
                    m = pe.transpose(AT[:, j * P:(j + 1) * P], a_o[:, j * P:(j + 1) * P], ident[:, :])
                m.then_inc(a_o_turned, 1)

            def a_end2(s, c, par):
                pe.wait_ge(a_ot_ready, CH * s + c + 1)
                pe.wait_ge(a_t_ready, units_by(s, c, 10))
                for j in range(4):
                    m = pe.matmul(AT[:, 0:P], a_ot[:, j, :], w_out[:, j, :], start=(j == 0), stop=(j == 3))
                m.then_inc(a_outed, 1)

            def f_sc(s, u, par):
                c, h = divmod(u, H)
                if u == 0:
                    pe.wait_ge(qf_ready, s + 1)
                    pe.wait_ge(kf_ready, H * (s + 1))
                t = (u + F_LAG) % UNITS
                pe.wait_ge(*bank_before(s + 1 + (u + F_LAG) // UNITS, 2 * t + 1))
                pe.matmul(score_bank(t, "f")[:, :], q_f[par][:, c * P:(c + 1) * P], k_f[par][:, h, :],
                          start=True, stop=True).then_inc(f_scores, 1)

            def f_v(s, u, par):
                c, h = divmod(u, H)
                if u == 0:
                    pe.wait_ge(vf_ready, s + 1)
                pe.wait_ge(f_t_ready, UNITS * s + u + 1)
                if h == 0:
                    wait(pe, f_norm, CH * s + c)
                for j in range(CH):
                    m = pe.matmul(FO[:, h * (HD + 1):(h + 1) * (HD + 1)], f_pt[:, u % 2, j, :], v_f[par][:, j, h, :],
                                  start=(h == 0 and j == 0), stop=(j == CH - 1), skip_group_check=True)
                m.then_inc(f_pv, 1)

            def f_turn(s, u, par):
                turn(s, u, FT, f_p, f_probs, f_t_ready, f_ot_ready, out_ready, f_turned)

            def f_end1(s, c, par):
                pe.wait_ge(f_norm, CH * s + c + 1)
                pe.wait_ge(f_t_ready, units_by(s, c, 9))
                pe.transpose(FT[:, 0:P], f_o[:, :], ident[:, :]).then_inc(f_o_turned, 1)

            def f_end2(s, c, par):
                pe.wait_ge(f_ot_ready, CH * s + c + 1)
                pe.wait_ge(f_t_ready, units_by(s, c, 10))
                pe.matmul(FT[:, 0:P], f_ot[:, :], f_wo[:, :], start=True, stop=True).then_inc(f_outed, 1)

            tasks = [("a", False, 0, a_s), ("f", False, 0, f_sc), ("a", True, 3, a_end1), ("f", True, 4, f_end1),
                     ("a", True, 4, a_end2), ("f", True, 5, f_end2), "piece", ("a", False, 2, a_v), ("f", False, 3, f_v),
                     ("a", False, 1, a_turn), ("f", False, 2, f_turn)]
            pre_a = [(11, 1, turn_a)] + [(12 + 4 * j + w, 1, project(j, w)) for j in range(4) for w in range(4)] \
                + [(28 + c, 1, project_v(c)) for c in range(CH)]
            pre_f = [(5, -1, turn_f), (7, -1, f_q), (8, -1, f_k), (9, -1, f_vals)]

            pe.wait_ge(weights_in, LOADS)
            pe.wait_ge(weights_ready, 1)
            for _, _, f in pre_a:
                f(0, 0)
            rounds(pe, lambda b, par: walk(b, par, tasks, pre_a + pre_f))

        @block.scalar
        def _(act):
            def squares_a(s, par):
                act.wait_ge(squares, s + 1)
                for c in range(CH):
                    nc.scalar.activation(sq[:, :], u_a[:, c, :], ACT.Square, accum_out=ss[:, c:c + 1]).then_inc(squares_done, 1)
                    act.wait_ge(squares_done, CH * s + c + 1)

            def turn_a(s, par):
                act.wait_ge(xn_turned, s + 1)
                nc.scalar.copy(xn_t[:, :], R[:, :]).then_inc(xn_ready, 1)

            def project_v(c):
                def f(s, par):
                    act.wait_ge(v_proj, CH * s + c + 1)
                    nc.scalar.copy(v_a[par][:, c, :], R[:, :]).then_inc(v_ready, 1)
                return f

            def turn_f(s, par):
                act.wait_ge(uf_turned, s + 1)
                nc.scalar.copy(u_t[:, 1:T + 1], R[:, :]).then_inc(ut_ready, 1)

            def f_q(s, par):
                act.wait_ge(f_proj, 2 * s + 1)
                nc.scalar.activation(q_f[par][:, :], R[:, :], ACT.Identity, bias=f_bqk[:, 0:1], scale=float(D) ** -0.5
                                     ).then_inc(qf_ready, 1)

            def f_k(s, par):
                act.wait_ge(f_proj, 2 * s + 2)
                for h in range(H):
                    nc.scalar.activation(k_f[par][:, h, :], R[:, :], ACT.Identity, scale=head_rows[:, h:h + 1],
                                         bias=f_bk[:, h:h + 1]).then_inc(kf_ready, 1)

            def a_e(s, u, par):
                act.wait_ge(a_max, UNITS * s + u + 1)
                wait(act, a_turned, UNITS * s + u - 1)
                nc.scalar.activation(a_p[:, u % 2, :], score_bank(u, "a")[:, :], ACT.Exp, bias=a_nmax[:, u % 2:u % 2 + 1],
                                     accum_out=a_sum[:, u:u + 1]).then_inc(a_exp, 1)

            def a_ev(s, u, par):
                act.wait_ge(a_turned, UNITS * s + u + 1)
                wait(act, a_pv, UNITS * s + u - 1)
                nc.scalar.copy(a_pt[:, u % 2, :, :], AT[:, :].rearrange("p (j n) -> p j n", j=CH)).then_inc(a_t_ready, 1)

            def a_end(s, c, par):
                act.wait_ge(a_o_turned, CH * s + c + 1)
                nc.scalar.copy(a_ot[:, :, :], AT[:, :].rearrange("p (j n) -> p j n", j=4)).then_inc(a_ot_ready, 1)

            def f_e_(s, u, par):
                act.wait_ge(f_first, UNITS * s + u + 1)
                wait(act, f_probs, UNITS * s + u - 1)
                nc.scalar.activation(f_e[:, u % 2, :], score_bank((u + F_LAG) % UNITS, "f")[:, :], ACT.Exp,
                                     bias=f_nmax[:, u % 2:u % 2 + 1]).then_inc(f_exp, 1)

            def f_ev(s, u, par):
                act.wait_ge(f_turned, UNITS * s + u + 1)
                wait(act, f_pv, UNITS * s + u - 1)
                nc.scalar.copy(f_pt[:, u % 2, :, :], FT[:, :].rearrange("p (j n) -> p j n", j=CH)).then_inc(f_t_ready, 1)

            def f_end(s, c, par):
                act.wait_ge(f_o_turned, CH * s + c + 1)
                nc.scalar.copy(f_ot[:, :], FT[:, 0:P]).then_inc(f_ot_ready, 1)

            tasks = [("a", False, 0, a_e), ("a", True, 3, a_end), ("f", True, 4, f_end), ("f", False, 0, f_e_), "piece",
                     ("a", False, 1, a_ev), ("f", False, 2, f_ev)]
            pre_a = [(8, 1, squares_a), (11, 1, turn_a)] + [(28 + c, 1, project_v(c)) for c in range(CH)]
            pre_f = [(5, -1, turn_f), (7, -1, f_q), (8, -1, f_k)]

            nc.scalar.preload_act_table_set("exp_and_others")
            act.wait_ge(cleared, 5)
            act.wait_ge(weights_ready, 1)
            for _, _, f in pre_a:
                f(0, 0)
            rounds(act, lambda b, par: walk(b, par, tasks, pre_a + pre_f))

        @block.vector
        def _(dve):
            own = Steps(dve, dve_step)
            V = nc.vector

            def moments(src, mv):
                for c in range(CH):
                    own.mark(V.bn_stats(stats[:, c, :], src[:, c, :]))
                own.wait()
                for c in range(CH):
                    own.mark(V.bn_aggr(mv[:, c, :], stats[:, c, :]))
                own.wait()

            def apply_norm(src, dst, mv, rstd):
                for c in range(CH):
                    own.mark(V.tensor_scalar(dst[:, c, :], src[:, c, :], mv[:, c, 0:1], rstd[:, c:c + 1],
                                             ALU.subtract, ALU.mult))
                own.wait()

            def norm_a1(s, par):
                dve.wait_ge(h_loaded, 16 * (s + 1))
                moments(h_a[par], mv_a)

            def norm_a2(s, par):
                rsqrt_start(nc, own, rstd_a[:, :], mv_a[:, :, 1], nt_a, CH, LN_EPS)
                rsqrt_steps(nc, own, rstd_a[:, :], nt_a, CH, 1)

            def norm_a3(s, par):
                rsqrt_steps(nc, own, rstd_a[:, :], nt_a, CH, 2)

            def norm_a4(s, par):
                apply_norm(h_a[par], u_a, mv_a, rstd_a)
                dve.sem_inc(squares, 1)

            def scale_a1(s, par):
                dve.wait_ge(squares_done, CH * (s + 1))
                rsqrt_start(nc, own, rstd_a[:, :], ss[:, :], nt_a, CH, 0.0)
                rsqrt_steps(nc, own, rstd_a[:, :], nt_a, CH, 1)

            def scale_a2(s, par):
                rsqrt_steps(nc, own, rstd_a[:, :], nt_a, CH, 2)

            def scale_a3(s, par):
                own.then(V.tensor_scalar(rstd_a[:, :], rstd_a[:, :], 1e8, None, ALU.min))
                for c in range(CH):
                    own.mark(V.tensor_scalar(u_a[:, c, :], u_a[:, c, :], rstd_a[:, c:c + 1], None, ALU.mult))
                own.wait()
                dve.sem_inc(u_scaled, 1)

            def rotate(j, w):
                def f(s, par):
                    dst = (q_t[par][:, j, :], turned[:, 0, :], turned[:, 2, :], turned[:, 1, :])[w]
                    dve.wait_ge(proj, 16 * s + 4 * j + w + 1)
                    if w:
                        wait(dve, rope_added, 12 * s + 3 * j - (2 if w == 1 else 0))
                    V.tensor_tensor(dst, R[:, :], rope[:, w, :], ALU.mult).then_inc(proj_used, 1)
                return f

            def norm_f1(s, par):
                dve.wait_ge(h1_ready, CH * (s + 1))
                moments(h1, mv_f)
                rsqrt_start(nc, own, rstd_f[:, :], mv_f[:, :, 1], nt_f, CH, LN_EPS)

            def norm_f2(s, par):
                rsqrt_steps(nc, own, rstd_f[:, :], nt_f, CH, 3)
                apply_norm(h1, u_f, mv_f, rstd_f)
                dve.sem_inc(uf_ready, 1)

            def convolve(s, par):
                dve.wait_ge(ut_ready, s + 1)
                own.then(V.tensor_scalar(x_c[:, :], u_t[:, 0:T], conv_w[:, 0:1], conv_b[:, 0:1], ALU.mult, ALU.add))
                own.then(V.scalar_tensor_tensor(x_c[:, :], u_t[:, 1:T + 1], conv_w[:, 1:2], x_c[:, :], ALU.mult, ALU.add))
                own.then(V.scalar_tensor_tensor(x_c[:, :], u_t[:, 2:T + 2], conv_w[:, 2:3], x_c[:, :], ALU.mult, ALU.add))
                V.tensor_tensor(x_f[:, :], x_c[:, :], u_t[:, 1:T + 1], ALU.add).then_inc(xf_ready, 1)

            def f_vals(s, par):
                dve.wait_ge(f_vproj, s + 1)
                V.tensor_tensor(v_f[par][:, :, :, 0:HD], R[:, :].rearrange("p (c h e) -> p c h e", c=CH, h=H),
                                f_bv[:, :].rearrange("p (h e) -> p h e", h=H).unsqueeze(1).to_broadcast([P, CH, H, HD]),
                                ALU.add).then_inc(vf_ready, 1)

            def a_m(s, u, par):
                dve.wait_ge(a_scores, UNITS * s + u + 1)
                wait(dve, a_exp, UNITS * s + u - 1)
                V.tensor_reduce(a_nmax[:, u % 2:u % 2 + 1], score_bank(u, "a")[:, :], AX, ALU.max, negate=True
                                ).then_inc(a_max, 1)

            def f_max1(s, u, par):
                wait_apart(dve, (weights_in, LOADS), (f_scores, UNITS * s + u + 1))
                own.mark(V.max(top_a[:, u % 2, :], score_bank((u + F_LAG) % UNITS, "f")[:, :]))

            def f_strike1(s, u, par):
                pq = u % 2
                own.wait()
                own.mark(V.match_replace(f_s[:, pq, :], top_a[:, pq, :], score_bank((u + F_LAG) % UNITS, "f")[:, :], NEG))
                wait(dve, f_exp, UNITS * s + u - 1)
                own.mark(V.tensor_scalar(f_nmax[:, pq:pq + 1], top_a[:, pq, 0:1], -1.0, None, ALU.mult))

            def f_max2(s, u, par):
                own.wait()
                dve.sem_inc(f_first, 1)
                own.then(V.max(top_b[:, u % 2, :], f_s[:, u % 2, :]))
                own.mark(V.match_replace(f_s[:, u % 2, :], top_b[:, u % 2, :], f_s[:, u % 2, :], NEG))

            def f_mask(s, u, par):
                pq = u % 2
                own.wait_lag(0 if isinstance(s, int) and s == B - 1 and u == UNITS - 1 else 2)
                dve.wait_ge(f_exp, UNITS * s + u + 1)
                wait(dve, f_turned, UNITS * s + u - 1)
                V.scalar_tensor_tensor(f_p[:, pq, :], f_s[:, pq, :], 0.1 * NEG, f_e[:, pq, :], ALU.is_le, ALU.mult
                                       ).then_inc(f_probs, 1)

            def a_n(s, c, par):
                dve.wait_ge(a_pv, UNITS * s + H * (c + 1))
                own.then(V.reciprocal(a_inv[:, :], a_sum[:, c * H:(c + 1) * H]))
                wait(dve, a_o_turned, CH * s + c)
                V.tensor_tensor(a_o[:, :].rearrange("p (h e) -> p h e", h=H), AO[:, :].rearrange("p (h e) -> p h e", h=H),
                                a_inv[:, :].unsqueeze(2).to_broadcast([P, H, DH]), ALU.mult).then_inc(a_norm, 1)

            def a_h(s, c, par):
                dve.wait_ge(a_outed, CH * s + c + 1)
                if c == 0:
                    wait(dve, hf_ready, s)
                V.tensor_tensor(h1[:, c, :], AT[:, 0:P], h_a[par][:, c, :], ALU.add).then_inc(h1_ready, 1)

            def f_n(s, c, par):
                dve.wait_ge(f_pv, UNITS * s + H * (c + 1))
                acc = FO[:, 0:H * (HD + 1)].rearrange("p (h e) -> p h e", h=H)
                own.then(V.reciprocal(f_inv[:, :].unsqueeze(2), acc[:, :, HD:HD + 1]))
                wait(dve, f_o_turned, CH * s + c)
                V.tensor_tensor(f_o[:, :].rearrange("p (h e) -> p h e", h=H), acc[:, :, 0:HD],
                                f_inv[:, :].unsqueeze(2).to_broadcast([P, H, HD]), ALU.mult).then_inc(f_norm, 1)

            def f_h(s, c, par):
                dve.wait_ge(f_outed, CH * s + c + 1)
                if c == 0:
                    dve.wait_ge(hf_ready, s + 1)
                    wait(dve, out_stored, 16 * s)
                V.tensor_tensor(f_out[:, c, :], FT[:, 0:P], h_f[par][:, c, :], ALU.add).then_inc(out_ready, 1)

            tasks = [("f", False, 0, f_max1), ("a", False, 0, a_m), ("f", False, 0, f_strike1), ("a", True, 4, a_h),
                     ("f", True, 5, f_h), ("f", False, 1, f_mask), ("f", False, 0, f_max2),
                     ("a", True, 2, a_n), ("f", True, 3, f_n), "piece"]
            pre_a = [(4, 1, norm_a1), (5, 1, norm_a2), (6, 1, norm_a3), (7, 1, norm_a4),
                     (8, 1, scale_a1), (9, 1, scale_a2), (10, 1, scale_a3)] \
                + [(12 + 4 * j + w, 1, rotate(j, w)) for j in range(4) for w in range(4)]
            pre_f = [(3, -1, norm_f1), (4, -1, norm_f2), (6, -1, convolve), (9, -1, f_vals)]

            dve.wait_ge(weights_in, LOADS)
            own.mark(V.tensor_scalar(w_qkv[:, :, :], w_qkv[:, :, :], gamma[:, 0:1], float(D) ** 0.5, ALU.mult, ALU.mult))
            own.mark(V.tensor_scalar(f_bk[:, :], head_rows[:, :], f_bqk[:, 1:2], None, ALU.mult))
            own.mark(V.tensor_scalar(f_bqk[:, 0:1], f_bqk[:, 0:1], float(D) ** -0.5, None, ALU.mult))
            own.wait()
            dve.sem_inc(weights_ready, 1)
            dve.wait_ge(cleared, 5)
            for _, _, f in pre_a:
                f(0, 0)
            own.wait()
            rounds(dve, lambda b, par: walk(b, par, tasks, pre_a + pre_f, own))


def build(nc, d, out):
    hidden = nc.dram_tensor("hidden", (TILES, P, D), F32, kind="Internal").ap()
    layer0(nc, d, hidden)
    layer1(nc, d, hidden, out)


def kernel(**inputs):
    import numpy as np
    import concourse.bacc as bacc
    from concourse.bass_utils import run_bass_kernel_spmd as run

    nc = bacc.Bacc("TRN2", target_bir_lowering=False, num_devices=1)
    arrays, d = {}, {}

    def give(name, a):
        a = np.ascontiguousarray(a)
        arrays[f"{name}_dram"] = a
        d[name] = nc.dram_tensor(f"{name}_dram", a.shape, mybir.dt.from_np(a.dtype), kind="ExternalInput").ap()

    v = {k: np.asarray(a) for k, a in inputs.items()}
    give("token_ids", v["x"].reshape(B, TILES, STEPS).transpose(2, 0, 1).reshape(P, TILES))
    give("tok_w", v["L0_tok_W"].T)
    give("w_ih", v["L0_attn_gru_wih"].transpose(2, 0, 1).reshape(P, -1))
    give("w_hh", v["L0_attn_gru_whh"].transpose(2, 0, 1).reshape(P, -1))
    give("b_in", v["L0_attn_gru_bih"].reshape(K, GATES, P).transpose(2, 0, 1))
    give("b_hid", v["L0_attn_gru_bhh"].reshape(K, GATES, P).transpose(2, 0, 1))
    for name in ("wq", "wk", "wv"):
        give(f"w_{name[1]}", v[f"L0_attn_{name}"].transpose(2, 0, 1).reshape(P, -1))
    give("w_beat", v["L0_attn_w_beat"].reshape(K, P, 2, P).transpose(3, 0, 2, 1))
    give("w_mix", v["L0_attn_w_mix"].reshape(P, K, P).transpose(2, 1, 0))
    give("norm_g", v["L0_attn_norm_g"].reshape(K, P).T)
    give("norm_b", v["L0_attn_norm_b"].reshape(K, P).T)
    give("bn_g", v["L0_attn_bn_g"])
    give("bn_b", v["L0_attn_bn_b"])
    give("key_wq", v["L0_ffn_Wq"].T)
    give("key_bq", v["L0_ffn_bq"].reshape(H, P).T)
    give("keys", v["L0_ffn_keys"].transpose(1, 3, 0, 2).reshape(P, H, EXPERTS))
    give("experts", np.concatenate([v["L0_ffn_w_down_embed"], v["L0_ffn_w_up_embed"]], axis=1))
    pairs = v["L1_attn_w_qkv"].reshape(D, 3, H * DH // 2, 2)
    plain, swapped = pairs.reshape(D, 3, -1), pairs[..., ::-1].reshape(D, 3, -1)
    give("qkv1", np.stack([plain[:, 0], swapped[:, 0], plain[:, 1], swapped[:, 1], plain[:, 2]], axis=1))
    give("gamma", v["L1_attn_gamma"].reshape(P, 1))
    give("w_out", v["L1_attn_w_out"].reshape(4, P, D).transpose(1, 0, 2))
    give("conv_w", v["L1_ffn_pos_w"].reshape(P, 3))
    give("conv_b", v["L1_ffn_pos_b"].reshape(P, 1))
    give("f_wqkv", v["L1_ffn_qkv_w"].reshape(3, P, D).transpose(2, 0, 1))
    give("f_bqk", v["L1_ffn_qkv_b"][:2 * D].reshape(2, P).T)
    give("f_bv", v["L1_ffn_qkv_b"][2 * D:])
    give("f_wo", v["L1_ffn_wo_w"].T)
    give("f_bo", v["L1_ffn_wo_b"])
    for name, a in shape_constants().items():
        give(name, a)
    out = nc.dram_tensor("out", (B, T, D), F32, kind="ExternalOutput").ap()
    build(nc, d, out)
    r = run(nc, [arrays], core_ids=[0])
    return r.results[0]["out"]


def shape_constants():
    import math

    pos = np.arange(T, dtype=np.float32)[:, None]
    div = np.exp(np.arange(0, D, 2, dtype=np.float32) * (-math.log(10000.0) / D))
    pe = np.zeros((T, D), np.float32)
    pe[:, 0::2] = np.sin(pos * div)
    pe[:, 1::2] = np.cos(pos * div)
    tala = np.zeros((T, D), np.float32)
    slots = D // 4
    half = slots // 2
    harm = np.arange(1, half + 1, dtype=np.float32)
    for n, c in enumerate(CYCLES):
        phase = pos % c / c * 2.0 * math.pi
        tala[:, n * slots:n * slots + half] = np.sin(phase * harm)
        tala[:, n * slots + half:(n + 1) * slots] = np.cos(phase * harm)
    table = (0.5 * pe + 0.5 * tala).astype(np.float32)
    step, seq = np.arange(P) // B, np.arange(P) % B
    mask = np.full((P, K, 2, P), NEG, np.float32)
    for k, c in enumerate(CYCLES):
        for half_ in range(2):
            diff = step[:, None] - (step[None, :] - STEPS * (1 - half_))
            ok = (seq[:, None] == seq[None, :]) & (diff >= 0) & (diff < c)
            mask[:, k, half_, :][ok] = 0.0
    mask = np.concatenate([mask, mask[:, :, :1]], axis=2)
    first = mask.copy()
    first[:, :, 0::2, :] = NEG
    inv_freq = (1.0 / ROPE_THETA ** (np.arange(0, DH, 2, dtype=np.float32) / np.float32(DH))).astype(np.float32)
    angle = np.repeat(np.arange(T, dtype=np.float32)[:, None] * inv_freq[None, :], 2, axis=-1).T
    cos, sin = np.cos(angle), np.sin(angle)
    sin[0::2] *= -1.0
    rope = np.stack([cos * DH ** -0.5, sin * DH ** -0.5, cos, sin], axis=1).astype(np.float32)
    head = np.arange(P) // HD
    return {
        "rope": np.tile(rope, (2, 1, 1)),
        "head_rows": (head[:, None] == np.arange(H)).astype(np.float32),
        "pe": np.repeat(table.reshape(TILES, STEPS, 1, D), B, axis=2).reshape(TILES, P, D),
        "mask": mask,
        "mask_first": first,
        "ident": np.eye(P, dtype=np.float32),
        "iota8": np.tile(np.arange(TOP, dtype=np.float32), (P, 1)),
    }
```
